# Optimizing a Trainium2 kernel written in Bass

```python
import numpy as np
import jax
import jax.numpy as jnp

def _softmax(x, axis=-1):
    return jax.nn.softmax(x, axis=axis)

def _gelu(x):
    return jax.nn.gelu(x, approximate=True)

def _silu(x):
    return jax.nn.silu(x)

def _sigmoid(x):
    return jax.nn.sigmoid(x)

def _layernorm(x, axis=-1, eps=1e-05):
    m = jnp.mean(x, axis=axis, keepdims=True)
    v = jnp.var(x, axis=axis, keepdims=True)
    return (x - m) / jnp.sqrt(v + eps)

def _scatter_add(tgt, idx, src, axis=0):
    return tgt.at[idx].add(src)

def _segment_sum(src, seg, n):
    return jax.ops.segment_sum(src, seg, n)
kernel_name = 'mk_gnn_resnorm_d4_gnn_r8_46d63d'

def setup_inputs(seed: int=0):
    np.random.seed(seed)
    _w = jnp.asarray

    def _rec_inputs():
        import jax
        import jax.numpy as jnp
        _gk = jax.random.key(seed)
        x = -0.000202 + 1 * jax.random.normal(jax.random.fold_in(_gk, 1), (6250, 128), jnp.float32)
        _s = jax.random.randint(jax.random.fold_in(_gk, 2), (50000,), 0, 6250, jnp.int32)
        _d = jax.random.randint(jax.random.fold_in(_gk, 3), (50000,), 0, 6250, jnp.int32)
        _loop = jnp.arange(6250, dtype=jnp.int32)
        src = jnp.concatenate([_s, _d, _loop])
        dst = jnp.concatenate([_d, _s, _loop])
        _o = jnp.argsort(dst, stable=True)
        src = src[_o]
        dst = dst[_o]
        edge_attr_128 = -2.25437e-05 + 0.999858 * jax.random.normal(jax.random.fold_in(_gk, 13), (106250, 128), jnp.float32)
        edge_attr_64 = 0.000189758 + 1.00013 * jax.random.normal(jax.random.fold_in(_gk, 14), (106250, 64), jnp.float32)
        return (x, src, dst, edge_attr_128, edge_attr_64)
    x, src, dst, edge_attr_128, edge_attr_64 = _rec_inputs()

    def _L0_gnn_setup():
        import jax, jax.numpy as jnp
        import numpy as np
        N_NODES = 6250
        N_EDGES = 62500
        D_N = 128
        D_E = 128
        D_EO = 128
        EPS = 1e-05
        SLOPE = 0.01

        def _inst_norm(x):
            mu = jnp.mean(x, axis=1, keepdims=True)
            var = jnp.var(x, axis=1, keepdims=True)
            return (x - mu) * jax.lax.rsqrt(var + EPS)

        def _leaky_relu(x):
            return jnp.where(x >= 0, x, SLOPE * x)
        key = jax.random.key(seed)
        ks = jax.random.split(key, 9)
        d_in_e = D_E + 2 * D_N
        d_in_n = D_N + D_EO
        return {'nfeat': jax.random.normal(ks[0], (N_NODES, D_N), dtype=jnp.float32), 'efeat': jax.random.normal(ks[1], (N_EDGES, D_E), dtype=jnp.float32), 'W_e': jax.random.normal(ks[2], (D_EO, d_in_e), dtype=jnp.float32) / np.sqrt(d_in_e), 'b_e': jax.random.normal(ks[3], (D_EO,), dtype=jnp.float32) * 0.01, 'a_e': jax.random.normal(ks[4], (D_EO,), dtype=jnp.float32) / np.sqrt(D_EO), 'W_n': jax.random.normal(ks[5], (D_N, d_in_n), dtype=jnp.float32) / np.sqrt(d_in_n), 'b_n': jax.random.normal(ks[6], (D_N,), dtype=jnp.float32) * 0.01, 'src': jax.random.randint(ks[7], (N_EDGES,), 0, N_NODES, dtype=jnp.int32), 'dst': jax.random.randint(ks[8], (N_EDGES,), 0, N_NODES, dtype=jnp.int32)}
    _L0_gnn_all = _L0_gnn_setup()
    _L0_gnn_in = {k: v for k, v in _L0_gnn_all.items() if k in ('W_e', 'b_e', 'a_e', 'W_n', 'b_n')}
    del _L0_gnn_all

    def _L1_gnn_setup():
        import jax, jax.numpy as jnp
        import numpy as np
        N, F_IN, F_OUT, H, E = (6250, 128, 32, 4, 200000)
        key = jax.random.key(seed)
        ks = jax.random.split(key, 8)
        features = jax.random.normal(ks[0], (N, F_IN), dtype=jnp.float32)
        edge_src = jax.random.randint(ks[1], (E,), 0, N, dtype=jnp.int32)
        edge_dst = jax.random.randint(ks[2], (E,), 0, N, dtype=jnp.int32)
        W_w = jax.random.normal(ks[3], (F_IN, F_OUT * H), dtype=jnp.float32) * 0.05
        W_b = jax.random.normal(ks[4], (F_OUT * H,), dtype=jnp.float32) * 0.05
        a_w = jax.random.normal(ks[5], (H, 2 * F_OUT), dtype=jnp.float32) * 0.05
        a_b = jax.random.normal(ks[6], (H,), dtype=jnp.float32) * 0.05
        return {'features': features, 'edge_src': edge_src, 'edge_dst': edge_dst, 'W_w': W_w, 'W_b': W_b, 'a_w': a_w, 'a_b': a_b}
    _L1_gnn_all = _L1_gnn_setup()
    _L1_gnn_in = {k: v for k, v in _L1_gnn_all.items() if k in ('W_w', 'W_b', 'a_w', 'a_b')}
    del _L1_gnn_all

    def _L2_gnn_setup():
        import jax, jax.numpy as jnp
        import numpy as np
        N_NODES = 6250
        N_EDGES = 100000
        N_GRAPHS = 64
        NEG_SLOPE = 0.01

        def leaky_relu(x):
            return jnp.where(x >= 0, x, NEG_SLOPE * x)
        key = jax.random.key(seed)
        ks = jax.random.split(key, 10)
        x = jax.random.normal(ks[0], (N_NODES, 128), dtype=jnp.float32)
        edge_index = jax.random.randint(ks[1], (2, N_EDGES), 0, N_NODES, dtype=jnp.int64)
        edge_attr = jax.random.normal(ks[2], (N_EDGES, 64), dtype=jnp.float32)
        u = jax.random.normal(ks[3], (N_GRAPHS, 64), dtype=jnp.float32)
        batch = jnp.sort(jax.random.randint(ks[4], (N_NODES,), 0, N_GRAPHS, dtype=jnp.int64))
        s1 = 1.0 / np.sqrt(256)
        w1 = jax.random.uniform(ks[5], (256, 256), jnp.float32, -s1, s1)
        b1 = jnp.zeros((256,), jnp.float32)
        w2 = jax.random.uniform(ks[6], (256, 256), jnp.float32, -s1, s1)
        b2 = jnp.zeros((256,), jnp.float32)
        w3 = jax.random.uniform(ks[7], (256, 128), jnp.float32, -s1, s1)
        b3 = jnp.zeros((128,), jnp.float32)
        return {'x': x, 'edge_index': edge_index, 'edge_attr': edge_attr, 'u': u, 'batch': batch, 'w1': w1, 'b1': b1, 'w2': w2, 'b2': b2, 'w3': w3, 'b3': b3}
    _L2_gnn_all = _L2_gnn_setup()
    _L2_gnn_in = {k: v for k, v in _L2_gnn_all.items() if k in ('u', 'w1', 'b1', 'w2', 'b2', 'w3', 'b3')}
    del _L2_gnn_all

    def _L3_gnn_setup():
        import jax, jax.numpy as jnp
        import numpy as np
        N_NODES = 6250
        N_EDGES = 100000
        IN_CH = 128
        HEADS = 4
        OUT_CH = 32
        NEG_SLOPE = 0.2
        BN_EPS = 1e-05
        key = jax.random.key(seed)
        ks = jax.random.split(key, 8)
        x = jax.random.normal(ks[0], (N_NODES, IN_CH), dtype=jnp.float32)
        edge_index = jax.random.randint(ks[1], (2, N_EDGES), 0, N_NODES, dtype=jnp.int64 if jax.config.jax_enable_x64 else jnp.int32)
        W = jax.random.normal(ks[2], (IN_CH, HEADS * OUT_CH), dtype=jnp.float32) / np.sqrt(IN_CH)
        att_src = jax.random.normal(ks[3], (HEADS, OUT_CH), dtype=jnp.float32) * 0.1
        att_dst = jax.random.normal(ks[4], (HEADS, OUT_CH), dtype=jnp.float32) * 0.1
        bias = jnp.zeros((HEADS * OUT_CH,), dtype=jnp.float32)
        W_res = jax.random.normal(ks[5], (IN_CH, HEADS * OUT_CH), dtype=jnp.float32) / np.sqrt(IN_CH)
        bn_gamma = jnp.ones((HEADS * OUT_CH,), dtype=jnp.float32)
        bn_beta = jnp.zeros((HEADS * OUT_CH,), dtype=jnp.float32)
        bn_mean = jax.random.normal(ks[6], (HEADS * OUT_CH,), dtype=jnp.float32) * 0.1
        bn_var = jax.random.uniform(ks[7], (HEADS * OUT_CH,), dtype=jnp.float32, minval=0.5, maxval=1.5)
        return {'x': x, 'edge_index': edge_index, 'W': W, 'att_src': att_src, 'att_dst': att_dst, 'bias': bias, 'W_res': W_res, 'bn_gamma': bn_gamma, 'bn_beta': bn_beta, 'bn_mean': bn_mean, 'bn_var': bn_var}
    _L3_gnn_all = _L3_gnn_setup()
    _L3_gnn_in = {k: v for k, v in _L3_gnn_all.items() if k in ('W', 'att_src', 'att_dst', 'bias', 'W_res', 'bn_gamma', 'bn_beta', 'bn_mean', 'bn_var')}
    del _L3_gnn_all
    return {'x': x, 'src': src, 'dst': dst, 'edge_attr_128': edge_attr_128, 'edge_attr_64': edge_attr_64, 'L0_gnn_W_e': _L0_gnn_in['W_e'], 'L0_gnn_b_e': _L0_gnn_in['b_e'], 'L0_gnn_a_e': _L0_gnn_in['a_e'], 'L0_gnn_W_n': _L0_gnn_in['W_n'], 'L0_gnn_b_n': _L0_gnn_in['b_n'], 'L1_gnn_W_w': _L1_gnn_in['W_w'], 'L1_gnn_W_b': _L1_gnn_in['W_b'], 'L1_gnn_a_w': _L1_gnn_in['a_w'], 'L1_gnn_a_b': _L1_gnn_in['a_b'], 'L2_gnn_u': _L2_gnn_in['u'], 'L2_gnn_w1': _L2_gnn_in['w1'], 'L2_gnn_b1': _L2_gnn_in['b1'], 'L2_gnn_w2': _L2_gnn_in['w2'], 'L2_gnn_b2': _L2_gnn_in['b2'], 'L2_gnn_w3': _L2_gnn_in['w3'], 'L2_gnn_b3': _L2_gnn_in['b3'], 'L3_gnn_W': _L3_gnn_in['W'], 'L3_gnn_att_src': _L3_gnn_in['att_src'], 'L3_gnn_att_dst': _L3_gnn_in['att_dst'], 'L3_gnn_bias': _L3_gnn_in['bias'], 'L3_gnn_W_res': _L3_gnn_in['W_res'], 'L3_gnn_bn_gamma': _L3_gnn_in['bn_gamma'], 'L3_gnn_bn_beta': _L3_gnn_in['bn_beta'], 'L3_gnn_bn_mean': _L3_gnn_in['bn_mean'], 'L3_gnn_bn_var': _L3_gnn_in['bn_var']}

def reference(x, src, dst, edge_attr_128, edge_attr_64, L0_gnn_W_e, L0_gnn_b_e, L0_gnn_a_e, L0_gnn_W_n, L0_gnn_b_n, L1_gnn_W_w, L1_gnn_W_b, L1_gnn_a_w, L1_gnn_a_b, L2_gnn_u, L2_gnn_w1, L2_gnn_b1, L2_gnn_w2, L2_gnn_b2, L2_gnn_w3, L2_gnn_b3, L3_gnn_W, L3_gnn_att_src, L3_gnn_att_dst, L3_gnn_bias, L3_gnn_W_res, L3_gnn_bn_gamma, L3_gnn_bn_beta, L3_gnn_bn_mean, L3_gnn_bn_var):
    import jax
    import jax.numpy as jnp

    def _L0_gnn_ref(nfeat, efeat, W_e, b_e, a_e, W_n, b_n, src, dst):
        import jax, jax.numpy as jnp
        import numpy as np
        N_NODES = 6250
        N_EDGES = 62500
        D_N = 128
        D_E = 128
        D_EO = 128
        EPS = 1e-05
        SLOPE = 0.01

        def _inst_norm(x):
            mu = jnp.mean(x, axis=1, keepdims=True)
            var = jnp.var(x, axis=1, keepdims=True)
            return (x - mu) * jax.lax.rsqrt(var + EPS)

        def _leaky_relu(x):
            return jnp.where(x >= 0, x, SLOPE * x)
        x = jnp.concatenate([nfeat[src], efeat, nfeat[dst]], axis=1)
        x = _inst_norm(x)
        e = _leaky_relu(x @ W_e.T + b_e)
        attn = e @ a_e
        m = jax.ops.segment_max(attn, dst, num_segments=N_NODES)
        ex = jnp.exp(attn - m[dst])
        denom = jax.ops.segment_sum(ex, dst, num_segments=N_NODES)
        alpha = ex / denom[dst]
        attn_feat = jax.ops.segment_sum(alpha[:, None] * e, dst, num_segments=N_NODES)
        h = jnp.concatenate([nfeat, attn_feat], axis=1)
        h = _inst_norm(h)
        h = _leaky_relu(h @ W_n.T + b_n)
        return h

    def _L1_gnn_ref(features, edge_src, edge_dst, W_w, W_b, a_w, a_b):
        import jax, jax.numpy as jnp
        import numpy as np
        N, F_IN, F_OUT, H, E = (6250, 128, 32, 4, 200000)
        n = features.shape[0]
        h = a_w.shape[0]
        f_out = a_w.shape[1] // 2
        self_idx = jnp.arange(n, dtype=edge_src.dtype)
        src = jnp.concatenate([edge_src, self_idx])
        dst = jnp.concatenate([edge_dst, self_idx])
        key = (features @ W_w + W_b).reshape(n, h, f_out)
        a_dst = a_w[:, :f_out]
        a_src = a_w[:, f_out:]
        s_dst = jnp.einsum('nhf,hf->nh', key, a_dst)
        s_src = jnp.einsum('nhf,hf->nh', key, a_src)
        e = jax.nn.leaky_relu(s_dst[dst] + s_src[src] + a_b, negative_slope=0.2)
        m = jax.ops.segment_max(e, dst, num_segments=n)
        e_exp = jnp.exp(e - m[dst])
        denom = jax.ops.segment_sum(e_exp, dst, num_segments=n)
        alpha = e_exp / denom[dst]
        out = jax.ops.segment_sum(alpha[:, :, None] * key[src], dst, num_segments=n)
        return out.reshape(n, h * f_out)

    def _L2_gnn_ref(x, edge_index, edge_attr, u, batch, w1, b1, w2, b2, w3, b3):
        import jax, jax.numpy as jnp
        import numpy as np
        N_NODES = 6250
        N_EDGES = 100000
        N_GRAPHS = 64
        NEG_SLOPE = 0.01

        def leaky_relu(x):
            return jnp.where(x >= 0, x, NEG_SLOPE * x)
        col = edge_index[1]
        agg = jax.ops.segment_sum(edge_attr, col, num_segments=x.shape[0])
        h = jnp.concatenate([x, agg, u[batch]], axis=1)
        h = leaky_relu(h @ w1 + b1)
        h = leaky_relu(h @ w2 + b2)
        return h @ w3 + b3

    def _L3_gnn_ref(x, edge_index, W, att_src, att_dst, bias, W_res, bn_gamma, bn_beta, bn_mean, bn_var):
        import jax, jax.numpy as jnp
        import numpy as np
        N_NODES = 6250
        N_EDGES = 100000
        IN_CH = 128
        HEADS = 4
        OUT_CH = 32
        NEG_SLOPE = 0.2
        BN_EPS = 1e-05
        N = x.shape[0]
        H, C = att_src.shape
        loops = jnp.arange(N, dtype=edge_index.dtype)
        src = jnp.concatenate([edge_index[0], loops])
        dst = jnp.concatenate([edge_index[1], loops])
        h = (x @ W).reshape(N, H, C)
        a_src = jnp.einsum('nhc,hc->nh', h, att_src)
        a_dst = jnp.einsum('nhc,hc->nh', h, att_dst)
        logits = jax.nn.leaky_relu(a_src[src] + a_dst[dst], NEG_SLOPE)
        m = jax.lax.stop_gradient(jax.ops.segment_max(logits, dst, num_segments=N))
        e = jnp.exp(logits - m[dst])
        s = jax.ops.segment_sum(e, dst, num_segments=N)
        alpha = e / s[dst]
        msg = h[src] * alpha[:, :, None]
        out = jax.ops.segment_sum(msg, dst, num_segments=N).reshape(N, H * C)
        out = out + x @ W_res + bias
        out = (out - bn_mean) * jax.lax.rsqrt(bn_var + BN_EPS) * bn_gamma + bn_beta
        return jax.nn.elu(out)
    edge_index = jnp.stack([src, dst])
    batch0 = jnp.zeros((6250,), jnp.int32)
    x = _layernorm(x + _L0_gnn_ref(x, edge_attr_128, L0_gnn_W_e, L0_gnn_b_e, L0_gnn_a_e, L0_gnn_W_n, L0_gnn_b_n, src, dst), axis=-1)
    x = _layernorm(x + _L1_gnn_ref(x, src, dst, L1_gnn_W_w, L1_gnn_W_b, L1_gnn_a_w, L1_gnn_a_b), axis=-1)
    x = _layernorm(x + _L2_gnn_ref(x, edge_index, edge_attr_64, L2_gnn_u, batch0, L2_gnn_w1, L2_gnn_b1, L2_gnn_w2, L2_gnn_b2, L2_gnn_w3, L2_gnn_b3), axis=-1)
    x = _layernorm(x + _L3_gnn_ref(x, edge_index, L3_gnn_W, L3_gnn_att_src, L3_gnn_att_dst, L3_gnn_bias, L3_gnn_W_res, L3_gnn_bn_gamma, L3_gnn_bn_beta, L3_gnn_bn_mean, L3_gnn_bn_var), axis=-1)
    return x

_drawn_inputs = setup_inputs


def setup_inputs(seed=0):
    import zlib

    import numpy as np

    out = dict(_drawn_inputs(seed))
    spreads = {'L2_gnn_b1': (0.0, 0.483),
     'L2_gnn_b2': (0.0, 0.1),
     'L2_gnn_b3': (0.0, 0.1),
     'L3_gnn_bias': (0.0, 0.1),
     'L3_gnn_bn_gamma': (1.0, 0.2),
     'L3_gnn_bn_beta': (0.0, 0.1)}
    factors = {'L0_gnn_b_e': 8.0, 'L0_gnn_b_n': 7.524, 'L1_gnn_a_w': 2.737, 'L1_gnn_a_b': 30.31}
    for name, (base, spread) in spreads.items():
        noise = np.random.default_rng([zlib.crc32(name.encode()), seed]).standard_normal(out[name].shape)
        drawn = base * np.exp(spread * noise) if base else spread * noise
        out[name] = jnp.asarray(drawn.astype(out[name].dtype))
    for name, factor in factors.items():
        out[name] = (out[name] * factor).astype(out[name].dtype)
    return out
```

```python
import concourse.bass as bass
from concourse import mybir
from contextlib import ExitStack

P = 128
N = 6250
E = 106250
D = 128
H = 4
F = D // H
DU = 64
TC = 32
CH = -(-E // (P * TC))
NT = CH * TC
EP = NT * P
PAIRS = CH // 2
SB = 8
NSB = TC // SB
GN = 256
GK = GN // P
NP_ = 26 * GN
GROUPS = NP_ // GN
GPAIRS = GROUPS // 2
ZW = D + 2
KW = D + H
TW = D + 2 * H
OHT_RING, S_RING, AGG_RING = 8, 16, 4
BIG = -1.0e30
EPS = 1e-5
TINY = 1e-30
LAST_FULL = (E - (CH - 1) * TC * P) // P
LAST_REST = E - (E // P) * P

EXP_CREDIT, OHT_CREDIT, SQ_CREDIT, ACC_CREDIT, AGG_CREDIT = 2 * SB, 2 * SB, 2 * SB, 2 * TC, S_RING

DTF_READY, STF_READY, DCOL_READY, NEXT_READY, BN_VAR, CENTRED, SETUP_DONE = 1, 2, 7, 8, 16, 22, 95
N_WEIGHTS = 33

NODE_BUFFERS = {"x": 0, "xt": 256, "xt2": 512, "at": 768, "at2": 1024, "tmp": 1280, "h": 1536, "new": 1792,
                "newt": 2048, "tab": 2304, "h1": 2824, "h2": 3336, "small": 3848}

STEPS = {"edges0": 64, "edges1": 36, "edges2": 32, "nodes0": 0, "nodes1": 24, "nodes2": 18, "nodes3": 18}


def graph_kernel(nc, t, out):
    nc.disable_value_cache = True
    f32, i32, bf16 = mybir.dt.float32, mybir.dt.int32, mybir.dt.bfloat16
    ALU, ACT, AX = mybir.AluOpType, mybir.ActivationFunctionType, mybir.AxisListType
    ctx = ExitStack()
    with ctx:
        def sb(name, shape, dt=f32):
            return ctx.enter_context(nc.sbuf_tensor(name, shape, dt))

        def sem(name):
            return ctx.enter_context(nc.semaphore(name))

        def dram(name, shape, dt=f32):
            return nc.dram_tensor(name, shape, dt, kind="Internal").ap()

        dst_pad = dram("dst_pad", [EP], i32)
        x_pad = dram("x_pad", [NP_, D])
        x1_pad = dram("x1_pad", [NP_, D])
        x3_pad = dram("x3_pad", [NP_, D])
        src_tab = [dram("src_tab0", [NP_, ZW]), dram("src_tab1", [NP_, KW]), dram("src_tab3", [NP_, KW])]
        dst_tab = [dram("dst_tab0", [NP_, ZW]), dram("dst_tab1", [NP_, H]), dram("dst_tab3", [NP_, H])]

        acc = sb("acc", [P, 2, NP_])
        pen_f = sb("pen_f", [P, CH, P], bf16)
        pen_r = sb("pen_r", [P, CH, P], bf16)
        pen_first = sb("pen_first", [P, CH, P], bf16)
        pen_last = sb("pen_last", [P, CH, P], bf16)
        pen_join = sb("pen_join", [P, NT + 1], bf16)
        carry_f = sb("carry_f", [P, NT + 1], bf16)
        carry_r = sb("carry_r", [P, CH, TC], bf16)
        rel = sb("rel", [P, NT])
        nodew = sb("nodew", [P, NT])
        times = sb("times", [P, NT], bf16)
        src_i = sb("src_i", [P, NT], mybir.dt.uint16)
        first_i = sb("first_i", [1, NT], i32)
        idx = sb("idx", [P, 2, TC], i32)
        gall = sb("gall", [P, 2 * TC * KW])
        ze = sb("ze", [P, TC, ZW])
        s_oh = sb("s_oh", [P, S_RING, P])
        efr = sb("efr", [P, 2, SB, D])
        dst_row = sb("dst_row", [P, 2, SB * P], i32)
        oht = sb("oht", [P, OHT_RING, P])
        eft = sb("eft", [P, 2, 4 * P])
        win = sb("win", [P, 2, SB, ZW])
        lg = sb("lg", [P, P])
        lg2 = sb("lg2", [P, P])
        mx = sb("mx", [P, P])
        mx2 = sb("mx2", [P, P])
        ext = sb("ext", [P, P])
        ex = sb("ex", [P, P])
        blk = sb("blk", [P, 8, 32])
        cin = sb("cin", [P, 2, 33])
        att = sb("att", [P, 8, TC])
        fac = sb("fac", [P, 2])
        junk = sb("junk", [P, 2, P])
        ident = sb("ident", [P, P])
        sel = sb("sel", [P, P])
        iota_row = sb("iota_row", [P, P])
        col_i = sb("col_i", [P, 2], i32)
        cols = sb("cols", [P, 8])
        w_sd = sb("w_sd", [P, 2 * ZW])
        w_ef = sb("w_ef", [P, ZW])
        w_n = sb("w_n", [P, 2, ZW])
        w_t = sb("w_t", [P, 2, TW])
        b_t = sb("b_t", [P, 2, TW])
        w1 = sb("w1", [P, 2, 256])
        w1u = sb("w1u", [DU, 256])
        w2 = sb("w2", [P, 2, 256])
        w3 = sb("w3", [P, 2, D])
        w_res = sb("w_res", [P, D])
        rows = sb("rows", [P, 4, D])
        vec = sb("vec", [P, 16])
        be, ae, bn_row, b3_row = (rows[:, k, :] for k in range(4))
        eps, den_mask, attr_mask, one_c, iota_c = (cols[:, k:k + 1] for k in range(5))
        b1_c, b2_c, bn_scale, bn_shift = vec[:, 0:2], vec[:, 2:4], vec[:, 4:5], vec[:, 5:6]
        bn_raw = vec[:, 6:11]

        def g(q, j, width=KW):
            return gall[:, (q * TC + j) * KW:(q * TC + j) * KW + width]

        def gq(q):
            return gall[:, q * TC * KW:(q + 1) * TC * KW].rearrange("p (j d) -> p j d", d=KW)

        def nb(name, p, width=GN):
            at = p * TC * KW + NODE_BUFFERS[name]
            return gall[:, at:at + width]

        bank = [ctx.enter_context(nc.psum_tensor(f"bank{k}", [P, 512], f32)) for k in range(2)]
        zb = ctx.enter_context(nc.psum_tensor("zb", [P, 2, 512], f32))
        bank += [zb[:, 0, :], zb[:, 1, :]]
        bank += [ctx.enter_context(nc.psum_tensor(f"bank{k}", [P, 512], f32)) for k in range(4, 8)]

        def agg_ps(slot):
            return bank[(0, 1, 4, 5)[slot]][:, 0:2 * P]

        efb = bank[4:6]
        lt_ps, ex_ps = bank[6][:, 0:P], bank[7][:, 0:P]

        weights_in = sem("weights_in")
        edges_in = sem("edges_in")
        consts = sem("consts")
        padded = sem("padded")
        w1_zero = sem("w1_zero")
        bn_std = sem("bn_std")
        setup_dve = sem("setup_dve")
        setup_pe = sem("setup_pe")
        pads_out = sem("pads_out")
        chain = sem("chain")
        row_in = [sem(f"row_in{k}") for k in range(2)]
        win_in = [sem(f"win_in{k}") for k in range(2)]
        ef_in = [sem(f"ef_in{k}") for k in range(2)]
        gather_in = [[sem(f"gather_in{q}{k}") for k in range(NSB)] for q in range(2)]
        idx_ready = sem("idx_ready")
        oht_ready = sem("oht_ready")
        s_ready = sem("s_ready")
        expanded = sem("expanded")
        agg_done = sem("agg_done")
        acc_done = sem("acc_done")
        ef_turned = sem("ef_turned")
        eft_copied = sem("eft_copied")
        squared = sem("squared")
        z_copied = sem("z_copied")
        var_ready = sem("var_ready")
        std_ready = sem("std_ready")
        logits_ready = sem("logits_ready")
        logits_turned = sem("logits_turned")
        shifted = sem("shifted")
        weights_t = sem("weights_t")
        weights_turned = sem("weights_turned")
        ex_ready = sem("ex_ready")
        fac_arg = sem("fac_arg")
        fac_ready = sem("fac_ready")
        values_weighted = sem("values_weighted")
        attr_copied = sem("attr_copied")
        den_cols = sem("den_cols")
        host = sem("host")
        x_in = [sem(f"x_in{p}") for p in range(2)]
        x_turned = sem("x_turned")
        x_copied = sem("x_copied")
        x_squared = sem("x_squared")
        den_picked = sem("den_picked")
        attn_ready = sem("attn_ready")
        attn_squared = sem("attn_squared")
        attn_turned = sem("attn_turned")
        norm_done = sem("norm_done")
        norm_var = sem("norm_var")
        norm_std = sem("norm_std")
        ln_var = sem("ln_var")
        ln_std = sem("ln_std")
        mid_ready = sem("mid_ready")
        mid_turned = sem("mid_turned")
        mid_copied = sem("mid_copied")
        h_done = sem("h_done")
        h_biased = sem("h_biased")
        h_ready = sem("h_ready")
        h3_done = sem("h3_done")
        x_new = sem("x_new")
        new_turned = sem("new_turned")
        new_copied = sem("new_copied")
        tab_done = sem("tab_done")
        tab_copied = sem("tab_copied")
        tab_out = [sem(f"tab_out{p}") for p in range(2)]
        rows_out = [sem(f"rows_out{p}") for p in range(2)]
        res_done = sem("res_done")
        elu_arg = sem("elu_arg")
        elu_exp = sem("elu_exp")
        zeroed = sem("zeroed")

        dti = gall[:, 0:CH * P].bitcast(i32).rearrange("p (c e) -> p c e", e=P)
        dtf = gall[:, CH * P:2 * CH * P].rearrange("p (c e) -> p c e", e=P)
        sti = ze[:, :, :].rearrange("p a b -> p (a b)")[0:TC, 0:CH * P].bitcast(i32).rearrange("p (c e) -> p c e", e=P)
        stf = acc[0:TC, 0, 0:CH * P].rearrange("p (c e) -> p c e", e=P)
        dcol = acc[:, 1, 0:NT]
        first_b = acc[:, 1, NT:2 * NT]
        last_b = acc[:, 1, 2 * NT:3 * NT]
        diff = acc[:, 0, 3400:3400 + CH * P // 2]
        pen_single = acc[:, 1, 3 * NT:4 * NT]
        pick = acc[:, 1, 4 * NT:4 * NT + 2 * P].rearrange("p (k m) -> p k m", k=2)
        iota_i = acc[:, 0, 5100:5100 + P].bitcast(i32)
        pen_join_f = acc[:, 1, 5 * NT:6 * NT + 1]
        tile_tmp = acc[:, 1, 6 * NT + 8:7 * NT + 8]
        zeros = s_oh[:, 0:8, :].rearrange("p a b -> p (a b)")
        we_raw = efr[:, 0, 0:3, :].rearrange("p a b -> p (a b)")
        wn_raw = efr[:, 0, 3:5, :].rearrange("p a b -> p (a b)")
        a_raw = efr[:, 1, 0:4, :]
        prod = efr[:, 1, 4:6, :]
        b_raw = efr[:, 1, 6, :]
        ab_raw = efr[:, 1, 7, 0:H]
        u_col = efr[0:DU, 0, 5, 0:1]
        rsum = att[:, 0, 0:8]

        block = ctx.enter_context(nc.Block())


        def nth(counted_in, phase, i, p):
            return counted_in.index(str(phase)) * GROUPS + 2 * i + p + 1

        def started(i):
            return not (isinstance(i, int) and i == 0)

        def group_pairs(engine, body):
            body(0)
            with engine.Fori(1, GPAIRS) as i:
                body(i)

        def group_rows(tab, i, p):
            return tab[bass.ds((2 * i + p) * GN, GN), :].rearrange("(k n) d -> n k d", n=P)

        def tiles(ap):
            return ap.rearrange("p (k d) -> p k d", k=GK)

        @block.sync
        def _(sp):
            def tile_rows(a, tile0, n):
                return a[tile0 * P:(tile0 + n) * P].rearrange("(t e) -> t e", e=P)

            def raw_indices(into, a, r0, skip=0):
                a = a[skip:E]
                sp.dma_start(into[r0:r0 + TC, 0:CH - 1, :],
                             tile_rows(a, 0, (CH - 1) * TC).rearrange("(c j) e -> j c e", j=TC)).then_inc(edges_in, 16)
                sp.dma_start(into[r0:r0 + LAST_FULL, CH - 1, :],
                             tile_rows(a, (CH - 1) * TC, LAST_FULL)).then_inc(edges_in, 16)
                sp.dma_start(into[r0 + LAST_FULL:r0 + LAST_FULL + 1, CH - 1, 0:LAST_REST - skip],
                             a[E - LAST_REST:E - skip].unsqueeze(0)).then_inc(edges_in, 16)

            sp.wait_ge(padded, 2)
            for h in range(H):
                raw_indices(dti, t["dst"], TC * h)
            raw_indices(sti, t["src"], 0)

            def load_weight(into, a):
                sp.dma_start(into, a).then_inc(weights_in, 16)

            load_weight(we_raw, t["L0_gnn_W_e"])
            load_weight(wn_raw, t["L0_gnn_W_n"])
            load_weight(be, t["L0_gnn_b_e"].partition_broadcast(P))
            load_weight(ae, t["L0_gnn_a_e"].partition_broadcast(P))
            load_weight(bn_row, t["L0_gnn_b_n"].partition_broadcast(P))
            load_weight(b3_row, t["L2_gnn_b3"].partition_broadcast(P))
            load_weight(w_t[:, 0, 0:D], t["L1_gnn_W_w"])
            load_weight(w_t[:, 1, 0:D], t["L3_gnn_W"])
            for k, a in enumerate((t["L1_gnn_a_w"][:, F:2 * F], t["L1_gnn_a_w"][:, 0:F],
                                   t["L3_gnn_att_src"], t["L3_gnn_att_dst"])):
                load_weight(a_raw[:, k, :].rearrange("p (h f) -> p h f", h=H), a.partition_broadcast(P))
            load_weight(b_t[:, 0, 0:D], t["L1_gnn_W_b"].partition_broadcast(P))
            load_weight(ab_raw, t["L1_gnn_a_b"].partition_broadcast(P))
            load_weight(w1[:, 0, :], t["L2_gnn_w1"][0:D, :])
            sp.wait_ge(w1_zero, 1)
            for h in range(H):
                load_weight(w1[F * h + F // 2:F * h + F, 1, :], t["L2_gnn_w1"][D + F // 2 * h:D + F // 2 * (h + 1), :])
            load_weight(w1u[:, :], t["L2_gnn_w1"][D + DU:D + 2 * DU, :])
            load_weight(u_col, t["L2_gnn_u"][0, :].unsqueeze(1))
            load_weight(w2[:, :, :], t["L2_gnn_w2"].rearrange("(k p) n -> p k n", p=P))
            load_weight(w3[:, :, :], t["L2_gnn_w3"].rearrange("(k p) n -> p k n", p=P))
            load_weight(w_res[:, :], t["L3_gnn_W_res"])
            for k in range(2):
                load_weight(b1_c[:, k:k + 1], t["L2_gnn_b1"][k * P:k * P + P].unsqueeze(1))
                load_weight(b2_c[:, k:k + 1], t["L2_gnn_b2"][k * P:k * P + P].unsqueeze(1))
            for k, name in enumerate(("bias", "bn_mean", "bn_var", "bn_gamma", "bn_beta")):
                load_weight(bn_raw[:, k:k + 1], t["L3_gnn_" + name].unsqueeze(1))

            sp.wait_ge(padded, 4)
            raw_indices(sti, t["dst"], 0, skip=1)

            sp.wait_ge(edges_in, 16 * 18)
            sp.dma_start(dst_pad.rearrange("(c j e) -> j c e", j=TC, e=P), dti[0:TC, :, :]).then_inc(pads_out, 16)
            sp.dma_start(x_pad[0:N, :], t["x"]).then_inc(pads_out, 16)
            sp.wait_ge(padded, 3)
            rest = (NP_ - N) // 7
            sp.dma_start(x_pad[N:NP_, :].rearrange("(p r) d -> p (r d)", r=7), zeros[0:rest, 0:7 * D]).then_inc(pads_out, 16)
            sp.wait_ge(pads_out, 48)

            def node_io(phase, x_from, store, x_free):
                def body(i):
                    for p in range(2):
                        if started(i):
                            x_free(i - 1, p)
                        sp.dma_start(tiles(nb("x", p)), group_rows(x_from, i, p)).then_inc(x_in[p], 16)
                        if started(i):
                            store(i - 1, p)
                group_pairs(sp, body)
                for p in range(2):
                    x_free(GPAIRS - 1, p)
                    store(GPAIRS - 1, p)

            def store_tables(layer, i, p, w0, w1_):
                tab = nb("tab", p, GK * (w0 + w1_)).rearrange("p (k w) -> p k w", k=GK)
                sp.dma_start(group_rows(src_tab[layer], i, p), tab[:, :, 0:w0]).then_inc(tab_out[p], 16)
                sp.dma_start(group_rows(dst_tab[layer], i, p), tab[:, :, w0:w0 + w1_]).then_inc(tab_out[p], 16)

            def store0(i, p):
                sp.wait_ge(tab_copied, nth("012", 0, i, p))
                store_tables(0, i, p, ZW, ZW)

            def free0(i, p):
                sp.wait_ge(x_turned, nth("013", 0, i, p))
                sp.wait_ge(x_squared, nth("01", 0, i, p))

            def store_gat(phase, x_to):
                def store(i, p):
                    sp.dma_start(group_rows(x_to, i, p), tiles(nb("new", p))).then_inc(tab_out[p], 16)
                    sp.wait_ge(tab_copied, nth("012", phase, i, p))
                    store_tables(phase, i, p, KW, H)
                return store

            def free_new(phase):
                return lambda i, p: sp.wait_ge(x_new, nth("123", phase, i, p))

            def edge_io(k, attr, width):
                regs = [sp.alloc_register(f"sp_first{k}_{m}") for m in range(SB)]

                def body(i, last=False):
                    for q in range(2):
                        for s in range(NSB):
                            u = 2 * NSB * i + (NSB * q + s + NSB * CH * k)
                            tile0 = 2 * TC * i + (q * TC + s * SB)
                            slot = s % 2
                            sp.wait_ge(oht_ready, u * SB + (OHT_CREDIT - SB))
                            sp.dma_start(dst_row[:, slot, :],
                                         dst_pad[bass.ds(tile0 * P, SB * P)].partition_broadcast(P)).then_inc(row_in[slot], 16)
                            sp.load(regs, first_i[0:1, bass.ds(tile0, SB)])
                            sp.wait_ge(expanded, u * SB + (EXP_CREDIT - SB))
                            for m in range(SB):
                                v = sp.snap(regs[m], min_val=0, max_val=N)
                                w = ZW if k == 0 else H
                                sp.dma_start(win[:, slot, m, 0:w], dst_tab[k][bass.ds(v, P), :]).then_inc(win_in[slot], 16)
                            if attr is None:
                                continue
                            if k == 0:
                                sp.wait_ge(squared, u * SB + (SQ_CREDIT - SB))
                            else:
                                sp.wait_ge(attr_copied, 2 * NSB * i + (NSB * q + s) + 1)
                            full = max(0, min(SB, LAST_FULL - s * SB)) if last and q == 1 else SB
                            for lo, hi in ((0, 6), (6, SB)):
                                if full >= hi:
                                    sp.dma_start(efr[:, slot, lo:hi, 0:width],
                                                 attr[bass.ds(tile0 * P + lo * P, (hi - lo) * P), :]
                                                 .rearrange("(j p) d -> p j d", p=P)).then_inc(ef_in[slot], 16)
                                else:
                                    assert lo == full
                                    sp.dma_start(efr[0:LAST_REST, slot, lo, 0:width],
                                                 attr[E - LAST_REST:E, :]).then_inc(ef_in[slot], 16)
                with sp.Fori(0, PAIRS - 1) as i:
                    body(i)
                body(PAIRS - 1, last=True)

            sp.wait_ge(setup_dve, SETUP_DONE)
            node_io(0, x_pad, store0, free0)
            for p in range(2):
                sp.wait_ge(tab_out[p], 32 * GPAIRS)
            edge_io(0, t["edge_attr_128"], D)
            sp.wait_ge(acc_done, NT + ACC_CREDIT)
            node_io(1, x_pad, store_gat(1, x1_pad), free_new(1))
            for p in range(2):
                sp.wait_ge(tab_out[p], (32 + 48) * GPAIRS)
            edge_io(1, t["edge_attr_64"], DU)
            sp.wait_ge(acc_done, 2 * NT + ACC_CREDIT)
            node_io(2, x1_pad, store_gat(2, x3_pad), free_new(2))
            for p in range(2):
                sp.wait_ge(tab_out[p], (32 + 96) * GPAIRS)
            edge_io(2, None, 0)
            sp.wait_ge(acc_done, 3 * NT + ACC_CREDIT)

            def store_out(i, p):
                here = GN if not isinstance(i, int) else min(GN, N - (2 * i + p) * GN)
                if here == GN:
                    sp.dma_start(group_rows(out, i, p), tiles(nb("new", p))).then_inc(rows_out[p], 16)
                elif here > 0:
                    assert here <= P
                    sp.dma_start(out[N - here:N, :], nb("new", p)[0:here, 0:D]).then_inc(rows_out[p], 16)

            node_io(3, x3_pad, store_out, free_new(3))
            for p in range(2):
                stored = GPAIRS - 1 + (N > (GROUPS - 2 + p) * GN)
                sp.wait_ge(rows_out[p], 16 * stored)

        @block.gpsimd
        def _(pool):
            pool.memset(dti[:, :, :], N).then_inc(padded, 1)
            pool.memset(sti[:, :, :], 0).then_inc(padded, 1)
            pool.memset(zeros, 0.0).then_inc(padded, 1)
            pool.memset(ident[:, :], 0.0).then_inc(consts, 1)
            pool.memset(sel[:, :], 0.0).then_inc(consts, 1)
            pool.memset(w1[:, 1, :], 0.0).then_inc(w1_zero, 1)
            pool.memset(pick, 0.0).then_inc(consts, 1)
            pool.wait_ge(setup_dve, STF_READY)
            pool.memset(sti[:, :, :], N).then_inc(padded, 1)
            pool.iota(iota_i, [[1, P]], 0, 0).then_inc(consts, 1)
            pool.iota(col_i[:, :], [[0, 2]], 0, 1).then_inc(consts, 1)
            pool.wait_ge(consts, 5)
            pool.affine_select(out=ident[:, :], in_=ident[:, :], compare_op=ALU.not_equal, fill=1.0,
                               base=0, pattern=[[-1, P]], channel_multiplier=1).then_inc(consts, 1)
            s4 = sel[:, :].rearrange("p (h f) -> p h f", h=H)
            pool.affine_select(out=s4, in_=s4, compare_op=ALU.not_equal, fill=1.0,
                               base=0, pattern=[[-F, H], [0, F]], channel_multiplier=1).then_inc(consts, 1)
            pool.affine_select(out=pick, in_=pick, compare_op=ALU.not_equal, fill=1.0,
                               base=0, pattern=[[-(P - 1), 2], [0, P]], channel_multiplier=1).then_inc(consts, 1)

            def gathers(k):
                width = ZW if k == 0 else KW

                def body(i):
                    for q in range(2):
                        gc = 2 * i + (q + CH * k)
                        pool.wait_ge(acc_done, gc * TC + (ACC_CREDIT - TC))
                        pool.sem_inc(host, 1)
                        pool.tensor_copy(idx[:, q, :], src_i[:, bass.ds(2 * TC * i + q * TC, TC)]).then_inc(idx_ready, 1)
                        pool.wait_ge(idx_ready, gc + 1)
                        pool.sem_inc(host, 1)
                        for j in range(TC):
                            pool.indirect_dma_start(g(q, j, width), None, src_tab[k],
                                                    bass.IndirectOffsetOnAxis(idx[:, q, j:j + 1], 0)
                                                    ).then_inc(gather_in[q][j // SB], 16)
                with pool.Fori(0, PAIRS) as i:
                    body(i)

            def clear_acc(n):
                pool.memset(acc[:, :, :], 0.0).then_inc(zeroed, 1)

            pool.wait_ge(setup_dve, SETUP_DONE)
            clear_acc(1)
            for p in range(2):
                pool.wait_ge(tab_out[p], 32 * GPAIRS)
            gathers(0)
            pool.wait_ge(norm_done, nth("1", 1, GPAIRS - 1, 1))
            clear_acc(2)
            for p in range(2):
                pool.wait_ge(tab_out[p], (32 + 48) * GPAIRS)
            gathers(1)
            pool.wait_ge(h_ready, 2 * GROUPS)
            clear_acc(3)
            for p in range(2):
                pool.wait_ge(tab_out[p], (32 + 96) * GPAIRS)
            gathers(2)

        @block.scalar
        def _(act):
            act.sem_inc(eft_copied, 2)
            act.sem_inc(z_copied, 1)
            act.sem_inc(squared, SQ_CREDIT)
            act.sem_inc(attr_copied, 2)
            act.wait_ge(setup_dve, BN_VAR)
            nc.scalar.activation(vec[:, 11:12], bn_raw[:, 2:3], ACT.Sqrt, bias=eps).then_inc(bn_std, 1)

            def nodes0(i):
                for p in range(2):
                    act.wait_ge(x_turned, nth("013", 0, i, p))
                    if started(i):
                        act.wait_ge(tab_done, nth("012", 0, i - 1, p))
                    nc.scalar.activation(nb("xt", p), bank[4 * p][:, 0:GN], ACT.Copy).then_inc(x_copied, 1)
                    if started(i):
                        act.wait_ge(tab_copied, nth("012", 0, i - 1, p))
                    for kk in range(GK):
                        ins = nc.scalar.activation(nb("xt2", p)[:, kk * P:kk * P + P], nb("x", p)[:, kk * P:kk * P + P],
                                                   ACT.Square, accum_out=nb("small", p, 2)[:, kk:kk + 1])
                    ins.then_inc(x_squared, 1)

            def chunk_tail(gc):
                act.wait_ge(shifted, gc + 1)
                nc.scalar.activation(ext[:, :], lg[:, :], ACT.Exp).then_inc(weights_t, 1)
                act.wait_ge(fac_arg, gc + 1)
                nc.scalar.activation(fac[:, 0:1], blk[:, 0, 0:1], ACT.Exp).then_inc(fac_ready, 1)

            def edges0(i):
                for q in range(2):
                    gc = 2 * i + q
                    act.wait_ge(acc_done, gc * TC + ACC_CREDIT)

                    def copy_turned(g4):
                        gg = 2 * 8 * i + (q * 8 + g4)
                        act.wait_ge(ef_turned, gg + 1)
                        act.wait_ge(expanded, 4 * gg + (EXP_CREDIT - 4))
                        nc.scalar.activation(eft[:, g4 % 2, :], efb[g4 % 2][:, :], ACT.Copy).then_inc(eft_copied, 1)

                    copy_turned(0)
                    for g4 in range(8):
                        if g4 + 1 < 8:
                            copy_turned(g4 + 1)
                        gg = 2 * 8 * i + (q * 8 + g4)
                        act.wait_ge(ef_in[(g4 // 2) % 2], 128 * i + (64 * q + 32 * (g4 // 4) + 32))
                        for m in range(4):
                            j = 4 * g4 + m
                            tt = 2 * TC * i + (q * TC + j)
                            act.wait_ge(squared, tt + (SQ_CREDIT - 1))
                            nc.scalar.activation(junk[:, m % 2, :], efr[:, (g4 // 2) % 2, j % SB, :], ACT.Square,
                                                 accum_out=att[:, 0, j:j + 1]).then_inc(squared, 1)
                        act.wait_ge(expanded, 4 * gg + 4 + EXP_CREDIT)
                        nc.scalar.activation(ze[:, 4 * g4:4 * g4 + 4, :].rearrange("p (a b) d -> p a b d", a=2),
                                             zb[:, :, 0:2 * ZW].rearrange("p a (b d) -> p a b d", b=2),
                                             ACT.Copy).then_inc(z_copied, 1)
                    act.wait_ge(var_ready, gc + 1)
                    nc.scalar.activation(att[:, 3, :], att[:, 2, :], ACT.Sqrt, bias=eps).then_inc(std_ready, 1)
                    chunk_tail(gc)
                    act.wait_ge(ex_ready, gc + 1)
                    for j in range(TC):
                        ins = nc.scalar.activation(ze[:, j, 0:D], ze[:, j, 0:D], ACT.Copy, scale=ex[:, j:j + 1])
                        if j % SB == SB - 1:
                            ins.then_inc(values_weighted, 1)

            def edges1(i):
                for q in range(2):
                    gc = 2 * i + (q + CH)
                    act.wait_ge(acc_done, gc * TC + ACC_CREDIT)
                    for s in range(NSB):
                        act.wait_ge(ef_in[s % 2], 128 * i + (64 * q + 32 * (s // 2) + 32) + 64 * CH)
                        nc.scalar.activation(
                            ze[:, s * SB:s * SB + SB, 0:D].rearrange("p j (h x) -> p j h x", h=H)[:, :, :, F // 2:F],
                            efr[:, s % 2, :, 0:DU].rearrange("p j (h x) -> p j h x", h=H), ACT.Copy).then_inc(attr_copied, 1)
                    chunk_tail(gc)
                    act.wait_ge(ex_ready, gc + 1)
                    nc.scalar.activation(
                        ze[:, :, 0:D].rearrange("p j (h x) -> p j h x", h=H)[:, :, :, 0:F // 2],
                        ex[:, :].rearrange("p (h j) -> p j h", h=H).unsqueeze(3).to_broadcast([P, TC, H, F // 2]),
                        ACT.Copy).then_inc(den_cols, 1)

            def edges2(i):
                for q in range(2):
                    gc = 2 * i + (q + 2 * CH)
                    act.wait_ge(acc_done, gc * TC + ACC_CREDIT)
                    chunk_tail(gc)
                    act.wait_ge(ex_ready, gc + 1)
                    nc.scalar.activation(
                        ze[:, :, 0:D].rearrange("p j (h x) -> p j h x", h=H),
                        ex[:, :].rearrange("p (h j) -> p j h", h=H).unsqueeze(3).to_broadcast([P, TC, H, F]),
                        ACT.Copy).then_inc(den_cols, 1)

            def sqrt_step(wait_on, count, out_ap, in_ap, scale, done):
                act.wait_ge(wait_on, count)
                nc.scalar.activation(out_ap, in_ap, ACT.Sqrt, bias=eps, scale=scale).then_inc(done, 1)

            def turn_new(phase, i, p, bank_ap):
                act.wait_ge(new_turned, nth("12", phase, i, p))
                if started(i):
                    act.wait_ge(tab_done, nth("012", phase, i - 1, p))
                nc.scalar.activation(nb("newt", p), bank_ap, ACT.Copy).then_inc(new_copied, 1)

            def nodes1(i):
                for p in range(2):
                    act.wait_ge(x_turned, nth("013", 1, i, p))
                    if started(i):
                        act.wait_ge(norm_done, nth("1", 1, i - 1, p))
                    nc.scalar.activation(nb("xt", p), bank[4 * p][:, 0:GN], ACT.Copy).then_inc(x_copied, 1)
                    nc.scalar.activation(nb("xt2", p), bank[4 * p][:, 0:GN], ACT.Square).then_inc(x_squared, 1)
                    act.wait_ge(attn_ready, nth("123", 1, i, p))
                    nc.scalar.activation(nb("at2", p), nb("at", p), ACT.Square).then_inc(attn_squared, 1)
                    sm = nb("small", p, 40)
                    sqrt_step(norm_var, nth("1", 1, i, p), sm[:, 6:8], sm[:, 4:6], 1.0, norm_std)
                    mv = sm[:, 24:28].rearrange("p (k s) -> p k s", k=GK)
                    sqrt_step(ln_var, nth("1", 1, i, p), sm[:, 28:30], mv[:, :, 1], 1.0, ln_std)
                    turn_new(1, i, p, bank[4 * p + 2][:, 0:GN])

            def nodes2(i):
                for p in range(2):
                    sm = nb("small", p, 40)
                    mv = sm[:, 24:28].rearrange("p (k s) -> p k s", k=GK)
                    gn = 2 * i + p
                    sqrt_step(ln_var, GROUPS + 2 * gn + 1, sm[:, 28:30], mv[:, :, 1], 1.0, ln_std)
                    act.wait_ge(mid_turned, gn + 1)
                    if started(i):
                        act.wait_ge(h_done, 2 * gn - 3)
                    nc.scalar.activation(nb("xt", p), bank[4 * p + 1][:, 0:GN], ACT.Copy).then_inc(mid_copied, 1)
                    for layer, (buf, bias) in enumerate((("h1", b1_c), ("h2", b2_c))):
                        act.wait_ge(h_done, 2 * gn + 1 + layer)
                        if started(i):
                            act.wait_ge(h3_done, gn - 1)
                        for o in range(2):
                            ins = nc.scalar.activation(nb(buf, p, 2 * GN)[:, o * GN:o * GN + GN],
                                                       bank[4 * p + 2 + layer][:, o * GN:o * GN + GN],
                                                       ACT.Identity, bias=bias[:, o:o + 1])
                        ins.then_inc(h_biased, 1)
                    sqrt_step(ln_var, GROUPS + 2 * gn + 2, sm[:, 28:30], mv[:, :, 1], 1.0, ln_std)
                    turn_new(2, i, p, bank[4 * p + 1][:, GN:2 * GN])

            def nodes3(i):
                for p in range(2):
                    act.wait_ge(x_turned, nth("013", 3, i, p))
                    if started(i):
                        act.wait_ge(res_done, nth("3", 3, i - 1, p))
                    nc.scalar.activation(nb("xt", p), bank[4 * p][:, 0:GN], ACT.Copy).then_inc(x_copied, 1)
                    act.wait_ge(elu_arg, nth("3", 3, i, p))
                    nc.scalar.activation(nb("at2", p), nb("tmp", p), ACT.Exp).then_inc(elu_exp, 1)
                    sm = nb("small", p, 40)
                    mv = sm[:, 24:28].rearrange("p (k s) -> p k s", k=GK)
                    sqrt_step(ln_var, 3 * GROUPS + 2 * i + p + 1, sm[:, 28:30], mv[:, :, 1], 1.0, ln_std)

            group_pairs(act, nodes0)
            with act.Fori(0, PAIRS) as i:
                edges0(i)
            group_pairs(act, nodes1)
            with act.Fori(0, PAIRS) as i:
                edges1(i)
            group_pairs(act, nodes2)
            with act.Fori(0, PAIRS) as i:
                edges2(i)
            group_pairs(act, nodes3)

        @block.tensor
        def _(pe):
            mm = nc.tensor.matmul
            pe.sem_inc(expanded, EXP_CREDIT)
            pe.sem_inc(agg_done, AGG_CREDIT)

            pe.wait_ge(consts, 8)
            pe.wait_ge(setup_dve, DTF_READY)
            for c in range(CH):
                ins = nc.tensor.transpose(bank[c // 16][:, TC * (c % 16):TC * (c % 16) + TC], dtf[0:TC, c, :], ident[0:TC, 0:TC])
            ins.then_inc(setup_pe, 1)
            pe.wait_ge(setup_dve, STF_READY)
            for c in range(CH):
                ins = nc.tensor.transpose(zb[:, c // 16, TC * (c % 16):TC * (c % 16) + TC], stf[:, c, :], ident[0:TC, 0:TC])
            ins.then_inc(setup_pe, 1)
            pe.wait_ge(setup_dve, DCOL_READY)
            for k in range(2):
                for n in range(2):
                    lo, hi = 512 * n, min(512 * n + 512, NT)
                    ins = mm(bank[4 + 2 * k + n][:, 0:hi - lo], pick[:, k, :], dcol[:, lo:hi], start=True, stop=True)
            ins.then_inc(setup_pe, 1)
            pe.wait_ge(setup_dve, NEXT_READY)
            for c in range(CH):
                ins = nc.tensor.transpose(zb[:, c // 16, TC * (c % 16):TC * (c % 16) + TC], stf[:, c, :], ident[0:TC, 0:TC])
            ins.then_inc(setup_pe, 1)
            pe.wait_ge(setup_dve, CENTRED)
            for k in range(3):
                nc.tensor.transpose(bank[0][:, k * P:k * P + P], we_raw[:, k * P:k * P + P], ident[:, :])
            for k in range(2):
                nc.tensor.transpose(bank[1][:, k * P:k * P + P], wn_raw[:, k * P:k * P + P], ident[:, :])
            for o in range(2):
                ins = mm(bank[1][:, 2 * P + o:2 * P + o + 1], w1u[:, o * P:o * P + P], u_col, start=True, stop=True)
            ins.then_inc(setup_pe, 1)
            pe.wait_ge(setup_dve, SETUP_DONE)

            def turn(src_ap, bank_ap, done):
                for kk in range(GK):
                    ins = nc.tensor.transpose(bank_ap[:, kk * P:kk * P + P], src_ap[:, kk * P:kk * P + P], ident[:, :])
                ins.then_inc(done, 1)

            def turn_x(phase, i, p):
                base = {0: 0, 1: 1, 2: 2, 3: 3}[phase] * 16 * GPAIRS
                pe.wait_ge(x_in[p], 16 * i + (base + 16))
                turn(nb("x", p), bank[4 * p][:, 0:GN], x_turned)

            def nodes0(i):
                for p in range(2):
                    if started(i):
                        pe.wait_ge(tab_copied, nth("012", 0, i - 1, p))
                    turn_x(0, i, p)
                    pe.wait_ge(x_copied, nth("013", 0, i, p))
                    for kk in range(GK):
                        ins = mm(bank[4 * p + 1 + kk][:, 0:2 * ZW], nb("xt", p)[:, kk * P:kk * P + P], w_sd[:, :],
                                 start=True, stop=True)
                    ins.then_inc(tab_done, 1)

            def sum_windows(gc, i, q, k, vals, dens):
                for j in range(TC):
                    tt = gc * TC + j
                    if j % SB == 0:
                        pe.wait_ge(values_weighted, gc * NSB + (j // SB + 1))
                    pe.wait_ge(s_ready, tt + 1)
                    pe.wait_ge(acc_done, tt + (ACC_CREDIT + 1 - AGG_RING))
                    slot = agg_ps(j % AGG_RING)
                    mm(slot[:, 0:P], vals(j), s_oh[:, j % S_RING, :], start=True, stop=True)
                    mm(slot[:, P:2 * P], dens(j), s_oh[:, j % S_RING, :], start=True, stop=True).then_inc(agg_done, 1)

            def softmax_turns(gc):
                pe.wait_ge(logits_ready, gc + 1)
                nc.tensor.transpose(lt_ps, lg2[:, :], ident[:, :]).then_inc(logits_turned, 1)
                pe.wait_ge(weights_t, gc + 1)
                nc.tensor.transpose(ex_ps, ext[:, :], ident[:, :]).then_inc(weights_turned, 1)

            def edges0(i):
                for q in range(2):
                    gc = 2 * i + q
                    pe.wait_ge(acc_done, gc * TC + ACC_CREDIT)

                    def turn_edges(g4):
                        gg = 16 * i + (q * 8 + g4)
                        pe.wait_ge(ef_in[(g4 // 2) % 2], 128 * i + (64 * q + 32 * (g4 // 4) + 32))
                        pe.wait_ge(eft_copied, gg + 1)
                        for m in range(4):
                            ins = nc.tensor.transpose(efb[g4 % 2][:, m * P:m * P + P], efr[:, (g4 // 2) % 2, (4 * g4 + m) % SB, :],
                                                      ident[:, :])
                        ins.then_inc(ef_turned, 1)

                    turn_edges(0)
                    for g4 in range(8):
                        if g4 + 1 < 8:
                            turn_edges(g4 + 1)
                        gg = 16 * i + (q * 8 + g4)
                        s = g4 // 2
                        pe.wait_ge(eft_copied, gg + 1 + 2)
                        pe.wait_ge(z_copied, gg + 1)
                        if g4 % 2 == 0:
                            pe.wait_ge(gather_in[q][s], 128 * i + 128)
                            pe.wait_ge(win_in[s % 2], 512 * i + (256 * q + 128 * (s // 2) + 128))
                        for m in range(4):
                            j = 4 * g4 + m
                            z = zb[:, m // 2, ZW * (m % 2):ZW * (m % 2) + ZW]
                            mm(z, eft[:, g4 % 2, m * P:m * P + P], w_ef[:, :], start=True, stop=False)
                            mm(z, ident[:, :], g(q, j, ZW), start=False, stop=False)
                            pe.wait_ge(oht_ready, 2 * TC * i + (q * TC + j) + 1 + OHT_CREDIT)
                            mm(z, oht[:, j % OHT_RING, :], win[:, s % 2, j % SB, :], start=False, stop=True).then_inc(expanded, 1)
                    softmax_turns(gc)
                    sum_windows(gc, i, q, 0, lambda j: ze[:, j, 0:D], lambda j: ex[:, j:j + 1].to_broadcast([P, P]))

            def edges_gat(k):
                def edges(i):
                    for q in range(2):
                        gc = 2 * i + (q + CH * k)
                        for j in range(TC):
                            s = j // SB
                            if j % SB == 0:
                                pe.wait_ge(win_in[s % 2], 512 * i + (256 * q + 128 * (s // 2) + 128) + 256 * CH * k)
                            pe.wait_ge(oht_ready, gc * TC + j + 1 + OHT_CREDIT)
                            mm(bank[2][:, j:j + 3 * TC + 1:TC], oht[:, j % OHT_RING, :], win[:, s % 2, j % SB, 0:H],
                               start=True, stop=True).then_inc(expanded, 1)
                        softmax_turns(gc)
                        pe.wait_ge(den_cols, gc - (CH - 1))
                        sum_windows(gc, i, q, k, lambda j: g(q, j, D), lambda j: ze[:, j, 0:D])
                return edges

            def tables(phase, i, p, bank_ap):
                pe.wait_ge(new_copied, nth("12", phase, i, p))
                if started(i):
                    pe.wait_ge(tab_copied, nth("012", phase, i - 1, p))
                for kk in range(GK):
                    ins = mm(bank_ap[:, kk * TW:kk * TW + TW], nb("newt", p)[:, kk * P:kk * P + P], w_t[:, phase - 1, :],
                             start=True, stop=True)
                ins.then_inc(tab_done, 1)

            def nodes1(i):
                for p in range(2):
                    turn_x(1, i, p)
                    pe.wait_ge(attn_squared, nth("1", 1, i, p))
                    for kk in range(GK):
                        z = bank[4 * p + 1][:, kk * ZW:kk * ZW + ZW]
                        c = slice(kk * P, kk * P + P)
                        mm(z, nb("xt", p)[:, c], w_n[:, 0, :], start=True, stop=False)
                        mm(z, nb("at", p)[:, c], w_n[:, 1, :], start=False, stop=False)
                        mm(z[:, D + 1:ZW], nb("xt2", p)[:, c], one_c, start=False, stop=False)
                        ins = mm(z[:, D + 1:ZW], nb("at2", p)[:, c], one_c, start=False, stop=True)
                    ins.then_inc(norm_done, 1)
                    pe.wait_ge(x_new, nth("123", 1, i, p))
                    turn(nb("new", p), bank[4 * p + 2][:, 0:GN], new_turned)
                    tables(1, i, p, bank[4 * p + 3])

            def nodes2(i):
                for p in range(2):
                    gn = 2 * i + p
                    nodes = bass.ds(2 * GN * i + p * GN, GN)
                    mm(bank[4 * p][:, 0:GN], sel[:, :], acc[:, 1, nodes], start=True, stop=True).then_inc(den_picked, 1)
                    pe.wait_ge(attn_ready, nth("123", 2, i, p))
                    turn(nb("at", p), bank[4 * p][:, GN:2 * GN], attn_turned)
                    pe.wait_ge(mid_ready, gn + 1)
                    turn(nb("at2", p), bank[4 * p + 1][:, 0:GN], mid_turned)
                    pe.wait_ge(mid_copied, gn + 1)
                    if started(i):
                        pe.wait_ge(tab_copied, nth("012", 2, i - 1, p))
                    for o in range(2):
                        z = bank[4 * p + 2][:, o * GN:o * GN + GN]
                        mm(z, w1[:, 0, o * P:o * P + P], nb("xt", p), start=True, stop=False)
                        ins = mm(z, w1[:, 1, o * P:o * P + P], acc[:, 1, nodes], start=False, stop=True)
                    ins.then_inc(h_done, 1)
                    pe.wait_ge(h_ready, 2 * gn + 1)
                    for o in range(2):
                        z = bank[4 * p + 3][:, o * GN:o * GN + GN]
                        for kk in range(2):
                            ins = mm(z, w2[:, kk, o * P:o * P + P], nb("h1", p, 2 * GN)[:, kk * GN:kk * GN + GN],
                                     start=(kk == 0), stop=(kk == 1))
                    ins.then_inc(h_done, 1)
                    pe.wait_ge(h_ready, 2 * gn + 2)
                    for n in range(GK):
                        z = bank[4 * p + 3][:, n * P:n * P + P]
                        for kk in range(2):
                            ins = mm(z, nb("h2", p, 2 * GN)[:, kk * GN + n * P:kk * GN + n * P + P], w3[:, kk, :],
                                     start=(kk == 0), stop=(kk == 1))
                    ins.then_inc(h3_done, 1)
                    pe.wait_ge(x_new, nth("123", 2, i, p))
                    turn(nb("new", p), bank[4 * p + 1][:, GN:2 * GN], new_turned)
                    tables(2, i, p, bank[4 * p + 2])

            def nodes3(i):
                for p in range(2):
                    turn_x(3, i, p)
                    pe.wait_ge(x_copied, nth("013", 3, i, p))
                    mm(bank[4 * p + 1][:, 0:GN], w_res[:, :], nb("xt", p), start=True, stop=True).then_inc(res_done, 1)
                    pe.wait_ge(attn_ready, nth("123", 3, i, p))
                    turn(nb("at", p), bank[4 * p + 2][:, 0:GN], attn_turned)

            group_pairs(pe, nodes0)
            pe.wait_ge(tab_copied, GROUPS)
            with pe.Fori(0, PAIRS) as i:
                edges0(i)
            pe.wait_ge(acc_done, NT + ACC_CREDIT)
            group_pairs(pe, nodes1)
            pe.wait_ge(tab_copied, 2 * GROUPS)
            with pe.Fori(0, PAIRS) as i:
                edges_gat(1)(i)
            pe.wait_ge(acc_done, 2 * NT + ACC_CREDIT)
            group_pairs(pe, nodes2)
            pe.wait_ge(tab_copied, 3 * GROUPS)
            with pe.Fori(0, PAIRS) as i:
                edges_gat(2)(i)
            pe.wait_ge(acc_done, 3 * NT + ACC_CREDIT)
            group_pairs(pe, nodes3)

        @block.vector
        def _(dve):
            v = nc.vector
            dve.sem_inc(oht_ready, OHT_CREDIT)
            dve.sem_inc(acc_done, ACC_CREDIT)

            count = [0]

            def did(ins):
                count[0] += 1
                ins.then_inc(setup_dve, 1)
                return count[0]

            def then(ins):
                dve.wait_ge(setup_dve, did(ins))

            dve.wait_ge(edges_in, 16 * 15)
            assert did(v.tensor_copy(dtf, dti)) == DTF_READY
            assert did(v.tensor_copy(stf, sti)) == STF_READY
            dve.wait_ge(setup_pe, 2)
            for n in range(2):
                lo, hi = 512 * n, min(512 * n + 512, NT)
                did(v.tensor_copy(dcol[:, lo:hi], bank[n][:, 0:hi - lo]))
                did(v.tensor_copy(src_i[:, lo:hi], zb[:, n, 0:hi - lo]))
            dve.wait_ge(setup_dve, count[0])
            assert did(v.tensor_copy(first_i[:, :], dcol[0:1, :])) == DCOL_READY
            dve.wait_ge(edges_in, 16 * 18)
            assert did(v.tensor_copy(stf, sti)) == NEXT_READY
            dve.wait_ge(consts, 8)
            did(v.tensor_copy(iota_row[:, :], iota_i))
            did(v.tensor_copy(iota_c, col_i[:, 0:1]))
            then(v.tensor_scalar(col_i[:, 1:2], col_i[:, 0:1], F // 2, None, ALU.bitwise_and))
            then(v.tensor_copy(attr_mask, col_i[:, 1:2]))
            then(v.tensor_scalar(attr_mask, attr_mask, 2.0 / F, None, ALU.mult))
            then(v.tensor_scalar(den_mask, attr_mask, -1.0, 1.0, ALU.mult, ALU.add))
            did(v.memset(one_c, 1.0))
            dve.wait_ge(weights_in, 16 * N_WEIGHTS)
            assert did(v.memset(eps, EPS)) == BN_VAR
            then(v.tensor_reduce(rsum[:, 0:1], we_raw, AX.X, ALU.add))
            then(v.tensor_reduce(rsum[:, 1:2], wn_raw, AX.X, ALU.add))
            then(v.tensor_scalar(rsum[:, 2:3], rsum[:, 0:1], -1.0 / (3 * D), None, ALU.mult))
            then(v.tensor_scalar(rsum[:, 3:4], rsum[:, 1:2], -1.0 / (2 * D), None, ALU.mult))
            did(v.tensor_scalar(we_raw, we_raw, rsum[:, 2:3], None, ALU.add))
            assert did(v.tensor_scalar(wn_raw, wn_raw, rsum[:, 3:4], None, ALU.add)) == CENTRED
            dve.wait_ge(setup_pe, 3)
            for k, into in enumerate((first_b, last_b)):
                for n in range(2):
                    lo, hi = 512 * n, min(512 * n + 512, NT)
                    did(v.tensor_copy(into[:, lo:hi], bank[4 + 2 * k + n][:, 0:hi - lo]))
            dve.wait_ge(setup_dve, count[0])
            did(v.tensor_tensor(rel[:, :], dcol, first_b, ALU.subtract))
            dve.wait_ge(setup_pe, 4)
            for n in range(2):
                lo, hi = 512 * n, min(512 * n + 512, NT)
                then(v.tensor_tensor(tile_tmp[:, lo:hi], dcol[:, lo:hi], zb[:, n, 0:hi - lo], ALU.not_equal))
            then(v.tensor_scalar(times[:, :], tile_tmp[:, 0:NT], 1.0, None, ALU.add))
            did(v.tensor_scalar(nodew[:, :], first_b, iota_c, None, ALU.add))
            then(v.tensor_tensor(pen_single, first_b, last_b, ALU.not_equal))
            then(v.tensor_tensor(pen_join_f[:, 1:NT], first_b[:, 1:NT], last_b[:, 0:NT - 1], ALU.not_equal))
            did(v.memset(pen_join_f[:, 0:1], 1.0))
            then(v.memset(pen_join_f[:, NT:NT + 1], 1.0))
            did(v.tensor_scalar(pen_join[:, :], pen_join_f, BIG, None, ALU.mult))
            did(v.memset(carry_f[:, 0:1], BIG))
            then(v.tensor_tensor(tile_tmp[:, 0:NT], pen_join_f[:, 1:NT + 1], pen_single, ALU.max))
            did(v.tensor_scalar(carry_f[:, 1:NT + 1], tile_tmp[:, 0:NT], BIG, None, ALU.mult))
            then(v.memset(fac[:, :], 1.0))
            then(v.tensor_tensor(tile_tmp[:, 0:NT], pen_join_f[:, 0:NT], pen_single, ALU.max))
            did(v.tensor_scalar(carry_r[:, :, 0:TC - 1],
                                tile_tmp[:, 0:NT].rearrange("p (c j) -> p c j", j=TC)[:, :, 1:TC][:, :, ::-1],
                                BIG, None, ALU.mult))
            did(v.memset(pen_f[:, :, 0:1], 0.0))
            did(v.memset(pen_r[:, :, 0:1], 0.0))
            half = CH // 2
            for n in range(2):
                cs = slice(n * half, n * half + half)
                d3 = dtf[:, cs, :]
                df = diff.rearrange("p (c e) -> p c e", e=P)
                dve.wait_ge(setup_dve, count[0])
                then(v.tensor_tensor(df[:, :, 1:P], d3[:, :, 1:P], d3[:, :, 0:P - 1], ALU.not_equal))
                did(v.tensor_scalar(pen_f[:, cs, 1:P], df[:, :, 1:P], BIG, None, ALU.mult))
                then(v.tensor_scalar(pen_r[:, cs, 1:P], df[:, :, 1:P][:, :, ::-1], BIG, None, ALU.mult))
                then(v.tensor_tensor(df, d3, d3[:, :, 0:1].to_broadcast([P, half, P]), ALU.not_equal))
                then(v.tensor_scalar(pen_first[:, cs, :], df, BIG, None, ALU.mult))
                then(v.tensor_tensor(df, d3, d3[:, :, P - 1:P].to_broadcast([P, half, P]), ALU.not_equal))
                then(v.tensor_scalar(pen_last[:, cs, :], df, BIG, None, ALU.mult))
            dve.wait_ge(setup_pe, 5)
            did(v.tensor_copy(w_sd[:, 0:D], bank[0][:, 0:D]))
            did(v.tensor_copy(w_ef[:, 0:D], bank[0][:, D:2 * D]))
            did(v.tensor_copy(w_sd[:, ZW:ZW + D], bank[0][:, 2 * D:3 * D]))
            for k in range(2):
                did(v.tensor_copy(w_n[:, k, 0:D], bank[1][:, k * D:k * D + D]))
                did(v.memset(w_n[:, k, D:D + 1], 1.0))
                did(v.memset(w_n[:, k, D + 1:ZW], 0.0))
                did(v.memset(w_sd[:, k * ZW + D:k * ZW + D + 1], 1.0))
                did(v.memset(w_sd[:, k * ZW + D + 1:k * ZW + ZW], 0.0))
            did(v.memset(w_ef[:, D:D + 1], 1.0))
            did(v.memset(w_ef[:, D + 1:ZW], 0.0))
            did(v.memset(b_t[:, 1, :], 0.0))
            for layer in range(2):
                for w in range(2):
                    a = a_raw[:, 2 * layer + w, :]
                    at = slice(D + H * w, D + H * w + H)
                    then(v.tensor_tensor(prod[:, w, :], w_t[:, layer, 0:D], a, ALU.mult))
                    then(v.tensor_reduce(w_t[:, layer, at], prod[:, w, :].rearrange("p (h f) -> p h f", h=H), AX.X, ALU.add))
                    if layer == 0:
                        then(v.tensor_tensor(prod[:, w, :], b_t[:, layer, 0:D], a, ALU.mult))
                        then(v.tensor_reduce(b_t[:, layer, at], prod[:, w, :].rearrange("p (h f) -> p h f", h=H), AX.X, ALU.add))
            then(v.tensor_tensor(b_t[:, 0, D + H:TW], b_t[:, 0, D + H:TW], ab_raw, ALU.add))
            dve.wait_ge(bn_std, 1)
            then(v.reciprocal(vec[:, 12:13], vec[:, 11:12]))
            then(v.tensor_tensor(bn_scale, vec[:, 12:13], bn_raw[:, 3:4], ALU.mult))
            then(v.tensor_tensor(vec[:, 13:14], bn_raw[:, 0:1], bn_raw[:, 1:2], ALU.subtract))
            then(v.tensor_tensor(vec[:, 14:15], vec[:, 13:14], bn_scale, ALU.mult))
            did(v.tensor_tensor(bn_shift, vec[:, 14:15], bn_raw[:, 4:5], ALU.add))
            dve.wait_ge(setup_pe, 5)
            did(v.tensor_tensor(b1_c, b1_c, bank[1][:, 2 * P:2 * P + 2], ALU.add))
            did(v.memset(blk[:, :, :], BIG))
            assert did(v.memset(cin[:, :, :], BIG)) == SETUP_DONE, count[0]
            dve.wait_ge(setup_dve, SETUP_DONE)

            steps = {"base": 0, "n": 0, "total": 0}

            def step(ins):
                steps["n"] += 1
                ins.then_inc(chain, 1)

            def ordered(ins=None):
                if ins is not None:
                    step(ins)
                dve.wait_ge(chain, steps["base"] + steps["n"])

            def stepped_loop(name, body, n, peel):
                per = STEPS[name]
                start = steps["total"]
                if peel:
                    steps.update(base=start, n=0)
                    body(0)
                    assert steps["n"] == per, (name, steps["n"])
                with dve.Fori(int(peel), n) as i:
                    steps.update(base=start + per * i, n=0)
                    body(i)
                    assert steps["n"] == per, (name, steps["n"])
                steps["total"] = start + per * n

            def nodes0(i):
                for p in range(2):
                    dve.wait_ge(tab_done, nth("012", 0, i, p))
                    dve.wait_ge(x_squared, nth("01", 0, i, p))
                    if started(i):
                        dve.wait_ge(tab_out[p], 32 * i)
                    tab = nb("tab", p, GK * 2 * ZW).rearrange("p (k s w) -> p k s w", k=GK, s=2)
                    for kk in range(GK):
                        v.tensor_copy(tab[:, kk, :, 0:D + 1],
                                      bank[4 * p + 1 + kk][:, 0:2 * ZW].rearrange("p (s w) -> p s w", s=2)[:, :, 0:D + 1])
                    v.tensor_copy(tab[:, :, :, D + 1],
                                  nb("small", p, 2).unsqueeze(2).to_broadcast([P, GK, 2])).then_inc(tab_copied, 1)

            def softmax(gc, i, q, k):
                c = bass.ds(2 * i + q, 1)
                t0 = 2 * TC * i + q * TC
                pf = pen_f[:, c, 0:P].rearrange("p a e -> p (a e)")
                pr = pen_r[:, c, :].rearrange("p a e -> p (a e)")
                p_first = pen_first[:, c, :].rearrange("p a e -> p (a e)")
                p_last = pen_last[:, c, :].rearrange("p a e -> p (a e)")
                cq, cp = cin[:, q, :], cin[:, 1 - q, :]
                dve.wait_ge(logits_turned, gc + 1)
                step(v.tensor_copy(cq[:, 0:1], cp[:, 32:33]))
                ordered(v.tensor_tensor_scan(mx[:, :], pf, lt_ps, BIG, ALU.add, ALU.max))
                ordered(v.transpose(blk[:, 0, :], mx[:, P - 32:P]))
                ordered(v.tensor_tensor(blk[:, 1, :], blk[:, 0, :], pen_join[:, bass.ds(t0 + 1, TC)], ALU.add))
                ordered(v.tensor_tensor_scan(cq[:, 1:33], carry_f[:, bass.ds(t0 + 1, TC)], blk[:, 1, :], cq[:, 0:1],
                                             ALU.add, ALU.max))
                ordered(v.transpose(blk[:, 2, :], cq[:, 0:32]))
                ordered(v.scalar_tensor_tensor(mx2[:, :], p_first, blk[:, 2, 31:32], mx[:, :], ALU.add, ALU.max))
                ordered(v.tensor_tensor_scan(mx[:, ::-1], pr, mx2[:, ::-1], BIG, ALU.add, ALU.max))
                ordered(v.transpose(blk[:, 3, :], mx[:, 0:32]))
                ordered(v.tensor_tensor(blk[:, 4, 0:TC - 1], blk[:, 3, 1:TC], pen_join[:, bass.ds(t0 + 1, TC - 1)], ALU.add))
                ordered(v.tensor_tensor_scan(blk[:, 5, 0:TC - 1][:, ::-1], carry_r[:, c, 0:TC - 1].rearrange("p a j -> p (a j)"),
                                             blk[:, 4, 0:TC - 1][:, ::-1], BIG, ALU.add, ALU.max))
                ordered(v.transpose(blk[:, 6, :], blk[:, 5, :]))
                ordered(v.scalar_tensor_tensor(mx2[:, :], p_last, blk[:, 6, 0:1], mx[:, :], ALU.add, ALU.max))
                v.tensor_tensor(lg[:, :], lt_ps, mx2[:, :], ALU.subtract).then_inc(shifted, 1)
                ordered(v.tensor_tensor(blk[:, 7, :], blk[:, 2, 31:32].to_broadcast([P, 32]),
                                        mx2[:, 0:1].to_broadcast([P, 32]), ALU.subtract))
                v.transpose(blk[:, 0, :], blk[:, 7, :]).then_inc(fac_arg, 1)

            def window_onehot(gc, i, q, j):
                dve.wait_ge(agg_done, gc * TC + j + 1)
                v.tensor_scalar(s_oh[:, j % S_RING, :], iota_row[:, :], rel[:, bass.ds(2 * TC * i + (q * TC + j), 1)], None,
                                ALU.is_equal).then_inc(s_ready, 1)

            def edge_onehots(gc, i, q, k):
                for j in range(TC):
                    s = j // SB
                    if j % SB == 0:
                        dve.wait_ge(row_in[s % 2], gc * 32 + (s // 2 + 1) * 16)
                    dve.wait_ge(expanded, gc * TC + (j - OHT_RING + 1 + EXP_CREDIT))
                    v.tensor_scalar(oht[:, j % OHT_RING, :], dst_row[:, s % 2, (j % SB) * P:(j % SB) * P + P],
                                    nodew[:, bass.ds(2 * TC * i + (q * TC + j), 1)], None, ALU.is_equal).then_inc(oht_ready, 1)

            def rescale_and_sum(gc, i, q, k, regs):
                dve.load(regs, first_i[0:1, bass.ds(2 * TC * i + q * TC, SB)])
                dve.wait_ge(fac_ready, gc + 1)
                first = dve.snap(regs[0], min_val=0, max_val=N)
                dve.wait_ge(acc_done, gc * TC + ACC_CREDIT)
                if k == 1:
                    ordered(v.scalar_tensor_tensor(fac[:, 1:2], fac[:, 0:1], den_mask, attr_mask, ALU.mult, ALU.add))
                    for half, f in ((0, fac[:, 0:1]), (1, fac[:, 1:2])):
                        col = acc[:, half, bass.ds(first, 1)]
                        step(v.tensor_scalar(col, col, f, None, ALU.mult))
                    ordered()
                else:
                    col = acc[:, 0:2, bass.ds(first, 1)]
                    ordered(v.tensor_scalar(col, col, fac[:, 0:1], None, ALU.mult))
                for j in range(TC):
                    if j and j % SB == 0:
                        dve.load(regs, first_i[0:1, bass.ds(2 * TC * i + (q * TC + j), SB)])
                    if j < TC - S_RING:
                        window_onehot(gc, i, q, j + S_RING)
                    first = dve.snap(regs[j % SB], min_val=0, max_val=N)
                    win_acc = acc[:, 0:2, bass.ds(first, P)]
                    dve.wait_ge(agg_done, gc * TC + j + 1 + AGG_CREDIT)
                    if j:
                        dve.wait_ge(acc_done, gc * TC + j + ACC_CREDIT)
                    v.tensor_tensor(win_acc, win_acc, agg_ps(j % AGG_RING).rearrange("p (a n) -> p a n", a=2),
                                    ALU.add).then_inc(acc_done, 1)

            def copy_weights(gc, i, q, k):
                dve.wait_ge(weights_turned, gc + 1)
                if k == 0:
                    v.tensor_copy(ex[:, :], ex_ps).then_inc(ex_ready, 1)
                else:
                    v.tensor_tensor(ex[:, :].rearrange("p (h j) -> p h j", h=H), ex_ps.rearrange("p (h j) -> p h j", h=H),
                                    times[:, bass.ds(2 * TC * i + q * TC, TC)].unsqueeze(1).to_broadcast([P, H, TC]),
                                    ALU.mult).then_inc(ex_ready, 1)

            def edges0(i):
                for q in range(2):
                    gc = 2 * i + q
                    edge_onehots(gc, i, q, 0)
                    for j in range(S_RING):
                        window_onehot(gc, i, q, j)
                    dve.wait_ge(z_copied, 8 * gc + 8 + 1)
                    dve.wait_ge(squared, gc * TC + (TC + SQ_CREDIT))
                    step(v.tensor_scalar(att[:, 1, :], ze[:, :, D], 1.0 / (3 * D), None, ALU.mult))
                    ordered(v.tensor_tensor(att[:, 4, :], ze[:, :, D + 1], att[:, 0, :], ALU.add))
                    ordered(v.tensor_tensor(att[:, 5, :], att[:, 1, :], att[:, 1, :], ALU.mult))
                    ordered(v.scalar_tensor_tensor(att[:, 6, :], att[:, 4, :], 1.0 / (3 * D), att[:, 5, :], ALU.mult, ALU.subtract))
                    v.tensor_scalar(att[:, 2, :], att[:, 6, :], 0.0, None, ALU.max).then_inc(var_ready, 1)
                    dve.wait_ge(std_ready, gc + 1)
                    ordered(v.reciprocal(att[:, 4, :], att[:, 3, :]))
                    for s in range(NSB):
                        for j in range(s * SB, s * SB + SB):
                            v_ins = v.scalar_tensor_tensor(ze[:, j, 0:D], ze[:, j, 0:D], att[:, 4, j:j + 1], be, ALU.mult, ALU.add)
                        ordered(v_ins)
                        zz = ze[:, s * SB:s * SB + SB, 0:D]
                        ordered(v.scalar_tensor_tensor(zz, zz, 0.01, zz, ALU.mult, ALU.max))
                        for j in range(s * SB, s * SB + SB):
                            v_ins = v.tensor_tensor_reduce(out=oht[:, j % OHT_RING, :], in0=ze[:, j, 0:D], in1=ae, scale=1.0,
                                                           scalar=0.0, op0=ALU.mult, op1=ALU.add, accum_out=att[:, 7, j:j + 1])
                        ordered(v_ins)
                    v.tensor_copy(lg2[:, :].rearrange("p (h j) -> p h j", h=H),
                                  att[:, 7, :].unsqueeze(1).to_broadcast([P, H, TC])).then_inc(logits_ready, 1)
                    softmax(gc, i, q, 0)
                    copy_weights(gc, i, q, 0)
                    rescale_and_sum(gc, i, q, 0, regs0)

            def edges_gat(k, regs):
                def edges(i):
                    for q in range(2):
                        gc = 2 * i + (q + CH * k)
                        edge_onehots(gc, i, q, k)
                        for j in range(S_RING):
                            window_onehot(gc, i, q, j)
                        dve.wait_ge(expanded, gc * TC + TC + EXP_CREDIT)
                        for s in range(NSB):
                            dve.wait_ge(gather_in[q][s], 128 * i + (128 + 128 * PAIRS * k))
                        ordered(v.tensor_tensor(lg[:, :].rearrange("p (h j) -> p h j", h=H),
                                                bank[2][:, 0:P].rearrange("p (h j) -> p h j", h=H),
                                                gq(q)[:, :, D:KW].rearrange("p j h -> p h j"), ALU.add))
                        v.scalar_tensor_tensor(lg2[:, :], lg[:, :], 0.2, lg[:, :], ALU.mult, ALU.max).then_inc(logits_ready, 1)
                        softmax(gc, i, q, k)
                        copy_weights(gc, i, q, k)
                        dve.wait_ge(ex_ready, gc + 1)
                        for s in range(NSB):
                            vals = gq(q)[:, s * SB:s * SB + SB, 0:D].rearrange("p j (h x) -> p j h x", h=H)
                            w = ex[:, :].rearrange("p (h j) -> p j h", h=H)[:, s * SB:s * SB + SB, :]
                            v.tensor_tensor(vals, vals, w.unsqueeze(3).to_broadcast([P, SB, H, F]),
                                            ALU.mult).then_inc(values_weighted, 1)
                        rescale_and_sum(gc, i, q, k, regs)
                return edges

            def small(p):
                return nb("small", p, 40)

            def layer_norm(p, y, into, var_count, done, before_write):
                sm = small(p)
                st = sm[:, 12:24].rearrange("p (k s) -> p k s", k=GK)
                mv = sm[:, 24:28].rearrange("p (k s) -> p k s", k=GK)
                for kk in range(GK):
                    ins = v.bn_stats(st[:, kk, :], y[:, kk * P:kk * P + P])
                ordered(ins)
                dve.sem_inc(host, 1)
                for kk in range(GK):
                    ins = v.bn_aggr(mv[:, kk, :], st[:, kk, :])
                ins.then_inc(ln_var, 1)
                dve.wait_ge(ln_std, var_count)
                ordered(v.reciprocal(sm[:, 30:32], sm[:, 28:30]))
                before_write()
                for kk in range(GK):
                    ins = v.tensor_scalar(into[:, kk * P:kk * P + P], y[:, kk * P:kk * P + P], mv[:, kk, 0:1],
                                          sm[:, 30 + kk:31 + kk], ALU.subtract, ALU.mult)
                ins.then_inc(done, 1)

            def stored(phase, i, p):
                def wait():
                    if not started(i):
                        return
                    if phase == 3:
                        dve.wait_ge(rows_out[p], 16 * i)
                    else:
                        dve.wait_ge(tab_out[p], 48 * i + 32 * GPAIRS + 48 * GPAIRS * (phase - 1))
                return wait

            def copy_tables(phase, i, p, bank_ap):
                dve.wait_ge(tab_done, nth("012", phase, i, p))
                v.tensor_tensor(nb("tab", p, GK * TW).rearrange("p (k w) -> p k w", k=GK),
                                bank_ap[:, 0:GK * TW].rearrange("p (k w) -> p k w", k=GK),
                                b_t[:, phase - 1, :].unsqueeze(1).to_broadcast([P, GK, TW]), ALU.add).then_inc(tab_copied, 1)

            def bc(row):
                return row.unsqueeze(1).to_broadcast([P, GK, D])

            def nodes1(i):
                for p in range(2):
                    nodes = bass.ds(2 * GN * i + p * GN, GN)
                    if started(i):
                        dve.wait_ge(norm_done, nth("1", 1, i - 1, p))
                    ordered(v.tensor_scalar(nb("tmp", p), acc[:, 1, nodes], TINY, None, ALU.max))
                    ordered(v.reciprocal(nb("tmp", p), nb("tmp", p)))
                    v.tensor_tensor(nb("at", p), acc[:, 0, nodes], nb("tmp", p), ALU.mult).then_inc(attn_ready, 1)
                    dve.wait_ge(norm_done, nth("1", 1, i, p))
                    z = bank[4 * p + 1][:, 0:GK * ZW].rearrange("p (k w) -> p k w", k=GK)
                    sm = small(p)
                    ordered(v.tensor_scalar(sm[:, 0:2], z[:, :, D], 1.0 / (2 * D), None, ALU.mult))
                    ordered(v.tensor_tensor(sm[:, 2:4], sm[:, 0:2], sm[:, 0:2], ALU.mult))
                    ordered(v.scalar_tensor_tensor(sm[:, 8:10], z[:, :, D + 1], 1.0 / (2 * D), sm[:, 2:4], ALU.mult, ALU.subtract))
                    v.tensor_scalar(sm[:, 4:6], sm[:, 8:10], 0.0, None, ALU.max).then_inc(norm_var, 1)
                    dve.wait_ge(norm_std, nth("1", 1, i, p))
                    ordered(v.reciprocal(sm[:, 10:12], sm[:, 6:8]))
                    h = nb("h", p)
                    ordered(v.tensor_tensor(tiles(h), z[:, :, 0:D], sm[:, 10:12].unsqueeze(2).to_broadcast([P, GK, D]), ALU.mult))
                    ordered(v.tensor_tensor(tiles(h), tiles(h), bc(bn_row), ALU.add))
                    ordered(v.scalar_tensor_tensor(h, h, 0.01, h, ALU.mult, ALU.max))
                    ordered(v.tensor_tensor(h, h, nb("x", p), ALU.add))
                    layer_norm(p, h, nb("new", p), nth("1", 1, i, p), x_new, stored(1, i, p))
                    copy_tables(1, i, p, bank[4 * p + 3])

            def nodes2(i):
                for p in range(2):
                    gn = 2 * i + p
                    nodes = bass.ds(2 * GN * i + p * GN, GN)
                    dve.wait_ge(den_picked, gn + 1)
                    ordered(v.tensor_scalar(nb("tmp", p), bank[4 * p][:, 0:GN], TINY, None, ALU.max))
                    ordered(v.reciprocal(nb("tmp", p), nb("tmp", p)))
                    if started(i):
                        dve.wait_ge(attn_turned, nth("23", 2, i - 1, p))
                    v.tensor_tensor(nb("at", p), acc[:, 0, nodes], nb("tmp", p), ALU.mult).then_inc(attn_ready, 1)
                    dve.wait_ge(attn_turned, nth("23", 2, i, p))
                    dve.wait_ge(x_in[p], 16 * i + 16 + 2 * 16 * GPAIRS)
                    h = nb("h", p)
                    ordered(v.tensor_tensor(h, bank[4 * p][:, GN:2 * GN], nb("x", p), ALU.add))
                    layer_norm(p, h, nb("at2", p), GROUPS + 2 * gn + 1, mid_ready, lambda: None)
                    for layer, buf in enumerate(("h1", "h2")):
                        dve.wait_ge(h_biased, 2 * gn + 1 + layer)
                        b = nb(buf, p, 2 * GN)
                        v.scalar_tensor_tensor(b, b, 0.01, b, ALU.mult, ALU.max).then_inc(h_ready, 1)
                    dve.wait_ge(h3_done, gn + 1)
                    ordered(v.tensor_tensor(tiles(h), tiles(bank[4 * p + 3][:, 0:GN]), bc(b3_row), ALU.add))
                    ordered(v.tensor_tensor(h, h, nb("at2", p), ALU.add))
                    layer_norm(p, h, nb("new", p), GROUPS + 2 * gn + 2, x_new, stored(2, i, p))
                    copy_tables(2, i, p, bank[4 * p + 2])

            def nodes3(i):
                for p in range(2):
                    nodes = bass.ds(2 * GN * i + p * GN, GN)
                    a, tmp = nb("at", p), nb("tmp", p)
                    ordered(v.tensor_scalar(nb("xt2", p), acc[:, 1, nodes], TINY, None, ALU.max))
                    ordered(v.reciprocal(nb("xt2", p), nb("xt2", p)))
                    if started(i):
                        dve.wait_ge(attn_turned, nth("23", 3, i - 1, p))
                    ordered(v.tensor_tensor(a, acc[:, 0, nodes], nb("xt2", p), ALU.mult))
                    dve.wait_ge(res_done, nth("3", 3, i, p))
                    ordered(v.tensor_tensor(a, a, bank[4 * p + 1][:, 0:GN], ALU.add))
                    ordered(v.tensor_scalar(a, a, bn_scale, bn_shift, ALU.mult, ALU.add))
                    v.tensor_scalar(tmp, a, 0.0, None, ALU.min).then_inc(elu_arg, 1)
                    dve.wait_ge(elu_exp, nth("3", 3, i, p))
                    ordered(v.scalar_tensor_tensor(a, a, 0.0, nb("at2", p), ALU.max, ALU.add))
                    v.tensor_scalar(a, a, -1.0, None, ALU.add).then_inc(attn_ready, 1)
                    dve.wait_ge(attn_turned, nth("23", 3, i, p))
                    h = nb("h", p)
                    ordered(v.tensor_tensor(h, bank[4 * p + 2][:, 0:GN], nb("x", p), ALU.add))
                    layer_norm(p, h, nb("new", p), 3 * GROUPS + 2 * i + p + 1, x_new, stored(3, i, p))

            regs0 = [dve.alloc_register(f"first_{m}") for m in range(SB)]

            def restart_carry(n):
                dve.wait_ge(zeroed, n)
                steps["base"], steps["n"] = steps["total"], 0
                ordered(v.memset(cin[:, 1, :], BIG))
                steps["total"] += 1

            stepped_loop("nodes0", nodes0, GPAIRS, True)
            restart_carry(1)
            stepped_loop("edges0", edges0, PAIRS, False)
            dve.wait_ge(acc_done, NT + ACC_CREDIT)
            stepped_loop("nodes1", nodes1, GPAIRS, True)
            restart_carry(2)
            stepped_loop("edges1", edges_gat(1, regs0), PAIRS, False)
            dve.wait_ge(acc_done, 2 * NT + ACC_CREDIT)
            stepped_loop("nodes2", nodes2, GPAIRS, True)
            restart_carry(3)
            stepped_loop("edges2", edges_gat(2, regs0), PAIRS, False)
            dve.wait_ge(acc_done, 3 * NT + ACC_CREDIT)
            stepped_loop("nodes3", nodes3, GPAIRS, True)


_INS = ['x', 'src', 'dst', 'edge_attr_128', 'edge_attr_64', 'L0_gnn_W_e', 'L0_gnn_b_e', 'L0_gnn_a_e', 'L0_gnn_W_n',
        'L0_gnn_b_n', 'L1_gnn_W_w', 'L1_gnn_W_b', 'L1_gnn_a_w', 'L1_gnn_a_b', 'L2_gnn_u', 'L2_gnn_w1', 'L2_gnn_b1',
        'L2_gnn_w2', 'L2_gnn_b2', 'L2_gnn_w3', 'L2_gnn_b3', 'L3_gnn_W', 'L3_gnn_att_src', 'L3_gnn_att_dst',
        'L3_gnn_bias', 'L3_gnn_W_res', 'L3_gnn_bn_gamma', 'L3_gnn_bn_beta', 'L3_gnn_bn_mean', 'L3_gnn_bn_var']
_OUT = ((N, D), 'float32')


def kernel(**inputs):
    import numpy as _np
    import concourse.bacc as _bacc
    from concourse import mybir as _mybir
    from concourse.bass_utils import run_bass_kernel_spmd as _run

    nc = _bacc.Bacc("TRN2", target_bir_lowering=False, num_devices=1)
    arrays, args = {}, {}
    for name in _INS:
        a = _np.ascontiguousarray(inputs[name])
        arrays[f"in_{name}_dram"] = a
        args[name] = nc.dram_tensor(f"in_{name}_dram", a.shape, _mybir.dt.from_np(a.dtype), kind="ExternalInput").ap()
    shape, dtype = _OUT
    out = nc.dram_tensor("out_0_dram", shape, _mybir.dt.from_np(_np.dtype(dtype)), kind="ExternalOutput").ap()
    graph_kernel(nc, args, out)
    r = _run(nc, [arrays], core_ids=[0])
    return r.results[0]["out_0_dram"]
```

```python
import concourse.bass as bass
from concourse import mybir
from contextlib import ExitStack

P = 128
N = 6250
E = 106250
D = 128
H = 4
F = D // H
DU = 64
TC = 32
CH = -(-E // (P * TC))
NT = CH * TC
EP = NT * P
PAIRS = CH // 2
SB = 8
NSB = TC // SB
GN = 256
GK = GN // P
NP_ = 26 * GN
GROUPS = NP_ // GN
GPAIRS = GROUPS // 2
ZW = D + 2
KW = D + H
TW = D + 2 * H
OHT_RING, S_RING, AGG_RING = 8, 16, 4
BIG = -1.0e30
EPS = 1e-5
TINY = 1e-30
LAST_FULL = (E - (CH - 1) * TC * P) // P
LAST_REST = E - (E // P) * P

EXP_CREDIT, OHT_CREDIT, SQ_CREDIT, ACC_CREDIT, AGG_CREDIT = 2 * SB, 2 * SB, 2 * SB, 2 * TC, S_RING

DTF_READY, STF_READY, DCOL_READY, NEXT_READY, BN_VAR, CENTRED, SETUP_DONE = 1, 2, 7, 8, 16, 22, 95
N_WEIGHTS = 33

NODE_BUFFERS = {"x": 0, "xt": 256, "xt2": 512, "at": 768, "at2": 1024, "tmp": 1280, "h": 1536, "new": 1792,
                "newt": 2048, "tab": 2304, "h1": 2824, "h2": 3336, "small": 3848}

STEPS = {"edges0": 64, "edges1": 36, "edges2": 32, "nodes0": 0, "nodes1": 24, "nodes2": 18, "nodes3": 18}


def graph_kernel(nc, t, out):
    nc.disable_value_cache = True
    f32, i32, bf16 = mybir.dt.float32, mybir.dt.int32, mybir.dt.bfloat16
    ALU, ACT, AX = mybir.AluOpType, mybir.ActivationFunctionType, mybir.AxisListType
    ctx = ExitStack()
    with ctx:
        def sb(name, shape, dt=f32):
            return ctx.enter_context(nc.sbuf_tensor(name, shape, dt))

        def sem(name):
            return ctx.enter_context(nc.semaphore(name))

        def dram(name, shape, dt=f32):
            return nc.dram_tensor(name, shape, dt, kind="Internal").ap()

        dst_pad = dram("dst_pad", [EP], i32)
        x_pad = dram("x_pad", [NP_, D])
        x1_pad = dram("x1_pad", [NP_, D])
        x3_pad = dram("x3_pad", [NP_, D])
        src_tab = [dram("src_tab0", [NP_, ZW]), dram("src_tab1", [NP_, KW]), dram("src_tab3", [NP_, KW])]
        dst_tab = [dram("dst_tab0", [NP_, ZW]), dram("dst_tab1", [NP_, H]), dram("dst_tab3", [NP_, H])]

        acc = sb("acc", [P, 2, NP_])
        pen_f = sb("pen_f", [P, CH, P], bf16)
        pen_r = sb("pen_r", [P, CH, P], bf16)
        pen_first = sb("pen_first", [P, CH, P], bf16)
        pen_last = sb("pen_last", [P, CH, P], bf16)
        pen_join = sb("pen_join", [P, NT + 1], bf16)
        carry_f = sb("carry_f", [P, NT + 1], bf16)
        carry_r = sb("carry_r", [P, CH, TC], bf16)
        rel = sb("rel", [P, NT])
        nodew = sb("nodew", [P, NT])
        times = sb("times", [P, NT], bf16)
        src_i = sb("src_i", [P, NT], mybir.dt.uint16)
        first_i = sb("first_i", [1, NT], i32)
        idx = sb("idx", [P, 2, TC], i32)
        gall = sb("gall", [P, 2 * TC * KW])
        ze = sb("ze", [P, TC, ZW])
        s_oh = sb("s_oh", [P, S_RING, P])
        efr = sb("efr", [P, 2, SB, D])
        dst_row = sb("dst_row", [P, 2, SB * P], i32)
        oht = sb("oht", [P, OHT_RING, P])
        eft = sb("eft", [P, 2, 4 * P])
        win = sb("win", [P, 2, SB, ZW])
        lg = sb("lg", [P, P])
        lg2 = sb("lg2", [P, P])
        mx = sb("mx", [P, P])
        mx2 = sb("mx2", [P, P])
        ext = sb("ext", [P, P])
        ex = sb("ex", [P, P])
        blk = sb("blk", [P, 8, 32])
        cin = sb("cin", [P, 2, 33])
        att = sb("att", [P, 8, TC])
        fac = sb("fac", [P, 2])
        junk = sb("junk", [P, 2, P])
        ident = sb("ident", [P, P])
        sel = sb("sel", [P, P])
        iota_row = sb("iota_row", [P, P])
        col_i = sb("col_i", [P, 2], i32)
        cols = sb("cols", [P, 8])
        w_sd = sb("w_sd", [P, 2 * ZW])
        w_ef = sb("w_ef", [P, ZW])
        w_n = sb("w_n", [P, 2, ZW])
        w_t = sb("w_t", [P, 2, TW])
        b_t = sb("b_t", [P, 2, TW])
        w1 = sb("w1", [P, 2, 256])
        w1u = sb("w1u", [DU, 256])
        w2 = sb("w2", [P, 2, 256])
        w3 = sb("w3", [P, 2, D])
        w_res = sb("w_res", [P, D])
        rows = sb("rows", [P, 4, D])
        vec = sb("vec", [P, 16])
        be, ae, bn_row, b3_row = (rows[:, k, :] for k in range(4))
        eps, den_mask, attr_mask, one_c, iota_c = (cols[:, k:k + 1] for k in range(5))
        b1_c, b2_c, bn_scale, bn_shift = vec[:, 0:2], vec[:, 2:4], vec[:, 4:5], vec[:, 5:6]
        bn_raw = vec[:, 6:11]

        def g(q, j, width=KW):
            return gall[:, (q * TC + j) * KW:(q * TC + j) * KW + width]

        def gq(q):
            return gall[:, q * TC * KW:(q + 1) * TC * KW].rearrange("p (j d) -> p j d", d=KW)

        def nb(name, p, width=GN):
            at = p * TC * KW + NODE_BUFFERS[name]
            return gall[:, at:at + width]

        bank = [ctx.enter_context(nc.psum_tensor(f"bank{k}", [P, 512], f32)) for k in range(2)]
        zb = ctx.enter_context(nc.psum_tensor("zb", [P, 2, 512], f32))
        bank += [zb[:, 0, :], zb[:, 1, :]]
        bank += [ctx.enter_context(nc.psum_tensor(f"bank{k}", [P, 512], f32)) for k in range(4, 8)]

        def agg_ps(slot):
            return bank[(0, 1, 4, 5)[slot]][:, 0:2 * P]

        efb = bank[4:6]
        lt_ps, ex_ps = bank[6][:, 0:P], bank[7][:, 0:P]

        weights_in = sem("weights_in")
        edges_in = sem("edges_in")
        consts = sem("consts")
        padded = sem("padded")
        w1_zero = sem("w1_zero")
        bn_std = sem("bn_std")
        setup_dve = sem("setup_dve")
        setup_pe = sem("setup_pe")
        pads_out = sem("pads_out")
        chain = sem("chain")
        row_in = [sem(f"row_in{k}") for k in range(2)]
        win_in = [sem(f"win_in{k}") for k in range(2)]
        ef_in = [sem(f"ef_in{k}") for k in range(2)]
        gather_in = [[sem(f"gather_in{q}{k}") for k in range(NSB)] for q in range(2)]
        idx_ready = sem("idx_ready")
        oht_ready = sem("oht_ready")
        s_ready = sem("s_ready")
        expanded = sem("expanded")
        agg_done = sem("agg_done")
        acc_done = sem("acc_done")
        ef_turned = sem("ef_turned")
        eft_copied = sem("eft_copied")
        squared = sem("squared")
        z_copied = sem("z_copied")
        var_ready = sem("var_ready")
        std_ready = sem("std_ready")
        logits_ready = sem("logits_ready")
        logits_turned = sem("logits_turned")
        shifted = sem("shifted")
        weights_t = sem("weights_t")
        weights_turned = sem("weights_turned")
        ex_ready = sem("ex_ready")
        fac_arg = sem("fac_arg")
        fac_ready = sem("fac_ready")
        values_weighted = sem("values_weighted")
        attr_copied = sem("attr_copied")
        den_cols = sem("den_cols")
        host = sem("host")
        x_in = [sem(f"x_in{p}") for p in range(2)]
        x_turned = sem("x_turned")
        x_copied = sem("x_copied")
        x_squared = sem("x_squared")
        den_picked = sem("den_picked")
        attn_ready = sem("attn_ready")
        attn_squared = sem("attn_squared")
        attn_turned = sem("attn_turned")
        norm_done = sem("norm_done")
        norm_var = sem("norm_var")
        norm_std = sem("norm_std")
        ln_var = sem("ln_var")
        ln_std = sem("ln_std")
        mid_ready = sem("mid_ready")
        mid_turned = sem("mid_turned")
        mid_copied = sem("mid_copied")
        h_done = sem("h_done")
        h_biased = sem("h_biased")
        h_ready = sem("h_ready")
        h3_done = sem("h3_done")
        x_new = sem("x_new")
        new_turned = sem("new_turned")
        new_copied = sem("new_copied")
        tab_done = sem("tab_done")
        tab_copied = sem("tab_copied")
        tab_out = [sem(f"tab_out{p}") for p in range(2)]
        rows_out = [sem(f"rows_out{p}") for p in range(2)]
        res_done = sem("res_done")
        elu_arg = sem("elu_arg")
        elu_exp = sem("elu_exp")
        zeroed = sem("zeroed")

        dti = gall[:, 0:CH * P].bitcast(i32).rearrange("p (c e) -> p c e", e=P)
        dtf = gall[:, CH * P:2 * CH * P].rearrange("p (c e) -> p c e", e=P)
        sti = ze[:, :, :].rearrange("p a b -> p (a b)")[0:TC, 0:CH * P].bitcast(i32).rearrange("p (c e) -> p c e", e=P)
        stf = acc[0:TC, 0, 0:CH * P].rearrange("p (c e) -> p c e", e=P)
        dcol = acc[:, 1, 0:NT]
        first_b = acc[:, 1, NT:2 * NT]
        last_b = acc[:, 1, 2 * NT:3 * NT]
        diff = acc[:, 0, 3400:3400 + CH * P // 2]
        pen_single = acc[:, 1, 3 * NT:4 * NT]
        pick = acc[:, 1, 4 * NT:4 * NT + 2 * P].rearrange("p (k m) -> p k m", k=2)
        iota_i = acc[:, 0, 5100:5100 + P].bitcast(i32)
        pen_join_f = acc[:, 1, 5 * NT:6 * NT + 1]
        tile_tmp = acc[:, 1, 6 * NT + 8:7 * NT + 8]
        zeros = s_oh[:, 0:8, :].rearrange("p a b -> p (a b)")
        we_raw = efr[:, 0, 0:3, :].rearrange("p a b -> p (a b)")
        wn_raw = efr[:, 0, 3:5, :].rearrange("p a b -> p (a b)")
        a_raw = efr[:, 1, 0:4, :]
        prod = efr[:, 1, 4:6, :]
        b_raw = efr[:, 1, 6, :]
        ab_raw = efr[:, 1, 7, 0:H]
        u_col = efr[0:DU, 0, 5, 0:1]
        rsum = att[:, 0, 0:8]

        block = ctx.enter_context(nc.Block())


        def nth(counted_in, phase, i, p):
            return counted_in.index(str(phase)) * GROUPS + 2 * i + p + 1

        def started(i):
            return not (isinstance(i, int) and i == 0)

        def group_pairs(engine, body):
            body(0)
            with engine.Fori(1, GPAIRS) as i:
                body(i)

        def group_rows(tab, i, p):
            return tab[bass.ds((2 * i + p) * GN, GN), :].rearrange("(k n) d -> n k d", n=P)

        def following(i, q, k, last):
            if q == 0:
                return 2 * i + (1 + CH * k), i, 1
            return None if last else (2 * i + (2 + CH * k), i + 1, 0)

        def tiles(ap):
            return ap.rearrange("p (k d) -> p k d", k=GK)

        @block.sync
        def _(sp):
            def tile_rows(a, tile0, n):
                return a[tile0 * P:(tile0 + n) * P].rearrange("(t e) -> t e", e=P)

            def raw_indices(into, a, r0, skip=0):
                a = a[skip:E]
                sp.dma_start(into[r0:r0 + TC, 0:CH - 1, :],
                             tile_rows(a, 0, (CH - 1) * TC).rearrange("(c j) e -> j c e", j=TC)).then_inc(edges_in, 16)
                sp.dma_start(into[r0:r0 + LAST_FULL, CH - 1, :],
                             tile_rows(a, (CH - 1) * TC, LAST_FULL)).then_inc(edges_in, 16)
                sp.dma_start(into[r0 + LAST_FULL:r0 + LAST_FULL + 1, CH - 1, 0:LAST_REST - skip],
                             a[E - LAST_REST:E - skip].unsqueeze(0)).then_inc(edges_in, 16)

            sp.wait_ge(padded, 2)
            for h in range(H):
                raw_indices(dti, t["dst"], TC * h)
            raw_indices(sti, t["src"], 0)

            def load_weight(into, a):
                sp.dma_start(into, a).then_inc(weights_in, 16)

            load_weight(we_raw, t["L0_gnn_W_e"])
            load_weight(wn_raw, t["L0_gnn_W_n"])
            load_weight(be, t["L0_gnn_b_e"].partition_broadcast(P))
            load_weight(ae, t["L0_gnn_a_e"].partition_broadcast(P))
            load_weight(bn_row, t["L0_gnn_b_n"].partition_broadcast(P))
            load_weight(b3_row, t["L2_gnn_b3"].partition_broadcast(P))
            load_weight(w_t[:, 0, 0:D], t["L1_gnn_W_w"])
            load_weight(w_t[:, 1, 0:D], t["L3_gnn_W"])
            for k, a in enumerate((t["L1_gnn_a_w"][:, F:2 * F], t["L1_gnn_a_w"][:, 0:F],
                                   t["L3_gnn_att_src"], t["L3_gnn_att_dst"])):
                load_weight(a_raw[:, k, :].rearrange("p (h f) -> p h f", h=H), a.partition_broadcast(P))
            load_weight(b_t[:, 0, 0:D], t["L1_gnn_W_b"].partition_broadcast(P))
            load_weight(ab_raw, t["L1_gnn_a_b"].partition_broadcast(P))
            load_weight(w1[:, 0, :], t["L2_gnn_w1"][0:D, :])
            sp.wait_ge(w1_zero, 1)
            for h in range(H):
                load_weight(w1[F * h + F // 2:F * h + F, 1, :], t["L2_gnn_w1"][D + F // 2 * h:D + F // 2 * (h + 1), :])
            load_weight(w1u[:, :], t["L2_gnn_w1"][D + DU:D + 2 * DU, :])
            load_weight(u_col, t["L2_gnn_u"][0, :].unsqueeze(1))
            load_weight(w2[:, :, :], t["L2_gnn_w2"].rearrange("(k p) n -> p k n", p=P))
            load_weight(w3[:, :, :], t["L2_gnn_w3"].rearrange("(k p) n -> p k n", p=P))
            load_weight(w_res[:, :], t["L3_gnn_W_res"])
            for k in range(2):
                load_weight(b1_c[:, k:k + 1], t["L2_gnn_b1"][k * P:k * P + P].unsqueeze(1))
                load_weight(b2_c[:, k:k + 1], t["L2_gnn_b2"][k * P:k * P + P].unsqueeze(1))
            for k, name in enumerate(("bias", "bn_mean", "bn_var", "bn_gamma", "bn_beta")):
                load_weight(bn_raw[:, k:k + 1], t["L3_gnn_" + name].unsqueeze(1))

            sp.wait_ge(padded, 4)
            raw_indices(sti, t["dst"], 0, skip=1)

            sp.wait_ge(edges_in, 16 * 18)
            sp.dma_start(dst_pad.rearrange("(c j e) -> j c e", j=TC, e=P), dti[0:TC, :, :]).then_inc(pads_out, 16)
            sp.dma_start(x_pad[0:N, :], t["x"]).then_inc(pads_out, 16)
            sp.wait_ge(padded, 3)
            rest = (NP_ - N) // 7
            sp.dma_start(x_pad[N:NP_, :].rearrange("(p r) d -> p (r d)", r=7), zeros[0:rest, 0:7 * D]).then_inc(pads_out, 16)
            sp.wait_ge(pads_out, 48)

            def node_io(phase, x_from, store, x_free):
                def body(i):
                    for p in range(2):
                        if started(i):
                            x_free(i - 1, p)
                        sp.dma_start(tiles(nb("x", p)), group_rows(x_from, i, p)).then_inc(x_in[p], 16)
                        if started(i):
                            store(i - 1, p)
                group_pairs(sp, body)
                for p in range(2):
                    x_free(GPAIRS - 1, p)
                    store(GPAIRS - 1, p)

            def store_tables(layer, i, p, w0, w1_):
                tab = nb("tab", p, GK * (w0 + w1_)).rearrange("p (k w) -> p k w", k=GK)
                sp.dma_start(group_rows(src_tab[layer], i, p), tab[:, :, 0:w0]).then_inc(tab_out[p], 16)
                sp.dma_start(group_rows(dst_tab[layer], i, p), tab[:, :, w0:w0 + w1_]).then_inc(tab_out[p], 16)

            def store0(i, p):
                sp.wait_ge(tab_copied, nth("012", 0, i, p))
                store_tables(0, i, p, ZW, ZW)

            def free0(i, p):
                sp.wait_ge(x_turned, nth("013", 0, i, p))
                sp.wait_ge(x_squared, nth("01", 0, i, p))

            def store_gat(phase, x_to):
                def store(i, p):
                    sp.dma_start(group_rows(x_to, i, p), tiles(nb("new", p))).then_inc(tab_out[p], 16)
                    sp.wait_ge(tab_copied, nth("012", phase, i, p))
                    store_tables(phase, i, p, KW, H)
                return store

            def free_new(phase):
                return lambda i, p: sp.wait_ge(x_new, nth("123", phase, i, p))

            def edge_io(k, attr, width):
                regs = [sp.alloc_register(f"sp_first{k}_{m}") for m in range(SB)]

                def body(i, last=False):
                    for q in range(2):
                        for s in range(NSB):
                            u = 2 * NSB * i + (NSB * q + s + NSB * CH * k)
                            tile0 = 2 * TC * i + (q * TC + s * SB)
                            slot = s % 2
                            sp.wait_ge(oht_ready, u * SB + (OHT_CREDIT - SB))
                            sp.dma_start(dst_row[:, slot, :],
                                         dst_pad[bass.ds(tile0 * P, SB * P)].partition_broadcast(P)).then_inc(row_in[slot], 16)
                            sp.load(regs, first_i[0:1, bass.ds(tile0, SB)])
                            sp.wait_ge(expanded, u * SB + (EXP_CREDIT - SB))
                            for m in range(SB):
                                v = sp.snap(regs[m], min_val=0, max_val=N)
                                w = ZW if k == 0 else H
                                sp.dma_start(win[:, slot, m, 0:w], dst_tab[k][bass.ds(v, P), :]).then_inc(win_in[slot], 16)
                            if attr is None:
                                continue
                            if k == 0:
                                sp.wait_ge(squared, u * SB + (SQ_CREDIT - SB))
                            else:
                                sp.wait_ge(attr_copied, 2 * NSB * i + (NSB * q + s) + 1)
                            full = max(0, min(SB, LAST_FULL - s * SB)) if last and q == 1 else SB
                            for lo, hi in ((0, 6), (6, SB)):
                                if full >= hi:
                                    sp.dma_start(efr[:, slot, lo:hi, 0:width],
                                                 attr[bass.ds(tile0 * P + lo * P, (hi - lo) * P), :]
                                                 .rearrange("(j p) d -> p j d", p=P)).then_inc(ef_in[slot], 16)
                                else:
                                    assert lo == full
                                    sp.dma_start(efr[0:LAST_REST, slot, lo, 0:width],
                                                 attr[E - LAST_REST:E, :]).then_inc(ef_in[slot], 16)
                with sp.Fori(0, PAIRS - 1) as i:
                    body(i)
                body(PAIRS - 1, last=True)

            sp.wait_ge(setup_dve, SETUP_DONE)
            node_io(0, x_pad, store0, free0)
            for p in range(2):
                sp.wait_ge(tab_out[p], 32 * GPAIRS)
            edge_io(0, t["edge_attr_128"], D)
            sp.wait_ge(acc_done, NT + ACC_CREDIT)
            node_io(1, x_pad, store_gat(1, x1_pad), free_new(1))
            for p in range(2):
                sp.wait_ge(tab_out[p], (32 + 48) * GPAIRS)
            edge_io(1, t["edge_attr_64"], DU)
            sp.wait_ge(acc_done, 2 * NT + ACC_CREDIT)
            node_io(2, x1_pad, store_gat(2, x3_pad), free_new(2))
            for p in range(2):
                sp.wait_ge(tab_out[p], (32 + 96) * GPAIRS)
            edge_io(2, None, 0)
            sp.wait_ge(acc_done, 3 * NT + ACC_CREDIT)

            def store_out(i, p):
                here = GN if not isinstance(i, int) else min(GN, N - (2 * i + p) * GN)
                if here == GN:
                    sp.dma_start(group_rows(out, i, p), tiles(nb("new", p))).then_inc(rows_out[p], 16)
                elif here > 0:
                    assert here <= P
                    sp.dma_start(out[N - here:N, :], nb("new", p)[0:here, 0:D]).then_inc(rows_out[p], 16)

            node_io(3, x3_pad, store_out, free_new(3))
            for p in range(2):
                stored = GPAIRS - 1 + (N > (GROUPS - 2 + p) * GN)
                sp.wait_ge(rows_out[p], 16 * stored)

        @block.gpsimd
        def _(pool):
            pool.memset(dti[:, :, :], N).then_inc(padded, 1)
            pool.memset(sti[:, :, :], 0).then_inc(padded, 1)
            pool.memset(zeros, 0.0).then_inc(padded, 1)
            pool.memset(ident[:, :], 0.0).then_inc(consts, 1)
            pool.memset(sel[:, :], 0.0).then_inc(consts, 1)
            pool.memset(w1[:, 1, :], 0.0).then_inc(w1_zero, 1)
            pool.memset(pick, 0.0).then_inc(consts, 1)
            pool.wait_ge(setup_dve, STF_READY)
            pool.memset(sti[:, :, :], N).then_inc(padded, 1)
            pool.iota(iota_i, [[1, P]], 0, 0).then_inc(consts, 1)
            pool.iota(col_i[:, :], [[0, 2]], 0, 1).then_inc(consts, 1)
            pool.wait_ge(consts, 5)
            pool.affine_select(out=ident[:, :], in_=ident[:, :], compare_op=ALU.not_equal, fill=1.0,
                               base=0, pattern=[[-1, P]], channel_multiplier=1).then_inc(consts, 1)
            s4 = sel[:, :].rearrange("p (h f) -> p h f", h=H)
            pool.affine_select(out=s4, in_=s4, compare_op=ALU.not_equal, fill=1.0,
                               base=0, pattern=[[-F, H], [0, F]], channel_multiplier=1).then_inc(consts, 1)
            pool.affine_select(out=pick, in_=pick, compare_op=ALU.not_equal, fill=1.0,
                               base=0, pattern=[[-(P - 1), 2], [0, P]], channel_multiplier=1).then_inc(consts, 1)

            def gathers(k):
                width = ZW if k == 0 else KW

                def body(i):
                    for q in range(2):
                        gc = 2 * i + (q + CH * k)
                        pool.wait_ge(acc_done, gc * TC + (ACC_CREDIT - TC))
                        pool.sem_inc(host, 1)
                        pool.tensor_copy(idx[:, q, :], src_i[:, bass.ds(2 * TC * i + q * TC, TC)]).then_inc(idx_ready, 1)
                        pool.wait_ge(idx_ready, gc + 1)
                        pool.sem_inc(host, 1)
                        for j in range(TC):
                            pool.indirect_dma_start(g(q, j, width), None, src_tab[k],
                                                    bass.IndirectOffsetOnAxis(idx[:, q, j:j + 1], 0)
                                                    ).then_inc(gather_in[q][j // SB], 16)
                with pool.Fori(0, PAIRS) as i:
                    body(i)

            def clear_acc(n):
                pool.memset(acc[:, :, :], 0.0).then_inc(zeroed, 1)

            pool.wait_ge(setup_dve, SETUP_DONE)
            clear_acc(1)
            for p in range(2):
                pool.wait_ge(tab_out[p], 32 * GPAIRS)
            gathers(0)
            pool.wait_ge(norm_done, nth("1", 1, GPAIRS - 1, 1))
            clear_acc(2)
            for p in range(2):
                pool.wait_ge(tab_out[p], (32 + 48) * GPAIRS)
            gathers(1)
            pool.wait_ge(h_ready, 2 * GROUPS)
            clear_acc(3)
            for p in range(2):
                pool.wait_ge(tab_out[p], (32 + 96) * GPAIRS)
            gathers(2)

        @block.scalar
        def _(act):
            act.sem_inc(eft_copied, 2)
            act.sem_inc(z_copied, 1)
            act.sem_inc(squared, SQ_CREDIT)
            act.sem_inc(attr_copied, 2)
            act.wait_ge(setup_dve, BN_VAR)
            nc.scalar.activation(vec[:, 11:12], bn_raw[:, 2:3], ACT.Sqrt, bias=eps).then_inc(bn_std, 1)

            def nodes0(i):
                for p in range(2):
                    act.wait_ge(x_turned, nth("013", 0, i, p))
                    if started(i):
                        act.wait_ge(tab_done, nth("012", 0, i - 1, p))
                    nc.scalar.activation(nb("xt", p), bank[4 * p][:, 0:GN], ACT.Copy).then_inc(x_copied, 1)
                    if started(i):
                        act.wait_ge(tab_copied, nth("012", 0, i - 1, p))
                    for kk in range(GK):
                        ins = nc.scalar.activation(nb("xt2", p)[:, kk * P:kk * P + P], nb("x", p)[:, kk * P:kk * P + P],
                                                   ACT.Square, accum_out=nb("small", p, 2)[:, kk:kk + 1])
                    ins.then_inc(x_squared, 1)

            def chunk_tail(gc):
                act.wait_ge(shifted, gc + 1)
                nc.scalar.activation(ext[:, :], lg[:, :], ACT.Exp).then_inc(weights_t, 1)
                act.wait_ge(fac_arg, gc + 1)
                nc.scalar.activation(fac[:, 0:1], blk[:, 0, 0:1], ACT.Exp).then_inc(fac_ready, 1)

            def edges0(i):
                for q in range(2):
                    gc = 2 * i + q
                    act.wait_ge(acc_done, gc * TC + ACC_CREDIT)

                    def copy_turned(g4):
                        gg = 2 * 8 * i + (q * 8 + g4)
                        act.wait_ge(ef_turned, gg + 1)
                        act.wait_ge(expanded, 4 * gg + (EXP_CREDIT - 4))
                        nc.scalar.activation(eft[:, g4 % 2, :], efb[g4 % 2][:, :], ACT.Copy).then_inc(eft_copied, 1)

                    copy_turned(0)
                    for g4 in range(8):
                        if g4 + 1 < 8:
                            copy_turned(g4 + 1)
                        gg = 2 * 8 * i + (q * 8 + g4)
                        act.wait_ge(ef_in[(g4 // 2) % 2], 128 * i + (64 * q + 32 * (g4 // 4) + 32))
                        for m in range(4):
                            j = 4 * g4 + m
                            tt = 2 * TC * i + (q * TC + j)
                            act.wait_ge(squared, tt + (SQ_CREDIT - 1))
                            nc.scalar.activation(junk[:, m % 2, :], efr[:, (g4 // 2) % 2, j % SB, :], ACT.Square,
                                                 accum_out=att[:, 0, j:j + 1]).then_inc(squared, 1)
                        act.wait_ge(expanded, 4 * gg + 4 + EXP_CREDIT)
                        nc.scalar.activation(ze[:, 4 * g4:4 * g4 + 4, :].rearrange("p (a b) d -> p a b d", a=2),
                                             zb[:, :, 0:2 * ZW].rearrange("p a (b d) -> p a b d", b=2),
                                             ACT.Copy).then_inc(z_copied, 1)
                    act.wait_ge(var_ready, gc + 1)
                    nc.scalar.activation(att[:, 3, :], att[:, 2, :], ACT.Sqrt, bias=eps).then_inc(std_ready, 1)
                    chunk_tail(gc)
                    act.wait_ge(ex_ready, gc + 1)
                    for j in range(TC):
                        ins = nc.scalar.activation(ze[:, j, 0:D], ze[:, j, 0:D], ACT.Copy, scale=ex[:, j:j + 1])
                        if j % SB == SB - 1:
                            ins.then_inc(values_weighted, 1)

            def edges1(i):
                for q in range(2):
                    gc = 2 * i + (q + CH)
                    for s in range(NSB):
                        act.wait_ge(acc_done, gc * TC + (ACC_CREDIT - TC + s * SB + SB))
                        act.wait_ge(ef_in[s % 2], 128 * i + (64 * q + 32 * (s // 2) + 32) + 64 * CH)
                        nc.scalar.activation(
                            ze[:, s * SB:s * SB + SB, 0:D].rearrange("p j (h x) -> p j h x", h=H)[:, :, :, F // 2:F],
                            efr[:, s % 2, :, 0:DU].rearrange("p j (h x) -> p j h x", h=H), ACT.Copy).then_inc(attr_copied, 1)
                    chunk_tail(gc)
                    act.wait_ge(ex_ready, gc + 1)
                    nc.scalar.activation(
                        ze[:, :, 0:D].rearrange("p j (h x) -> p j h x", h=H)[:, :, :, 0:F // 2],
                        ex[:, :].rearrange("p (h j) -> p j h", h=H).unsqueeze(3).to_broadcast([P, TC, H, F // 2]),
                        ACT.Copy).then_inc(den_cols, 1)

            def edges2(i):
                for q in range(2):
                    gc = 2 * i + (q + 2 * CH)
                    act.wait_ge(acc_done, gc * TC + ACC_CREDIT)
                    chunk_tail(gc)
                    act.wait_ge(ex_ready, gc + 1)
                    nc.scalar.activation(
                        ze[:, :, 0:D].rearrange("p j (h x) -> p j h x", h=H),
                        ex[:, :].rearrange("p (h j) -> p j h", h=H).unsqueeze(3).to_broadcast([P, TC, H, F]),
                        ACT.Copy).then_inc(den_cols, 1)

            def sqrt_step(wait_on, count, out_ap, in_ap, scale, done):
                act.wait_ge(wait_on, count)
                nc.scalar.activation(out_ap, in_ap, ACT.Sqrt, bias=eps, scale=scale).then_inc(done, 1)

            def ln_columns(p):
                sm = nb("small", p, 40)
                return sm[:, 28:30], sm[:, 24:28].rearrange("p (k s) -> p k s", k=GK)[:, :, 1]

            def turn_new(phase, i, p, bank_ap):
                act.wait_ge(new_turned, nth("12", phase, i, p))
                if started(i):
                    act.wait_ge(tab_done, nth("012", phase, i - 1, p))
                nc.scalar.activation(nb("newt", p), bank_ap, ACT.Copy).then_inc(new_copied, 1)

            def nodes1(i):
                for p in range(2):
                    act.wait_ge(x_turned, nth("013", 1, i, p))
                    if started(i):
                        act.wait_ge(norm_done, nth("1", 1, i - 1, p))
                    nc.scalar.activation(nb("xt", p), bank[4 * p][:, 0:GN], ACT.Copy).then_inc(x_copied, 1)
                    nc.scalar.activation(nb("xt2", p), bank[4 * p][:, 0:GN], ACT.Square).then_inc(x_squared, 1)
                for p in range(2):
                    act.wait_ge(attn_ready, nth("123", 1, i, p))
                    nc.scalar.activation(nb("at2", p), nb("at", p), ACT.Square).then_inc(attn_squared, 1)
                for p in range(2):
                    sm = nb("small", p, 40)
                    sqrt_step(norm_var, nth("1", 1, i, p), sm[:, 6:8], sm[:, 4:6], 1.0, norm_std)
                for p in range(2):
                    sqrt_step(ln_var, nth("1", 1, i, p), *ln_columns(p), 1.0, ln_std)
                for p in range(2):
                    turn_new(1, i, p, bank[4 * p + 2][:, 0:GN])

            def nodes2(i):
                for p in range(2):
                    sqrt_step(ln_var, GROUPS + 4 * i + p + 1, *ln_columns(p), 1.0, ln_std)
                for p in range(2):
                    act.wait_ge(mid_turned, 2 * i + p + 1)
                    if started(i):
                        act.wait_ge(h_done, 4 * i - 4 + p + 1)
                    nc.scalar.activation(nb("xt", p), bank[4 * p + 1][:, 0:GN], ACT.Copy).then_inc(mid_copied, 1)
                for layer, (buf, bias) in enumerate((("h1", b1_c), ("h2", b2_c))):
                    for p in range(2):
                        act.wait_ge(h_done, 4 * i + (2 * layer + p + 1))
                        if started(i):
                            act.wait_ge(h3_done, 2 * i + p - 1)
                        for o in range(2):
                            ins = nc.scalar.activation(nb(buf, p, 2 * GN)[:, o * GN:o * GN + GN],
                                                       bank[4 * p + 2 + layer][:, o * GN:o * GN + GN],
                                                       ACT.Identity, bias=bias[:, o:o + 1])
                        ins.then_inc(h_biased, 1)
                for p in range(2):
                    sqrt_step(ln_var, GROUPS + 4 * i + p + 3, *ln_columns(p), 1.0, ln_std)
                for p in range(2):
                    turn_new(2, i, p, bank[4 * p + 1][:, GN:2 * GN])

            def nodes3(i):
                for p in range(2):
                    act.wait_ge(x_turned, nth("013", 3, i, p))
                    if started(i):
                        act.wait_ge(res_done, nth("3", 3, i - 1, p))
                    nc.scalar.activation(nb("xt", p), bank[4 * p][:, 0:GN], ACT.Copy).then_inc(x_copied, 1)
                for p in range(2):
                    act.wait_ge(elu_arg, nth("3", 3, i, p))
                    nc.scalar.activation(nb("at2", p), nb("tmp", p), ACT.Exp).then_inc(elu_exp, 1)
                for p in range(2):
                    sqrt_step(ln_var, 3 * GROUPS + 2 * i + p + 1, *ln_columns(p), 1.0, ln_std)

            group_pairs(act, nodes0)
            with act.Fori(0, PAIRS) as i:
                edges0(i)
            group_pairs(act, nodes1)
            with act.Fori(0, PAIRS) as i:
                edges1(i)
            group_pairs(act, nodes2)
            with act.Fori(0, PAIRS) as i:
                edges2(i)
            group_pairs(act, nodes3)

        @block.tensor
        def _(pe):
            mm = nc.tensor.matmul
            pe.sem_inc(expanded, EXP_CREDIT)
            pe.sem_inc(agg_done, AGG_CREDIT)

            pe.wait_ge(consts, 8)
            pe.wait_ge(setup_dve, DTF_READY)
            for c in range(CH):
                ins = nc.tensor.transpose(bank[c // 16][:, TC * (c % 16):TC * (c % 16) + TC], dtf[0:TC, c, :], ident[0:TC, 0:TC])
            ins.then_inc(setup_pe, 1)
            pe.wait_ge(setup_dve, STF_READY)
            for c in range(CH):
                ins = nc.tensor.transpose(zb[:, c // 16, TC * (c % 16):TC * (c % 16) + TC], stf[:, c, :], ident[0:TC, 0:TC])
            ins.then_inc(setup_pe, 1)
            pe.wait_ge(setup_dve, DCOL_READY)
            for k in range(2):
                for n in range(2):
                    lo, hi = 512 * n, min(512 * n + 512, NT)
                    ins = mm(bank[4 + 2 * k + n][:, 0:hi - lo], pick[:, k, :], dcol[:, lo:hi], start=True, stop=True)
            ins.then_inc(setup_pe, 1)
            pe.wait_ge(setup_dve, NEXT_READY)
            for c in range(CH):
                ins = nc.tensor.transpose(zb[:, c // 16, TC * (c % 16):TC * (c % 16) + TC], stf[:, c, :], ident[0:TC, 0:TC])
            ins.then_inc(setup_pe, 1)
            pe.wait_ge(setup_dve, CENTRED)
            for k in range(3):
                nc.tensor.transpose(bank[0][:, k * P:k * P + P], we_raw[:, k * P:k * P + P], ident[:, :])
            for k in range(2):
                nc.tensor.transpose(bank[1][:, k * P:k * P + P], wn_raw[:, k * P:k * P + P], ident[:, :])
            for o in range(2):
                ins = mm(bank[1][:, 2 * P + o:2 * P + o + 1], w1u[:, o * P:o * P + P], u_col, start=True, stop=True)
            ins.then_inc(setup_pe, 1)
            pe.wait_ge(setup_dve, SETUP_DONE)

            def turn(src_ap, bank_ap, done):
                for kk in range(GK):
                    ins = nc.tensor.transpose(bank_ap[:, kk * P:kk * P + P], src_ap[:, kk * P:kk * P + P], ident[:, :])
                ins.then_inc(done, 1)

            def turn_x(phase, i, p):
                base = {0: 0, 1: 1, 2: 2, 3: 3}[phase] * 16 * GPAIRS
                pe.wait_ge(x_in[p], 16 * i + (base + 16))
                turn(nb("x", p), bank[4 * p][:, 0:GN], x_turned)

            def nodes0(i):
                for p in range(2):
                    if started(i):
                        pe.wait_ge(tab_copied, nth("012", 0, i - 1, p))
                    turn_x(0, i, p)
                    pe.wait_ge(x_copied, nth("013", 0, i, p))
                    for kk in range(GK):
                        ins = mm(bank[4 * p + 1 + kk][:, 0:2 * ZW], nb("xt", p)[:, kk * P:kk * P + P], w_sd[:, :],
                                 start=True, stop=True)
                    ins.then_inc(tab_done, 1)

            def expand(k, gc, i, q, which):
                for j in which:
                    s = j // SB
                    if j % SB == 0:
                        pe.wait_ge(win_in[s % 2], gc * 256 + 128 * (s // 2 + 1))
                    pe.wait_ge(oht_ready, gc * TC + (j + 1 + OHT_CREDIT))
                    mm(bank[2 + q][:, j:j + 3 * TC + 1:TC], oht[:, j % OHT_RING, :], win[:, s % 2, j % SB, 0:H],
                       start=True, stop=True).then_inc(expanded, 1)

            def sum_windows(gc, i, q, k, vals, dens, next_chunk=None):
                for j in range(TC):
                    tt = gc * TC + j
                    if j % SB == 0:
                        pe.wait_ge(values_weighted, gc * NSB + (j // SB + 1))
                    pe.wait_ge(s_ready, tt + 1)
                    pe.wait_ge(acc_done, tt + (ACC_CREDIT + 1 - AGG_RING))
                    slot = agg_ps(j % AGG_RING)
                    mm(slot[:, 0:P], vals(j), s_oh[:, j % S_RING, :], start=True, stop=True)
                    mm(slot[:, P:2 * P], dens(j), s_oh[:, j % S_RING, :], start=True, stop=True).then_inc(agg_done, 1)
                    if next_chunk is not None and j >= AGG_RING:
                        expand(k, *next_chunk, (j - AGG_RING,))
                if next_chunk is not None:
                    expand(k, *next_chunk, range(TC - AGG_RING, TC))

            def softmax_turns(gc):
                pe.wait_ge(logits_ready, gc + 1)
                nc.tensor.transpose(lt_ps, lg2[:, :], ident[:, :]).then_inc(logits_turned, 1)
                pe.wait_ge(weights_t, gc + 1)
                nc.tensor.transpose(ex_ps, ext[:, :], ident[:, :]).then_inc(weights_turned, 1)

            def edges0(i):
                for q in range(2):
                    gc = 2 * i + q
                    pe.wait_ge(acc_done, gc * TC + ACC_CREDIT)

                    def turn_edges(g4):
                        gg = 16 * i + (q * 8 + g4)
                        pe.wait_ge(ef_in[(g4 // 2) % 2], 128 * i + (64 * q + 32 * (g4 // 4) + 32))
                        pe.wait_ge(eft_copied, gg + 1)
                        for m in range(4):
                            ins = nc.tensor.transpose(efb[g4 % 2][:, m * P:m * P + P], efr[:, (g4 // 2) % 2, (4 * g4 + m) % SB, :],
                                                      ident[:, :])
                        ins.then_inc(ef_turned, 1)

                    turn_edges(0)
                    for g4 in range(8):
                        if g4 + 1 < 8:
                            turn_edges(g4 + 1)
                        gg = 16 * i + (q * 8 + g4)
                        s = g4 // 2
                        pe.wait_ge(eft_copied, gg + 1 + 2)
                        pe.wait_ge(z_copied, gg + 1)
                        if g4 % 2 == 0:
                            pe.wait_ge(gather_in[q][s], 128 * i + 128)
                            pe.wait_ge(win_in[s % 2], 512 * i + (256 * q + 128 * (s // 2) + 128))
                        for m in range(4):
                            j = 4 * g4 + m
                            z = zb[:, m // 2, ZW * (m % 2):ZW * (m % 2) + ZW]
                            mm(z, eft[:, g4 % 2, m * P:m * P + P], w_ef[:, :], start=True, stop=False)
                            mm(z, ident[:, :], g(q, j, ZW), start=False, stop=False)
                            pe.wait_ge(oht_ready, 2 * TC * i + (q * TC + j) + 1 + OHT_CREDIT)
                            mm(z, oht[:, j % OHT_RING, :], win[:, s % 2, j % SB, :], start=False, stop=True).then_inc(expanded, 1)
                    softmax_turns(gc)
                    sum_windows(gc, i, q, 0, lambda j: ze[:, j, 0:D], lambda j: ex[:, j:j + 1].to_broadcast([P, P]))

            def edges_gat(k):
                def edges(i, last=False):
                    for q in range(2):
                        gc = 2 * i + (q + CH * k)
                        softmax_turns(gc)
                        pe.wait_ge(den_cols, gc - (CH - 1))
                        sum_windows(gc, i, q, k, lambda j: g(q, j, D), lambda j: ze[:, j, 0:D],
                                    following(i, q, k, last))
                return edges

            def tables(phase, i, p, bank_ap):
                pe.wait_ge(new_copied, nth("12", phase, i, p))
                if started(i):
                    pe.wait_ge(tab_copied, nth("012", phase, i - 1, p))
                for kk in range(GK):
                    ins = mm(bank_ap[:, kk * TW:kk * TW + TW], nb("newt", p)[:, kk * P:kk * P + P], w_t[:, phase - 1, :],
                             start=True, stop=True)
                ins.then_inc(tab_done, 1)

            def nodes1(i):
                for p in range(2):
                    turn_x(1, i, p)
                for p in range(2):
                    pe.wait_ge(attn_squared, nth("1", 1, i, p))
                    for kk in range(GK):
                        z = bank[4 * p + 1][:, kk * ZW:kk * ZW + ZW]
                        c = slice(kk * P, kk * P + P)
                        mm(z, nb("xt", p)[:, c], w_n[:, 0, :], start=True, stop=False)
                        mm(z, nb("at", p)[:, c], w_n[:, 1, :], start=False, stop=False)
                        mm(z[:, D + 1:ZW], nb("xt2", p)[:, c], one_c, start=False, stop=False)
                        ins = mm(z[:, D + 1:ZW], nb("at2", p)[:, c], one_c, start=False, stop=True)
                    ins.then_inc(norm_done, 1)
                for p in range(2):
                    pe.wait_ge(x_new, nth("123", 1, i, p))
                    turn(nb("new", p), bank[4 * p + 2][:, 0:GN], new_turned)
                for p in range(2):
                    tables(1, i, p, bank[4 * p + 3])

            def nodes2(i):
                def nodes(p):
                    return bass.ds(2 * GN * i + p * GN, GN)
                for p in range(2):
                    mm(bank[4 * p][:, 0:GN], sel[:, :], acc[:, 1, nodes(p)], start=True, stop=True).then_inc(den_picked, 1)
                for p in range(2):
                    pe.wait_ge(attn_ready, nth("123", 2, i, p))
                    turn(nb("at", p), bank[4 * p][:, GN:2 * GN], attn_turned)
                for p in range(2):
                    pe.wait_ge(mid_ready, 2 * i + p + 1)
                    turn(nb("at2", p), bank[4 * p + 1][:, 0:GN], mid_turned)
                for p in range(2):
                    pe.wait_ge(mid_copied, 2 * i + p + 1)
                    if started(i):
                        pe.wait_ge(tab_copied, nth("012", 2, i - 1, p))
                    for o in range(2):
                        z = bank[4 * p + 2][:, o * GN:o * GN + GN]
                        mm(z, w1[:, 0, o * P:o * P + P], nb("xt", p), start=True, stop=False)
                        ins = mm(z, w1[:, 1, o * P:o * P + P], acc[:, 1, nodes(p)], start=False, stop=True)
                    ins.then_inc(h_done, 1)
                for p in range(2):
                    pe.wait_ge(h_ready, 4 * i + p + 1)
                    for o in range(2):
                        z = bank[4 * p + 3][:, o * GN:o * GN + GN]
                        for kk in range(2):
                            ins = mm(z, w2[:, kk, o * P:o * P + P], nb("h1", p, 2 * GN)[:, kk * GN:kk * GN + GN],
                                     start=(kk == 0), stop=(kk == 1))
                    ins.then_inc(h_done, 1)
                for p in range(2):
                    pe.wait_ge(h_ready, 4 * i + p + 3)
                    for n in range(GK):
                        z = bank[4 * p + 3][:, n * P:n * P + P]
                        for kk in range(2):
                            ins = mm(z, nb("h2", p, 2 * GN)[:, kk * GN + n * P:kk * GN + n * P + P], w3[:, kk, :],
                                     start=(kk == 0), stop=(kk == 1))
                    ins.then_inc(h3_done, 1)
                for p in range(2):
                    pe.wait_ge(x_new, nth("123", 2, i, p))
                    turn(nb("new", p), bank[4 * p + 1][:, GN:2 * GN], new_turned)
                for p in range(2):
                    tables(2, i, p, bank[4 * p + 2])

            def nodes3(i):
                for p in range(2):
                    turn_x(3, i, p)
                for p in range(2):
                    pe.wait_ge(x_copied, nth("013", 3, i, p))
                    mm(bank[4 * p + 1][:, 0:GN], w_res[:, :], nb("xt", p), start=True, stop=True).then_inc(res_done, 1)
                for p in range(2):
                    pe.wait_ge(attn_ready, nth("123", 3, i, p))
                    turn(nb("at", p), bank[4 * p + 2][:, 0:GN], attn_turned)

            group_pairs(pe, nodes0)
            pe.wait_ge(tab_copied, GROUPS)
            with pe.Fori(0, PAIRS) as i:
                edges0(i)
            pe.wait_ge(acc_done, NT + ACC_CREDIT)
            group_pairs(pe, nodes1)
            pe.wait_ge(tab_copied, 2 * GROUPS)
            expand(1, CH * 1, 0, 0, range(TC))
            with pe.Fori(0, PAIRS - 1) as i:
                edges_gat(1)(i)
            edges_gat(1)(PAIRS - 1, last=True)
            pe.wait_ge(acc_done, 2 * NT + ACC_CREDIT)
            group_pairs(pe, nodes2)
            pe.wait_ge(tab_copied, 3 * GROUPS)
            expand(2, CH * 2, 0, 0, range(TC))
            with pe.Fori(0, PAIRS - 1) as i:
                edges_gat(2)(i)
            edges_gat(2)(PAIRS - 1, last=True)
            pe.wait_ge(acc_done, 3 * NT + ACC_CREDIT)
            group_pairs(pe, nodes3)

        @block.vector
        def _(dve):
            v = nc.vector
            dve.sem_inc(oht_ready, OHT_CREDIT)
            dve.sem_inc(acc_done, ACC_CREDIT)

            count = [0]

            def did(ins):
                count[0] += 1
                ins.then_inc(setup_dve, 1)
                return count[0]

            def then(ins):
                dve.wait_ge(setup_dve, did(ins))

            dve.wait_ge(edges_in, 16 * 15)
            assert did(v.tensor_copy(dtf, dti)) == DTF_READY
            assert did(v.tensor_copy(stf, sti)) == STF_READY
            dve.wait_ge(setup_pe, 2)
            for n in range(2):
                lo, hi = 512 * n, min(512 * n + 512, NT)
                did(v.tensor_copy(dcol[:, lo:hi], bank[n][:, 0:hi - lo]))
                did(v.tensor_copy(src_i[:, lo:hi], zb[:, n, 0:hi - lo]))
            dve.wait_ge(setup_dve, count[0])
            assert did(v.tensor_copy(first_i[:, :], dcol[0:1, :])) == DCOL_READY
            dve.wait_ge(edges_in, 16 * 18)
            assert did(v.tensor_copy(stf, sti)) == NEXT_READY
            dve.wait_ge(consts, 8)
            did(v.tensor_copy(iota_row[:, :], iota_i))
            did(v.tensor_copy(iota_c, col_i[:, 0:1]))
            then(v.tensor_scalar(col_i[:, 1:2], col_i[:, 0:1], F // 2, None, ALU.bitwise_and))
            then(v.tensor_copy(attr_mask, col_i[:, 1:2]))
            then(v.tensor_scalar(attr_mask, attr_mask, 2.0 / F, None, ALU.mult))
            then(v.tensor_scalar(den_mask, attr_mask, -1.0, 1.0, ALU.mult, ALU.add))
            did(v.memset(one_c, 1.0))
            dve.wait_ge(weights_in, 16 * N_WEIGHTS)
            assert did(v.memset(eps, EPS)) == BN_VAR
            then(v.tensor_reduce(rsum[:, 0:1], we_raw, AX.X, ALU.add))
            then(v.tensor_reduce(rsum[:, 1:2], wn_raw, AX.X, ALU.add))
            then(v.tensor_scalar(rsum[:, 2:3], rsum[:, 0:1], -1.0 / (3 * D), None, ALU.mult))
            then(v.tensor_scalar(rsum[:, 3:4], rsum[:, 1:2], -1.0 / (2 * D), None, ALU.mult))
            did(v.tensor_scalar(we_raw, we_raw, rsum[:, 2:3], None, ALU.add))
            assert did(v.tensor_scalar(wn_raw, wn_raw, rsum[:, 3:4], None, ALU.add)) == CENTRED
            dve.wait_ge(setup_pe, 3)
            for k, into in enumerate((first_b, last_b)):
                for n in range(2):
                    lo, hi = 512 * n, min(512 * n + 512, NT)
                    did(v.tensor_copy(into[:, lo:hi], bank[4 + 2 * k + n][:, 0:hi - lo]))
            dve.wait_ge(setup_dve, count[0])
            did(v.tensor_tensor(rel[:, :], dcol, first_b, ALU.subtract))
            dve.wait_ge(setup_pe, 4)
            for n in range(2):
                lo, hi = 512 * n, min(512 * n + 512, NT)
                then(v.tensor_tensor(tile_tmp[:, lo:hi], dcol[:, lo:hi], zb[:, n, 0:hi - lo], ALU.not_equal))
            then(v.tensor_scalar(times[:, :], tile_tmp[:, 0:NT], 1.0, None, ALU.add))
            did(v.tensor_scalar(nodew[:, :], first_b, iota_c, None, ALU.add))
            then(v.tensor_tensor(pen_single, first_b, last_b, ALU.not_equal))
            then(v.tensor_tensor(pen_join_f[:, 1:NT], first_b[:, 1:NT], last_b[:, 0:NT - 1], ALU.not_equal))
            did(v.memset(pen_join_f[:, 0:1], 1.0))
            then(v.memset(pen_join_f[:, NT:NT + 1], 1.0))
            did(v.tensor_scalar(pen_join[:, :], pen_join_f, BIG, None, ALU.mult))
            did(v.memset(carry_f[:, 0:1], BIG))
            then(v.tensor_tensor(tile_tmp[:, 0:NT], pen_join_f[:, 1:NT + 1], pen_single, ALU.max))
            did(v.tensor_scalar(carry_f[:, 1:NT + 1], tile_tmp[:, 0:NT], BIG, None, ALU.mult))
            then(v.memset(fac[:, :], 1.0))
            then(v.tensor_tensor(tile_tmp[:, 0:NT], pen_join_f[:, 0:NT], pen_single, ALU.max))
            did(v.tensor_scalar(carry_r[:, :, 0:TC - 1],
                                tile_tmp[:, 0:NT].rearrange("p (c j) -> p c j", j=TC)[:, :, 1:TC][:, :, ::-1],
                                BIG, None, ALU.mult))
            did(v.memset(pen_f[:, :, 0:1], 0.0))
            did(v.memset(pen_r[:, :, 0:1], 0.0))
            half = CH // 2
            for n in range(2):
                cs = slice(n * half, n * half + half)
                d3 = dtf[:, cs, :]
                df = diff.rearrange("p (c e) -> p c e", e=P)
                dve.wait_ge(setup_dve, count[0])
                then(v.tensor_tensor(df[:, :, 1:P], d3[:, :, 1:P], d3[:, :, 0:P - 1], ALU.not_equal))
                did(v.tensor_scalar(pen_f[:, cs, 1:P], df[:, :, 1:P], BIG, None, ALU.mult))
                then(v.tensor_scalar(pen_r[:, cs, 1:P], df[:, :, 1:P][:, :, ::-1], BIG, None, ALU.mult))
                then(v.tensor_tensor(df, d3, d3[:, :, 0:1].to_broadcast([P, half, P]), ALU.not_equal))
                then(v.tensor_scalar(pen_first[:, cs, :], df, BIG, None, ALU.mult))
                then(v.tensor_tensor(df, d3, d3[:, :, P - 1:P].to_broadcast([P, half, P]), ALU.not_equal))
                then(v.tensor_scalar(pen_last[:, cs, :], df, BIG, None, ALU.mult))
            dve.wait_ge(setup_pe, 5)
            did(v.tensor_copy(w_sd[:, 0:D], bank[0][:, 0:D]))
            did(v.tensor_copy(w_ef[:, 0:D], bank[0][:, D:2 * D]))
            did(v.tensor_copy(w_sd[:, ZW:ZW + D], bank[0][:, 2 * D:3 * D]))
            for k in range(2):
                did(v.tensor_copy(w_n[:, k, 0:D], bank[1][:, k * D:k * D + D]))
                did(v.memset(w_n[:, k, D:D + 1], 1.0))
                did(v.memset(w_n[:, k, D + 1:ZW], 0.0))
                did(v.memset(w_sd[:, k * ZW + D:k * ZW + D + 1], 1.0))
                did(v.memset(w_sd[:, k * ZW + D + 1:k * ZW + ZW], 0.0))
            did(v.memset(w_ef[:, D:D + 1], 1.0))
            did(v.memset(w_ef[:, D + 1:ZW], 0.0))
            did(v.memset(b_t[:, 1, :], 0.0))
            for layer in range(2):
                for w in range(2):
                    a = a_raw[:, 2 * layer + w, :]
                    at = slice(D + H * w, D + H * w + H)
                    then(v.tensor_tensor(prod[:, w, :], w_t[:, layer, 0:D], a, ALU.mult))
                    then(v.tensor_reduce(w_t[:, layer, at], prod[:, w, :].rearrange("p (h f) -> p h f", h=H), AX.X, ALU.add))
                    if layer == 0:
                        then(v.tensor_tensor(prod[:, w, :], b_t[:, layer, 0:D], a, ALU.mult))
                        then(v.tensor_reduce(b_t[:, layer, at], prod[:, w, :].rearrange("p (h f) -> p h f", h=H), AX.X, ALU.add))
            then(v.tensor_tensor(b_t[:, 0, D + H:TW], b_t[:, 0, D + H:TW], ab_raw, ALU.add))
            dve.wait_ge(bn_std, 1)
            then(v.reciprocal(vec[:, 12:13], vec[:, 11:12]))
            then(v.tensor_tensor(bn_scale, vec[:, 12:13], bn_raw[:, 3:4], ALU.mult))
            then(v.tensor_tensor(vec[:, 13:14], bn_raw[:, 0:1], bn_raw[:, 1:2], ALU.subtract))
            then(v.tensor_tensor(vec[:, 14:15], vec[:, 13:14], bn_scale, ALU.mult))
            did(v.tensor_tensor(bn_shift, vec[:, 14:15], bn_raw[:, 4:5], ALU.add))
            dve.wait_ge(setup_pe, 5)
            did(v.tensor_tensor(b1_c, b1_c, bank[1][:, 2 * P:2 * P + 2], ALU.add))
            did(v.memset(blk[:, :, :], BIG))
            assert did(v.memset(cin[:, :, :], BIG)) == SETUP_DONE, count[0]
            dve.wait_ge(setup_dve, SETUP_DONE)

            steps = {"base": 0, "n": 0, "total": 0}

            def step(ins):
                steps["n"] += 1
                ins.then_inc(chain, 1)

            def ordered(ins=None):
                if ins is not None:
                    step(ins)
                dve.wait_ge(chain, steps["base"] + steps["n"])

            def stepped_loop(name, body, n, peel, peel_last=False):
                per = STEPS[name]
                start = steps["total"]
                if peel:
                    steps.update(base=start, n=0)
                    body(0)
                    assert steps["n"] == per, (name, steps["n"])
                with dve.Fori(int(peel), n - int(peel_last)) as i:
                    steps.update(base=start + per * i, n=0)
                    body(i)
                    assert steps["n"] == per, (name, steps["n"])
                if peel_last:
                    steps.update(base=start + per * (n - 1), n=0)
                    body(n - 1, last=True)
                    assert steps["n"] == per, (name, steps["n"])
                steps["total"] = start + per * n

            def nodes0(i):
                for p in range(2):
                    dve.wait_ge(tab_done, nth("012", 0, i, p))
                    dve.wait_ge(x_squared, nth("01", 0, i, p))
                    if started(i):
                        dve.wait_ge(tab_out[p], 32 * i)
                    tab = nb("tab", p, GK * 2 * ZW).rearrange("p (k s w) -> p k s w", k=GK, s=2)
                    for kk in range(GK):
                        v.tensor_copy(tab[:, kk, :, 0:D + 1],
                                      bank[4 * p + 1 + kk][:, 0:2 * ZW].rearrange("p (s w) -> p s w", s=2)[:, :, 0:D + 1])
                    v.tensor_copy(tab[:, :, :, D + 1],
                                  nb("small", p, 2).unsqueeze(2).to_broadcast([P, GK, 2])).then_inc(tab_copied, 1)

            def softmax(gc, i, q, k):
                c = bass.ds(2 * i + q, 1)
                t0 = 2 * TC * i + q * TC
                pf = pen_f[:, c, 0:P].rearrange("p a e -> p (a e)")
                pr = pen_r[:, c, :].rearrange("p a e -> p (a e)")
                p_first = pen_first[:, c, :].rearrange("p a e -> p (a e)")
                p_last = pen_last[:, c, :].rearrange("p a e -> p (a e)")
                cq, cp = cin[:, q, :], cin[:, 1 - q, :]
                made = [0]

                def ordered_(ins):
                    step(ins)
                    window_onehot(gc, i, q, made[0])
                    made[0] += 1
                    ordered()

                dve.wait_ge(logits_turned, gc + 1)
                step(v.tensor_copy(cq[:, 0:1], cp[:, 32:33]))
                ordered_(v.tensor_tensor_scan(mx[:, :], pf, lt_ps, BIG, ALU.add, ALU.max))
                ordered_(v.transpose(blk[:, 0, :], mx[:, P - 32:P]))
                ordered_(v.tensor_tensor(blk[:, 1, :], blk[:, 0, :], pen_join[:, bass.ds(t0 + 1, TC)], ALU.add))
                ordered_(v.tensor_tensor_scan(cq[:, 1:33], carry_f[:, bass.ds(t0 + 1, TC)], blk[:, 1, :], cq[:, 0:1],
                                             ALU.add, ALU.max))
                ordered_(v.transpose(blk[:, 2, :], cq[:, 0:32]))
                ordered_(v.scalar_tensor_tensor(mx2[:, :], p_first, blk[:, 2, 31:32], mx[:, :], ALU.add, ALU.max))
                ordered_(v.tensor_tensor_scan(mx[:, ::-1], pr, mx2[:, ::-1], BIG, ALU.add, ALU.max))
                ordered_(v.transpose(blk[:, 3, :], mx[:, 0:32]))
                ordered_(v.tensor_tensor(blk[:, 4, 0:TC - 1], blk[:, 3, 1:TC], pen_join[:, bass.ds(t0 + 1, TC - 1)], ALU.add))
                ordered_(v.tensor_tensor_scan(blk[:, 5, 0:TC - 1][:, ::-1], carry_r[:, c, 0:TC - 1].rearrange("p a j -> p (a j)"),
                                             blk[:, 4, 0:TC - 1][:, ::-1], BIG, ALU.add, ALU.max))
                ordered_(v.transpose(blk[:, 6, :], blk[:, 5, :]))
                ordered_(v.scalar_tensor_tensor(mx2[:, :], p_last, blk[:, 6, 0:1], mx[:, :], ALU.add, ALU.max))
                v.tensor_tensor(lg[:, :], lt_ps, mx2[:, :], ALU.subtract).then_inc(shifted, 1)
                ordered_(v.tensor_tensor(blk[:, 7, :], blk[:, 2, 31:32].to_broadcast([P, 32]),
                                        mx2[:, 0:1].to_broadcast([P, 32]), ALU.subtract))
                v.transpose(blk[:, 0, :], blk[:, 7, :]).then_inc(fac_arg, 1)
                for j in range(made[0], S_RING):
                    window_onehot(gc, i, q, j)

            def window_onehot(gc, i, q, j):
                dve.wait_ge(agg_done, gc * TC + j + 1)
                v.tensor_scalar(s_oh[:, j % S_RING, :], iota_row[:, :], rel[:, bass.ds(2 * TC * i + (q * TC + j), 1)], None,
                                ALU.is_equal).then_inc(s_ready, 1)

            def edge_onehots(gc, i, q, which):
                for j in which:
                    s = j // SB
                    if j % SB == 0:
                        dve.wait_ge(row_in[s % 2], gc * 32 + (s // 2 + 1) * 16)
                    dve.wait_ge(expanded, gc * TC + (j - OHT_RING + 1 + EXP_CREDIT))
                    v.tensor_scalar(oht[:, j % OHT_RING, :], dst_row[:, s % 2, (j % SB) * P:(j % SB) * P + P],
                                    nodew[:, bass.ds(2 * TC * i + (q * TC + j), 1)], None, ALU.is_equal).then_inc(oht_ready, 1)

            def rescale_and_sum(gc, i, q, k, regs, following=None):
                dve.load(regs, first_i[0:1, bass.ds(2 * TC * i + q * TC, SB)])
                dve.wait_ge(fac_ready, gc + 1)
                first = dve.snap(regs[0], min_val=0, max_val=N)
                dve.wait_ge(acc_done, gc * TC + ACC_CREDIT)
                if k == 1:
                    ordered(v.scalar_tensor_tensor(fac[:, 1:2], fac[:, 0:1], den_mask, attr_mask, ALU.mult, ALU.add))
                    for half, f in ((0, fac[:, 0:1]), (1, fac[:, 1:2])):
                        col = acc[:, half, bass.ds(first, 1)]
                        step(v.tensor_scalar(col, col, f, None, ALU.mult))
                    ordered()
                else:
                    col = acc[:, 0:2, bass.ds(first, 1)]
                    ordered(v.tensor_scalar(col, col, fac[:, 0:1], None, ALU.mult))
                for j in range(TC):
                    if j and j % SB == 0:
                        dve.load(regs, first_i[0:1, bass.ds(2 * TC * i + (q * TC + j), SB)])
                    if j < TC - S_RING:
                        window_onehot(gc, i, q, j + S_RING)
                    first = dve.snap(regs[j % SB], min_val=0, max_val=N)
                    win_acc = acc[:, 0:2, bass.ds(first, P)]
                    dve.wait_ge(agg_done, gc * TC + j + 1 + AGG_CREDIT)
                    if j:
                        dve.wait_ge(acc_done, gc * TC + j + ACC_CREDIT)
                    v.tensor_tensor(win_acc, win_acc, agg_ps(j % AGG_RING).rearrange("p (a n) -> p a n", a=2),
                                    ALU.add).then_inc(acc_done, 1)
                    if following is not None:
                        edge_onehots(*following, (j,))

            def copy_weights(gc, i, q, k):
                dve.wait_ge(weights_turned, gc + 1)
                if k == 0:
                    v.tensor_copy(ex[:, :], ex_ps).then_inc(ex_ready, 1)
                else:
                    v.tensor_tensor(ex[:, :].rearrange("p (h j) -> p h j", h=H), ex_ps.rearrange("p (h j) -> p h j", h=H),
                                    times[:, bass.ds(2 * TC * i + q * TC, TC)].unsqueeze(1).to_broadcast([P, H, TC]),
                                    ALU.mult).then_inc(ex_ready, 1)

            def edges0(i):
                for q in range(2):
                    gc = 2 * i + q
                    edge_onehots(gc, i, q, range(TC))
                    dve.wait_ge(z_copied, 8 * gc + 8 + 1)
                    dve.wait_ge(squared, gc * TC + (TC + SQ_CREDIT))
                    step(v.tensor_scalar(att[:, 1, :], ze[:, :, D], 1.0 / (3 * D), None, ALU.mult))
                    ordered(v.tensor_tensor(att[:, 4, :], ze[:, :, D + 1], att[:, 0, :], ALU.add))
                    ordered(v.tensor_tensor(att[:, 5, :], att[:, 1, :], att[:, 1, :], ALU.mult))
                    ordered(v.scalar_tensor_tensor(att[:, 6, :], att[:, 4, :], 1.0 / (3 * D), att[:, 5, :], ALU.mult, ALU.subtract))
                    v.tensor_scalar(att[:, 2, :], att[:, 6, :], 0.0, None, ALU.max).then_inc(var_ready, 1)
                    dve.wait_ge(std_ready, gc + 1)
                    ordered(v.reciprocal(att[:, 4, :], att[:, 3, :]))
                    for s in range(NSB):
                        for j in range(s * SB, s * SB + SB):
                            v_ins = v.scalar_tensor_tensor(ze[:, j, 0:D], ze[:, j, 0:D], att[:, 4, j:j + 1], be, ALU.mult, ALU.add)
                        ordered(v_ins)
                        zz = ze[:, s * SB:s * SB + SB, 0:D]
                        ordered(v.scalar_tensor_tensor(zz, zz, 0.01, zz, ALU.mult, ALU.max))
                        for j in range(s * SB, s * SB + SB):
                            v_ins = v.tensor_tensor_reduce(out=oht[:, j % OHT_RING, :], in0=ze[:, j, 0:D], in1=ae, scale=1.0,
                                                           scalar=0.0, op0=ALU.mult, op1=ALU.add, accum_out=att[:, 7, j:j + 1])
                        ordered(v_ins)
                    v.tensor_copy(lg2[:, :].rearrange("p (h j) -> p h j", h=H),
                                  att[:, 7, :].unsqueeze(1).to_broadcast([P, H, TC])).then_inc(logits_ready, 1)
                    softmax(gc, i, q, 0)
                    copy_weights(gc, i, q, 0)
                    rescale_and_sum(gc, i, q, 0, regs0)

            def edges_gat(k, regs):
                def edges(i, last=False):
                    for q in range(2):
                        gc = 2 * i + (q + CH * k)
                        dve.wait_ge(expanded, gc * TC + TC + EXP_CREDIT)
                        for s in range(NSB):
                            dve.wait_ge(gather_in[q][s], 128 * i + (128 + 128 * PAIRS * k))
                        ordered(v.tensor_tensor(lg[:, :].rearrange("p (h j) -> p h j", h=H),
                                                bank[2 + q][:, 0:P].rearrange("p (h j) -> p h j", h=H),
                                                gq(q)[:, :, D:KW].rearrange("p j h -> p h j"), ALU.add))
                        v.scalar_tensor_tensor(lg2[:, :], lg[:, :], 0.2, lg[:, :], ALU.mult, ALU.max).then_inc(logits_ready, 1)
                        softmax(gc, i, q, k)
                        copy_weights(gc, i, q, k)
                        dve.wait_ge(ex_ready, gc + 1)
                        for s in range(NSB):
                            vals = gq(q)[:, s * SB:s * SB + SB, 0:D].rearrange("p j (h x) -> p j h x", h=H)
                            w = ex[:, :].rearrange("p (h j) -> p j h", h=H)[:, s * SB:s * SB + SB, :]
                            v.tensor_tensor(vals, vals, w.unsqueeze(3).to_broadcast([P, SB, H, F]),
                                            ALU.mult).then_inc(values_weighted, 1)
                        rescale_and_sum(gc, i, q, k, regs, following(i, q, k, last))
                return edges

            def small(p):
                return nb("small", p, 40)

            def layer_norm(y, into, var_count, done, before_write):
                def part(p, lo, hi):
                    return small(p)[:, lo:hi].rearrange("p (k s) -> p k s", k=GK)
                for p in range(2):
                    for kk in range(GK):
                        ins = v.bn_stats(part(p, 12, 24)[:, kk, :], nb(y, p)[:, kk * P:kk * P + P])
                    step(ins)
                ordered()
                dve.sem_inc(host, 1)
                for p in range(2):
                    for kk in range(GK):
                        ins = v.bn_aggr(part(p, 24, 28)[:, kk, :], part(p, 12, 24)[:, kk, :])
                    ins.then_inc(ln_var, 1)
                for p in range(2):
                    dve.wait_ge(ln_std, var_count + p)
                    step(v.reciprocal(small(p)[:, 30:32], small(p)[:, 28:30]))
                ordered()
                for p in range(2):
                    before_write(p)
                    for kk in range(GK):
                        ins = v.tensor_scalar(nb(into, p)[:, kk * P:kk * P + P], nb(y, p)[:, kk * P:kk * P + P],
                                              part(p, 24, 28)[:, kk, 0:1], small(p)[:, 30 + kk:31 + kk],
                                              ALU.subtract, ALU.mult)
                    ins.then_inc(done, 1)

            def stored(phase, i):
                def wait(p):
                    if not started(i):
                        return
                    if phase == 3:
                        dve.wait_ge(rows_out[p], 16 * i)
                    else:
                        dve.wait_ge(tab_out[p], 48 * i + 32 * GPAIRS + 48 * GPAIRS * (phase - 1))
                return wait

            def copy_tables(phase, i, p, bank_ap):
                dve.wait_ge(tab_done, nth("012", phase, i, p))
                v.tensor_tensor(nb("tab", p, GK * TW).rearrange("p (k w) -> p k w", k=GK),
                                bank_ap[:, 0:GK * TW].rearrange("p (k w) -> p k w", k=GK),
                                b_t[:, phase - 1, :].unsqueeze(1).to_broadcast([P, GK, TW]), ALU.add).then_inc(tab_copied, 1)

            def bc(row):
                return row.unsqueeze(1).to_broadcast([P, GK, D])

            def both(make):
                for p in range(2):
                    step(make(p))
                ordered()

            def nodes1(i):
                def nodes(p):
                    return bass.ds(2 * GN * i + p * GN, GN)
                if started(i):
                    dve.wait_ge(norm_done, nth("1", 1, i - 1, 1))
                both(lambda p: v.tensor_scalar(nb("tmp", p), acc[:, 1, nodes(p)], TINY, None, ALU.max))
                both(lambda p: v.reciprocal(nb("tmp", p), nb("tmp", p)))
                for p in range(2):
                    v.tensor_tensor(nb("at", p), acc[:, 0, nodes(p)], nb("tmp", p), ALU.mult).then_inc(attn_ready, 1)
                z = [bank[4 * p + 1][:, 0:GK * ZW].rearrange("p (k w) -> p k w", k=GK) for p in range(2)]
                sm = [small(p) for p in range(2)]
                dve.wait_ge(norm_done, nth("1", 1, i, 1))
                both(lambda p: v.tensor_scalar(sm[p][:, 0:2], z[p][:, :, D], 1.0 / (2 * D), None, ALU.mult))
                both(lambda p: v.tensor_tensor(sm[p][:, 2:4], sm[p][:, 0:2], sm[p][:, 0:2], ALU.mult))
                both(lambda p: v.scalar_tensor_tensor(sm[p][:, 8:10], z[p][:, :, D + 1], 1.0 / (2 * D), sm[p][:, 2:4],
                                                      ALU.mult, ALU.subtract))
                for p in range(2):
                    v.tensor_scalar(sm[p][:, 4:6], sm[p][:, 8:10], 0.0, None, ALU.max).then_inc(norm_var, 1)
                dve.wait_ge(norm_std, nth("1", 1, i, 1))
                both(lambda p: v.reciprocal(sm[p][:, 10:12], sm[p][:, 6:8]))
                both(lambda p: v.tensor_tensor(tiles(nb("h", p)), z[p][:, :, 0:D],
                                               sm[p][:, 10:12].unsqueeze(2).to_broadcast([P, GK, D]), ALU.mult))
                both(lambda p: v.tensor_tensor(tiles(nb("h", p)), tiles(nb("h", p)), bc(bn_row), ALU.add))
                both(lambda p: v.scalar_tensor_tensor(nb("h", p), nb("h", p), 0.01, nb("h", p), ALU.mult, ALU.max))
                both(lambda p: v.tensor_tensor(nb("h", p), nb("h", p), nb("x", p), ALU.add))
                layer_norm("h", "new", nth("1", 1, i, 0), x_new, stored(1, i))
                for p in range(2):
                    copy_tables(1, i, p, bank[4 * p + 3])

            def nodes2(i):
                def nodes(p):
                    return bass.ds(2 * GN * i + p * GN, GN)
                dve.wait_ge(den_picked, 2 * i + 2)
                both(lambda p: v.tensor_scalar(nb("tmp", p), bank[4 * p][:, 0:GN], TINY, None, ALU.max))
                both(lambda p: v.reciprocal(nb("tmp", p), nb("tmp", p)))
                if started(i):
                    dve.wait_ge(attn_turned, nth("23", 2, i - 1, 1))
                for p in range(2):
                    v.tensor_tensor(nb("at", p), acc[:, 0, nodes(p)], nb("tmp", p), ALU.mult).then_inc(attn_ready, 1)
                dve.wait_ge(attn_turned, nth("23", 2, i, 1))
                for p in range(2):
                    dve.wait_ge(x_in[p], 16 * i + 16 + 2 * 16 * GPAIRS)
                    step(v.tensor_tensor(nb("h", p), bank[4 * p][:, GN:2 * GN], nb("x", p), ALU.add))
                ordered()
                layer_norm("h", "at2", GROUPS + 4 * i + 1, mid_ready, lambda p: None)
                for layer, buf in enumerate(("h1", "h2")):
                    for p in range(2):
                        dve.wait_ge(h_biased, 4 * i + (2 * layer + p + 1))
                        b = nb(buf, p, 2 * GN)
                        v.scalar_tensor_tensor(b, b, 0.01, b, ALU.mult, ALU.max).then_inc(h_ready, 1)
                dve.wait_ge(h3_done, 2 * i + 2)
                both(lambda p: v.tensor_tensor(tiles(nb("h", p)), tiles(bank[4 * p + 3][:, 0:GN]), bc(b3_row), ALU.add))
                both(lambda p: v.tensor_tensor(nb("h", p), nb("h", p), nb("at2", p), ALU.add))
                layer_norm("h", "new", GROUPS + 4 * i + 3, x_new, stored(2, i))
                for p in range(2):
                    copy_tables(2, i, p, bank[4 * p + 2])

            def nodes3(i):
                def nodes(p):
                    return bass.ds(2 * GN * i + p * GN, GN)
                a = [nb("at", p) for p in range(2)]
                both(lambda p: v.tensor_scalar(nb("xt2", p), acc[:, 1, nodes(p)], TINY, None, ALU.max))
                both(lambda p: v.reciprocal(nb("xt2", p), nb("xt2", p)))
                if started(i):
                    dve.wait_ge(attn_turned, nth("23", 3, i - 1, 1))
                both(lambda p: v.tensor_tensor(a[p], acc[:, 0, nodes(p)], nb("xt2", p), ALU.mult))
                dve.wait_ge(res_done, nth("3", 3, i, 1))
                both(lambda p: v.tensor_tensor(a[p], a[p], bank[4 * p + 1][:, 0:GN], ALU.add))
                both(lambda p: v.tensor_scalar(a[p], a[p], bn_scale, bn_shift, ALU.mult, ALU.add))
                for p in range(2):
                    v.tensor_scalar(nb("tmp", p), a[p], 0.0, None, ALU.min).then_inc(elu_arg, 1)
                dve.wait_ge(elu_exp, nth("3", 3, i, 1))
                both(lambda p: v.scalar_tensor_tensor(a[p], a[p], 0.0, nb("at2", p), ALU.max, ALU.add))
                for p in range(2):
                    v.tensor_scalar(a[p], a[p], -1.0, None, ALU.add).then_inc(attn_ready, 1)
                dve.wait_ge(attn_turned, nth("23", 3, i, 1))
                both(lambda p: v.tensor_tensor(nb("h", p), bank[4 * p + 2][:, 0:GN], nb("x", p), ALU.add))
                layer_norm("h", "new", 3 * GROUPS + 2 * i + 1, x_new, stored(3, i))

            regs0 = [dve.alloc_register(f"first_{m}") for m in range(SB)]

            def restart_carry(n):
                dve.wait_ge(zeroed, n)
                steps["base"], steps["n"] = steps["total"], 0
                ordered(v.memset(cin[:, 1, :], BIG))
                steps["total"] += 1

            stepped_loop("nodes0", nodes0, GPAIRS, True)
            restart_carry(1)
            stepped_loop("edges0", edges0, PAIRS, False)
            dve.wait_ge(acc_done, NT + ACC_CREDIT)
            stepped_loop("nodes1", nodes1, GPAIRS, True)
            restart_carry(2)
            edge_onehots(CH * 1, 0, 0, range(TC))
            stepped_loop("edges1", edges_gat(1, regs0), PAIRS, False, peel_last=True)
            dve.wait_ge(acc_done, 2 * NT + ACC_CREDIT)
            stepped_loop("nodes2", nodes2, GPAIRS, True)
            restart_carry(3)
            edge_onehots(CH * 2, 0, 0, range(TC))
            stepped_loop("edges2", edges_gat(2, regs0), PAIRS, False, peel_last=True)
            dve.wait_ge(acc_done, 3 * NT + ACC_CREDIT)
            stepped_loop("nodes3", nodes3, GPAIRS, True)


_INS = ['x', 'src', 'dst', 'edge_attr_128', 'edge_attr_64', 'L0_gnn_W_e', 'L0_gnn_b_e', 'L0_gnn_a_e', 'L0_gnn_W_n',
        'L0_gnn_b_n', 'L1_gnn_W_w', 'L1_gnn_W_b', 'L1_gnn_a_w', 'L1_gnn_a_b', 'L2_gnn_u', 'L2_gnn_w1', 'L2_gnn_b1',
        'L2_gnn_w2', 'L2_gnn_b2', 'L2_gnn_w3', 'L2_gnn_b3', 'L3_gnn_W', 'L3_gnn_att_src', 'L3_gnn_att_dst',
        'L3_gnn_bias', 'L3_gnn_W_res', 'L3_gnn_bn_gamma', 'L3_gnn_bn_beta', 'L3_gnn_bn_mean', 'L3_gnn_bn_var']
_OUT = ((N, D), 'float32')


def kernel(**inputs):
    import numpy as _np
    import concourse.bacc as _bacc
    from concourse import mybir as _mybir
    from concourse.bass_utils import run_bass_kernel_spmd as _run

    nc = _bacc.Bacc("TRN2", target_bir_lowering=False, num_devices=1)
    arrays, args = {}, {}
    for name in _INS:
        a = _np.ascontiguousarray(inputs[name])
        arrays[f"in_{name}_dram"] = a
        args[name] = nc.dram_tensor(f"in_{name}_dram", a.shape, _mybir.dt.from_np(a.dtype), kind="ExternalInput").ap()
    shape, dtype = _OUT
    out = nc.dram_tensor("out_0_dram", shape, _mybir.dt.from_np(_np.dtype(dtype)), kind="ExternalOutput").ap()
    graph_kernel(nc, args, out)
    r = _run(nc, [arrays], core_ids=[0])
    return r.results[0]["out_0_dram"]
```

```python
import concourse.bass as bass
from concourse import mybir
from contextlib import ExitStack

P = 128
N = 6250
E = 106250
D = 128
H = 4
F = D // H
DU = 64
TC = 32
CH = -(-E // (P * TC))
NT = CH * TC
PAIRS = CH // 2
SB = 8
NSB = TC // SB
GN = 256
GK = GN // P
NP_ = 26 * GN
GROUPS = NP_ // GN
GPAIRS = GROUPS // 2
ZW = D + 2
KW = D + H
TW = D + 2 * H
OHT_RING, AGG_RING = 8, 4
LAG = 4
Q4 = 4
BIG = -1.0e30
EPS = 1e-5
TINY = 1e-30
LAST_FULL = (E - (CH - 1) * TC * P) // P
LAST_REST = E - (E // P) * P

EXP_CREDIT, OHT_CREDIT, SQ_CREDIT, ACC_CREDIT, AGG_CREDIT = 2 * SB, 2, 2 * SB, 2 * TC, TC

DTF_READY, STF_READY, DCOL_READY, NEXT_READY, BN_VAR, CENTRED, SETUP_DONE = 1, 2, 7, 8, 16, 22, 94
N_WEIGHTS = 33

NODE_BUFFERS = {"x": 0, "xt": 256, "xt2": 512, "at": 768, "at2": 1024, "tmp": 1280, "h": 1536, "new": 1792,
                "newt": 2048, "tab": 2304, "h1": 2824, "h2": 3336, "small": 3848}

STEPS = {"edges0": 102, "edges1": 36, "edges2": 32, "nodes0": 0, "nodes1": 24, "nodes2": 18, "nodes3": 18}


def graph_kernel(nc, t, out):
    nc.disable_value_cache = True
    f32, i32, bf16 = mybir.dt.float32, mybir.dt.int32, mybir.dt.bfloat16
    ALU, ACT, AX = mybir.AluOpType, mybir.ActivationFunctionType, mybir.AxisListType
    ctx = ExitStack()
    with ctx:
        def sb(name, shape, dt=f32):
            return ctx.enter_context(nc.sbuf_tensor(name, shape, dt))

        def sem(name):
            return ctx.enter_context(nc.semaphore(name))

        def dram(name, shape, dt=f32):
            return nc.dram_tensor(name, shape, dt, kind="Internal").ap()

        x_pad = dram("x_pad", [NP_, D])
        x1_pad = dram("x1_pad", [NP_, D])
        x3_pad = dram("x3_pad", [NP_, D])
        src_tab = [dram("src_tab0", [NP_, ZW]), dram("src_tab1", [NP_, KW]), dram("src_tab3", [NP_, KW])]
        dst_tab = [dram("dst_tab0", [NP_, ZW]), dram("dst_tab1", [NP_, H]), dram("dst_tab3", [NP_, H])]

        acc = sb("acc", [P, 2, NP_])
        pen_f = sb("pen_f", [P, CH, P], bf16)
        pen_r = sb("pen_r", [P, CH, P], bf16)
        pen_first = sb("pen_first", [P, CH, P], bf16)
        pen_last = sb("pen_last", [P, CH, P], bf16)
        pen_join = sb("pen_join", [P, NT + 1], bf16)
        carry_f = sb("carry_f", [P, NT + 1], bf16)
        carry_r = sb("carry_r", [P, CH, TC], bf16)
        rel = sb("rel", [P, NT])
        times = sb("times", [P, NT], bf16)
        src_i = sb("src_i", [P, NT], mybir.dt.uint16)
        first_i = sb("first_i", [1, NT], i32)
        idx = sb("idx", [P, 2, TC], i32)
        gall = sb("gall", [P, 2 * TC * KW])
        ze = sb("ze", [P, TC, ZW])
        s_oh = sb("s_oh", [P, TC, P])
        efr = sb("efr", [P, 2, SB, D])
        oht = sb("oht", [P, OHT_RING, P])
        eft = sb("eft", [P, 2, 4 * P])
        win = sb("win", [P, 2, SB, ZW])
        lg = sb("lg", [P, P])
        lg2 = sb("lg2", [P, P])
        mx = sb("mx", [P, P])
        mx2 = sb("mx2", [P, P])
        ext = sb("ext", [P, P])
        ex = sb("ex", [P, P])
        blk = sb("blk", [P, 8, 32])
        cin = sb("cin", [P, 2, 33])
        att = sb("att", [P, 8, TC])
        fac = sb("fac", [P, 2])
        junk = sb("junk", [P, 2, P])
        ident = sb("ident", [P, P])
        sel = sb("sel", [P, P])
        iota_row = sb("iota_row", [P, P])
        col_i = sb("col_i", [P, 2], i32)
        cols = sb("cols", [P, 8])
        w_sd = sb("w_sd", [P, 2 * ZW])
        w_ef = sb("w_ef", [P, ZW])
        w_n = sb("w_n", [P, 2, ZW])
        w_t = sb("w_t", [P, 2, TW])
        b_t = sb("b_t", [P, 2, TW])
        w1 = sb("w1", [P, 2, 256])
        w1u = sb("w1u", [DU, 256])
        w2 = sb("w2", [P, 2, 256])
        w3 = sb("w3", [P, 2, D])
        w_res = sb("w_res", [P, D])
        rows = sb("rows", [P, 4, D])
        vec = sb("vec", [P, 16])
        be, ae, bn_row, b3_row = (rows[:, k, :] for k in range(4))
        eps, den_mask, attr_mask, one_c, iota_c = (cols[:, k:k + 1] for k in range(5))
        b1_c, b2_c, bn_scale, bn_shift = vec[:, 0:2], vec[:, 2:4], vec[:, 4:5], vec[:, 5:6]
        bn_raw = vec[:, 6:11]

        def g(q, j, width=KW):
            return gall[:, (q * TC + j) * KW:(q * TC + j) * KW + width]

        def gq(q):
            return gall[:, q * TC * KW:(q + 1) * TC * KW].rearrange("p (j d) -> p j d", d=KW)

        def nb(name, p, width=GN):
            at = p * TC * KW + NODE_BUFFERS[name]
            return gall[:, at:at + width]

        bank = [ctx.enter_context(nc.psum_tensor(f"bank{k}", [P, 512], f32)) for k in range(2)]
        zb = ctx.enter_context(nc.psum_tensor("zb", [P, 2, 512], f32))
        bank += [zb[:, 0, :], zb[:, 1, :]]
        bank += [ctx.enter_context(nc.psum_tensor(f"bank{k}", [P, 512], f32)) for k in range(4, 8)]

        def agg_ps(slot):
            return bank[(0, 1, 4, 5)[slot]][:, 0:2 * P]

        efb = bank[4:6]
        lt_ps, ex_ps = bank[6][:, 0:P], bank[7][:, 0:P]
        ohb = bank[6:8]

        weights_in = sem("weights_in")
        edges_in = sem("edges_in")
        consts = sem("consts")
        padded = sem("padded")
        w1_zero = sem("w1_zero")
        bn_std = sem("bn_std")
        setup_dve = sem("setup_dve")
        setup_pe = sem("setup_pe")
        pads_out = sem("pads_out")
        chain = sem("chain")
        win_in = [sem(f"win_in{k}") for k in range(NSB)]
        ef_in = [sem(f"ef_in{k}") for k in range(2)]
        gather_in = [[sem(f"gather_in{q}{k}") for k in range(NSB)] for q in range(2)]
        idx_ready = sem("idx_ready")
        s_ready = sem("s_ready")
        oh_turned = sem("oh_turned")
        oht_ready = sem("oht_ready")
        expanded = sem("expanded")
        agg_done = sem("agg_done")
        acc_done = sem("acc_done")
        ef_turned = sem("ef_turned")
        eft_copied = sem("eft_copied")
        squared = sem("squared")
        z_copied = sem("z_copied")
        var_ready = sem("var_ready")
        std_ready = sem("std_ready")
        logits_ready = sem("logits_ready")
        logits_turned = sem("logits_turned")
        shifted = sem("shifted")
        weights_t = sem("weights_t")
        weights_turned = sem("weights_turned")
        ex_ready = sem("ex_ready")
        fac_arg = sem("fac_arg")
        fac_ready = sem("fac_ready")
        values_weighted = sem("values_weighted")
        rest_weighted = sem("rest_weighted")
        attr_copied = sem("attr_copied")
        den_cols = sem("den_cols")
        host = sem("host")
        x_in = [sem(f"x_in{p}") for p in range(2)]
        x_turned = sem("x_turned")
        x_copied = sem("x_copied")
        x_squared = sem("x_squared")
        den_picked = sem("den_picked")
        attn_ready = sem("attn_ready")
        attn_squared = sem("attn_squared")
        attn_turned = sem("attn_turned")
        norm_done = sem("norm_done")
        norm_var = sem("norm_var")
        norm_std = sem("norm_std")
        ln_var = sem("ln_var")
        ln_std = sem("ln_std")
        mid_ready = sem("mid_ready")
        mid_turned = sem("mid_turned")
        mid_copied = sem("mid_copied")
        h_done = sem("h_done")
        h_biased = sem("h_biased")
        h_ready = sem("h_ready")
        h3_done = sem("h3_done")
        x_new = sem("x_new")
        new_turned = sem("new_turned")
        new_copied = sem("new_copied")
        tab_done = sem("tab_done")
        tab_copied = sem("tab_copied")
        tab_out = [sem(f"tab_out{p}") for p in range(2)]
        rows_out = [sem(f"rows_out{p}") for p in range(2)]
        res_done = sem("res_done")
        elu_arg = sem("elu_arg")
        elu_exp = sem("elu_exp")
        zeroed = sem("zeroed")

        dti = gall[:, 0:CH * P].bitcast(i32).rearrange("p (c e) -> p c e", e=P)
        dtf = gall[:, CH * P:2 * CH * P].rearrange("p (c e) -> p c e", e=P)
        sti = ze[:, :, :].rearrange("p a b -> p (a b)")[0:TC, 0:CH * P].bitcast(i32).rearrange("p (c e) -> p c e", e=P)
        stf = acc[0:TC, 0, 0:CH * P].rearrange("p (c e) -> p c e", e=P)
        dcol = acc[:, 1, 0:NT]
        first_b = acc[:, 1, NT:2 * NT]
        last_b = acc[:, 1, 2 * NT:3 * NT]
        diff = acc[:, 0, 3400:3400 + CH * P // 2]
        pen_single = acc[:, 1, 3 * NT:4 * NT]
        pick = acc[:, 1, 4 * NT:4 * NT + 2 * P].rearrange("p (k m) -> p k m", k=2)
        iota_i = acc[:, 0, 5100:5100 + P].bitcast(i32)
        pen_join_f = acc[:, 1, 5 * NT:6 * NT + 1]
        tile_tmp = acc[:, 1, 6 * NT + 8:7 * NT + 8]
        zeros = s_oh[:, 0:8, :].rearrange("p a b -> p (a b)")
        we_raw = efr[:, 0, 0:3, :].rearrange("p a b -> p (a b)")
        wn_raw = efr[:, 0, 3:5, :].rearrange("p a b -> p (a b)")
        a_raw = efr[:, 1, 0:4, :]
        prod = efr[:, 1, 4:6, :]
        ab_raw = efr[:, 1, 7, 0:H]
        u_col = efr[0:DU, 0, 5, 0:1]
        rsum = att[:, 0, 0:8]

        block = ctx.enter_context(nc.Block())


        def nth(counted_in, phase, i, p):
            return counted_in.index(str(phase)) * GROUPS + 2 * i + p + 1

        def started(i):
            return not (isinstance(i, int) and i == 0)

        def group_pairs(engine, body, peel_last=False):
            body(0)
            with engine.Fori(1, GPAIRS - int(peel_last)) as i:
                body(i)
            if peel_last:
                body(GPAIRS - 1)

        def more(i):
            return not (isinstance(i, int) and i == GPAIRS - 1)

        def group_rows(tab, i, p):
            return tab[bass.ds((2 * i + p) * GN, GN), :].rearrange("(k n) d -> n k d", n=P)

        def following(i, q, k, last):
            if q == 0:
                return 2 * i + (1 + CH * k), i, 1
            return None if last else (2 * i + (2 + CH * k), i + 1, 0)

        def window(k, s, m):
            if k == 0:
                return win[:, s % 2, m, :]
            return win[:, s % 2, m, (s // 2) * H:(s // 2) * H + H]

        def tiles(ap):
            return ap.rearrange("p (k d) -> p k d", k=GK)

        @block.sync
        def _(sp):
            def tile_rows(a, tile0, n):
                return a[tile0 * P:(tile0 + n) * P].rearrange("(t e) -> t e", e=P)

            def raw_indices(into, a, r0, skip=0):
                a = a[skip:E]
                sp.dma_start(into[r0:r0 + TC, 0:CH - 1, :],
                             tile_rows(a, 0, (CH - 1) * TC).rearrange("(c j) e -> j c e", j=TC)).then_inc(edges_in, 16)
                sp.dma_start(into[r0:r0 + LAST_FULL, CH - 1, :],
                             tile_rows(a, (CH - 1) * TC, LAST_FULL)).then_inc(edges_in, 16)
                sp.dma_start(into[r0 + LAST_FULL:r0 + LAST_FULL + 1, CH - 1, 0:LAST_REST - skip],
                             a[E - LAST_REST:E - skip].unsqueeze(0)).then_inc(edges_in, 16)

            sp.wait_ge(padded, 2)
            for h in range(H):
                raw_indices(dti, t["dst"], TC * h)
            raw_indices(sti, t["src"], 0)

            def load_weight(into, a):
                sp.dma_start(into, a).then_inc(weights_in, 16)

            load_weight(we_raw, t["L0_gnn_W_e"])
            load_weight(wn_raw, t["L0_gnn_W_n"])
            load_weight(be, t["L0_gnn_b_e"].partition_broadcast(P))
            load_weight(ae, t["L0_gnn_a_e"].partition_broadcast(P))
            load_weight(bn_row, t["L0_gnn_b_n"].partition_broadcast(P))
            load_weight(b3_row, t["L2_gnn_b3"].partition_broadcast(P))
            load_weight(w_t[:, 0, 0:D], t["L1_gnn_W_w"])
            load_weight(w_t[:, 1, 0:D], t["L3_gnn_W"])
            for k, a in enumerate((t["L1_gnn_a_w"][:, F:2 * F], t["L1_gnn_a_w"][:, 0:F],
                                   t["L3_gnn_att_src"], t["L3_gnn_att_dst"])):
                load_weight(a_raw[:, k, :].rearrange("p (h f) -> p h f", h=H), a.partition_broadcast(P))
            load_weight(b_t[:, 0, 0:D], t["L1_gnn_W_b"].partition_broadcast(P))
            load_weight(ab_raw, t["L1_gnn_a_b"].partition_broadcast(P))
            load_weight(w1[:, 0, :], t["L2_gnn_w1"][0:D, :])
            sp.wait_ge(w1_zero, 1)
            for h in range(H):
                load_weight(w1[F * h + F // 2:F * h + F, 1, :], t["L2_gnn_w1"][D + F // 2 * h:D + F // 2 * (h + 1), :])
            load_weight(w1u[:, :], t["L2_gnn_w1"][D + DU:D + 2 * DU, :])
            load_weight(u_col, t["L2_gnn_u"][0, :].unsqueeze(1))
            load_weight(w2[:, :, :], t["L2_gnn_w2"].rearrange("(k p) n -> p k n", p=P))
            load_weight(w3[:, :, :], t["L2_gnn_w3"].rearrange("(k p) n -> p k n", p=P))
            load_weight(w_res[:, :], t["L3_gnn_W_res"])
            for k in range(2):
                load_weight(b1_c[:, k:k + 1], t["L2_gnn_b1"][k * P:k * P + P].unsqueeze(1))
                load_weight(b2_c[:, k:k + 1], t["L2_gnn_b2"][k * P:k * P + P].unsqueeze(1))
            for k, name in enumerate(("bias", "bn_mean", "bn_var", "bn_gamma", "bn_beta")):
                load_weight(bn_raw[:, k:k + 1], t["L3_gnn_" + name].unsqueeze(1))

            sp.wait_ge(padded, 4)
            raw_indices(sti, t["dst"], 0, skip=1)

            sp.dma_start(x_pad[0:N, :], t["x"]).then_inc(pads_out, 16)
            sp.wait_ge(padded, 3)
            rest = (NP_ - N) // 7
            sp.dma_start(x_pad[N:NP_, :].rearrange("(p r) d -> p (r d)", r=7), zeros[0:rest, 0:7 * D]).then_inc(pads_out, 16)
            sp.wait_ge(pads_out, 32)

            def node_io(phase, x_from, store, x_free):
                def body(i):
                    for p in range(2):
                        if started(i):
                            x_free(i - 1, p)
                        sp.dma_start(tiles(nb("x", p)), group_rows(x_from, i, p)).then_inc(x_in[p], 16)
                        if started(i):
                            store(i - 1, p)
                group_pairs(sp, body)
                for p in range(2):
                    x_free(GPAIRS - 1, p)
                    store(GPAIRS - 1, p)

            def store_tables(layer, i, p, w0, w1_):
                tab = nb("tab", p, GK * (w0 + w1_)).rearrange("p (k w) -> p k w", k=GK)
                sp.dma_start(group_rows(src_tab[layer], i, p), tab[:, :, 0:w0]).then_inc(tab_out[p], 16)
                sp.dma_start(group_rows(dst_tab[layer], i, p), tab[:, :, w0:w0 + w1_]).then_inc(tab_out[p], 16)

            def store0(i, p):
                sp.wait_ge(tab_copied, nth("012", 0, i, p))
                store_tables(0, i, p, ZW, ZW)

            def free0(i, p):
                sp.wait_ge(x_turned, nth("013", 0, i, p))
                sp.wait_ge(x_squared, nth("01", 0, i, p))

            def store_gat(phase, x_to):
                def store(i, p):
                    sp.dma_start(group_rows(x_to, i, p), tiles(nb("new", p))).then_inc(tab_out[p], 16)
                    sp.wait_ge(tab_copied, nth("012", phase, i, p))
                    store_tables(phase, i, p, KW, H)
                return store

            def free_new(phase):
                return lambda i, p: sp.wait_ge(x_new, nth("123", phase, i, p))

            def edge_io(k, attr, width):
                regs = [sp.alloc_register(f"sp_first{k}_{m}") for m in range(SB)]

                def body(i, last=False):
                    for q in range(2):
                        for s in range(NSB):
                            u = 2 * NSB * i + (NSB * q + s + NSB * CH * k)
                            tile0 = 2 * TC * i + (q * TC + s * SB)
                            if k == 0:
                                edge_features(i, q, s, u, tile0, last)
                            sp.wait_ge(expanded, u * SB + (EXP_CREDIT - (SB if k == 0 else 3 * SB)))
                            sp.load(regs, first_i[0:1, bass.ds(tile0, SB)])
                            for m in range(SB):
                                v = sp.snap(regs[m], min_val=0, max_val=N)
                                sp.dma_start(window(k, s, m), dst_tab[k][bass.ds(v, P), :]).then_inc(win_in[s], 16)
                            if k == 1:
                                edge_features(i, q, s, u, tile0, last)

                def edge_features(i, q, s, u, tile0, last):
                    if k == 0:
                        sp.wait_ge(squared, u * SB + (SQ_CREDIT - SB))
                    else:
                        sp.wait_ge(attr_copied, 2 * NSB * i + (NSB * q + s) + 1)
                    full = max(0, min(SB, LAST_FULL - s * SB)) if last and q == 1 else SB
                    for lo, hi in ((0, 6), (6, SB)):
                        if full >= hi:
                            sp.dma_start(efr[:, s % 2, lo:hi, 0:width],
                                         attr[bass.ds(tile0 * P + lo * P, (hi - lo) * P), :]
                                         .rearrange("(j p) d -> p j d", p=P)).then_inc(ef_in[s % 2], 16)
                        else:
                            assert lo == full
                            sp.dma_start(efr[0:LAST_REST, s % 2, lo, 0:width],
                                         attr[E - LAST_REST:E, :]).then_inc(ef_in[s % 2], 16)
                with sp.Fori(0, PAIRS - 1) as i:
                    body(i)
                body(PAIRS - 1, last=True)

            sp.wait_ge(setup_dve, SETUP_DONE)
            node_io(0, x_pad, store0, free0)
            for p in range(2):
                sp.wait_ge(tab_out[p], 32 * GPAIRS)
            edge_io(0, t["edge_attr_128"], D)
            sp.wait_ge(acc_done, NT + ACC_CREDIT)
            node_io(1, x_pad, store_gat(1, x1_pad), free_new(1))
            for p in range(2):
                sp.wait_ge(tab_out[p], (32 + 48) * GPAIRS)
            edge_io(1, t["edge_attr_64"], DU)
            sp.wait_ge(acc_done, 2 * NT + ACC_CREDIT)
            node_io(2, x1_pad, store_gat(2, x3_pad), free_new(2))
            for p in range(2):
                sp.wait_ge(tab_out[p], (32 + 96) * GPAIRS)
            edge_io(2, None, 0)
            sp.wait_ge(acc_done, 3 * NT + ACC_CREDIT)

            def store_out(i, p):
                here = GN if not isinstance(i, int) else min(GN, N - (2 * i + p) * GN)
                if here == GN:
                    sp.dma_start(group_rows(out, i, p), tiles(nb("new", p))).then_inc(rows_out[p], 16)
                elif here > 0:
                    assert here <= P
                    sp.dma_start(out[N - here:N, :], nb("new", p)[0:here, 0:D]).then_inc(rows_out[p], 16)

            node_io(3, x3_pad, store_out, free_new(3))
            for p in range(2):
                stored = GPAIRS - 1 + (N > (GROUPS - 2 + p) * GN)
                sp.wait_ge(rows_out[p], 16 * stored)

        @block.gpsimd
        def _(pool):
            pool.memset(dti[:, :, :], N).then_inc(padded, 1)
            pool.memset(sti[:, :, :], 0).then_inc(padded, 1)
            pool.memset(zeros, 0.0).then_inc(padded, 1)
            pool.memset(ident[:, :], 0.0).then_inc(consts, 1)
            pool.memset(sel[:, :], 0.0).then_inc(consts, 1)
            pool.memset(w1[:, 1, :], 0.0).then_inc(w1_zero, 1)
            pool.memset(pick, 0.0).then_inc(consts, 1)
            pool.wait_ge(setup_dve, STF_READY)
            pool.memset(sti[:, :, :], N).then_inc(padded, 1)
            pool.iota(iota_i, [[1, P]], 0, 0).then_inc(consts, 1)
            pool.iota(col_i[:, :], [[0, 2]], 0, 1).then_inc(consts, 1)
            pool.wait_ge(consts, 5)
            pool.affine_select(out=ident[:, :], in_=ident[:, :], compare_op=ALU.not_equal, fill=1.0,
                               base=0, pattern=[[-1, P]], channel_multiplier=1).then_inc(consts, 1)
            s4 = sel[:, :].rearrange("p (h f) -> p h f", h=H)
            pool.affine_select(out=s4, in_=s4, compare_op=ALU.not_equal, fill=1.0,
                               base=0, pattern=[[-F, H], [0, F]], channel_multiplier=1).then_inc(consts, 1)
            pool.affine_select(out=pick, in_=pick, compare_op=ALU.not_equal, fill=1.0,
                               base=0, pattern=[[-(P - 1), 2], [0, P]], channel_multiplier=1).then_inc(consts, 1)

            def gathers(k):
                width = ZW if k == 0 else KW

                def body(i):
                    for q in range(2):
                        gc = 2 * i + (q + CH * k)
                        pool.wait_ge(acc_done, gc * TC + (ACC_CREDIT - TC))
                        pool.sem_inc(host, 1)
                        pool.tensor_copy(idx[:, q, :], src_i[:, bass.ds(2 * TC * i + q * TC, TC)]).then_inc(idx_ready, 1)
                        pool.wait_ge(idx_ready, gc + 1)
                        pool.sem_inc(host, 1)
                        for j in range(TC):
                            pool.indirect_dma_start(g(q, j, width), None, src_tab[k],
                                                    bass.IndirectOffsetOnAxis(idx[:, q, j:j + 1], 0)
                                                    ).then_inc(gather_in[q][j // SB], 16)
                with pool.Fori(0, PAIRS) as i:
                    body(i)

            def clear_acc(n):
                pool.memset(acc[:, :, :], 0.0).then_inc(zeroed, 1)

            pool.wait_ge(setup_dve, SETUP_DONE)
            clear_acc(1)
            for p in range(2):
                pool.wait_ge(tab_out[p], 32 * GPAIRS)
            gathers(0)
            pool.wait_ge(norm_done, nth("1", 1, GPAIRS - 1, 1))
            clear_acc(2)
            for p in range(2):
                pool.wait_ge(tab_out[p], (32 + 48) * GPAIRS)
            gathers(1)
            pool.wait_ge(h_ready, 2 * GROUPS)
            clear_acc(3)
            for p in range(2):
                pool.wait_ge(tab_out[p], (32 + 96) * GPAIRS)
            gathers(2)

        @block.scalar
        def _(act):
            act.sem_inc(eft_copied, 2)
            act.sem_inc(oht_ready, OHT_CREDIT)
            act.sem_inc(z_copied, 1)
            act.sem_inc(squared, SQ_CREDIT)
            act.sem_inc(attr_copied, 2)
            act.wait_ge(setup_dve, BN_VAR)
            nc.scalar.activation(vec[:, 11:12], bn_raw[:, 2:3], ACT.Sqrt, bias=eps).then_inc(bn_std, 1)

            def nodes0(i):
                for p in range(2):
                    act.wait_ge(x_turned, nth("013", 0, i, p))
                    if started(i):
                        act.wait_ge(tab_done, nth("012", 0, i - 1, p))
                    nc.scalar.activation(nb("xt", p), bank[4 * p][:, 0:GN], ACT.Copy).then_inc(x_copied, 1)
                    if started(i):
                        act.wait_ge(tab_copied, nth("012", 0, i - 1, p))
                    for kk in range(GK):
                        ins = nc.scalar.activation(nb("xt2", p)[:, kk * P:kk * P + P], nb("x", p)[:, kk * P:kk * P + P],
                                                   ACT.Square, accum_out=nb("small", p, 2)[:, kk:kk + 1])
                    ins.then_inc(x_squared, 1)

            def chunk_tail(gc):
                act.wait_ge(shifted, gc + 1)
                nc.scalar.activation(ext[:, :], lg[:, :], ACT.Exp).then_inc(weights_t, 1)
                act.wait_ge(fac_arg, gc + 1)
                nc.scalar.activation(fac[:, 0:1], blk[:, 0, 0:1], ACT.Exp).then_inc(fac_ready, 1)

            def copy_onehots(gc, g4):
                act.wait_ge(oh_turned, gc * (TC // Q4) + g4 + 1)
                act.wait_ge(expanded, gc * TC + (Q4 * g4 + EXP_CREDIT - Q4))
                nc.scalar.activation(oht[:, Q4 * (g4 % 2):Q4 * (g4 % 2) + Q4, :].rearrange("p a b -> p (a b)"),
                                     ohb[g4 % 2][:, :], ACT.Copy).then_inc(oht_ready, 1)

            def edges0(i):
                for q in range(2):
                    gc = 2 * i + q
                    act.wait_ge(acc_done, gc * TC + ACC_CREDIT)

                    def copy_turned(g4):
                        gg = 2 * 8 * i + (q * 8 + g4)
                        act.wait_ge(ef_turned, gg + 1)
                        act.wait_ge(expanded, 4 * gg + (EXP_CREDIT - 4))
                        nc.scalar.activation(eft[:, g4 % 2, :], efb[g4 % 2][:, :], ACT.Copy).then_inc(eft_copied, 1)

                    def root(s):
                        act.wait_ge(var_ready, gc * NSB + s + 1)
                        nc.scalar.activation(att[:, 3, s * SB:s * SB + SB], att[:, 2, s * SB:s * SB + SB], ACT.Sqrt,
                                             bias=eps).then_inc(std_ready, 1)

                    copy_turned(0)
                    copy_onehots(gc, 0)
                    for g4 in range(8):
                        if g4 + 1 < 8:
                            copy_turned(g4 + 1)
                            copy_onehots(gc, g4 + 1)
                        gg = 2 * 8 * i + (q * 8 + g4)
                        act.wait_ge(ef_in[(g4 // 2) % 2], 128 * i + (64 * q + 32 * (g4 // 4) + 32))
                        for m in range(4):
                            j = 4 * g4 + m
                            tt = 2 * TC * i + (q * TC + j)
                            act.wait_ge(squared, tt + (SQ_CREDIT - 1))
                            nc.scalar.activation(junk[:, m % 2, :], efr[:, (g4 // 2) % 2, j % SB, :], ACT.Square,
                                                 accum_out=att[:, 0, j:j + 1]).then_inc(squared, 1)
                        if g4 in (2, 4, 6):
                            root(g4 // 2 - 1)
                        act.wait_ge(expanded, 4 * gg + 4 + EXP_CREDIT)
                        nc.scalar.activation(ze[:, 4 * g4:4 * g4 + 4, :].rearrange("p (a b) d -> p a b d", a=2),
                                             zb[:, :, 0:2 * ZW].rearrange("p a (b d) -> p a b d", b=2),
                                             ACT.Copy).then_inc(z_copied, 1)
                    root(NSB - 1)
                    chunk_tail(gc)
                    act.wait_ge(ex_ready, gc + 1)
                    for j in range(SB, TC):
                        ins = nc.scalar.activation(ze[:, j, 0:D], ze[:, j, 0:D], ACT.Copy, scale=ex[:, j:j + 1])
                        if j % SB == SB - 1:
                            ins.then_inc(rest_weighted, 1)

            def prepare(k, gc, i, q):
                for s in range(NSB):
                    copy_onehots(gc, 2 * s)
                    copy_onehots(gc, 2 * s + 1)
                    if k == 1:
                        act.wait_ge(acc_done, gc * TC + (ACC_CREDIT - TC + s * SB + SB))
                        act.wait_ge(ef_in[s % 2], 128 * i + (64 * q + 32 * (s // 2) + 32) + 64 * CH)
                        nc.scalar.activation(
                            ze[:, s * SB:s * SB + SB, 0:D].rearrange("p j (h x) -> p j h x", h=H)[:, :, :, F // 2:F],
                            efr[:, s % 2, :, 0:DU].rearrange("p j (h x) -> p j h x", h=H), ACT.Copy).then_inc(attr_copied, 1)

            def edges_gat(k):
                def edges(i, last=False):
                    for q in range(2):
                        gc = 2 * i + (q + CH * k)
                        chunk_tail(gc)
                        act.wait_ge(ex_ready, gc + 1)
                        act.wait_ge(acc_done, gc * TC + ACC_CREDIT)
                        filled = F // 2 if k == 1 else F
                        nc.scalar.activation(
                            ze[:, :, 0:D].rearrange("p j (h x) -> p j h x", h=H)[:, :, :, 0:filled],
                            ex[:, :].rearrange("p (h j) -> p j h", h=H).unsqueeze(3).to_broadcast([P, TC, H, filled]),
                            ACT.Copy).then_inc(den_cols, 1)
                        for j in range(TC - SB, TC):
                            for h in range(H):
                                vals = g(q, j, D)[:, F * h:F * h + F]
                                ins = nc.scalar.activation(vals, vals, ACT.Copy, scale=ex[:, TC * h + j:TC * h + j + 1])
                        ins.then_inc(rest_weighted, 1)
                        next_chunk = following(i, q, k, last)
                        if next_chunk is not None:
                            prepare(k, *next_chunk)
                return edges

            def sqrt_step(wait_on, count, out_ap, in_ap, scale, done):
                act.wait_ge(wait_on, count)
                nc.scalar.activation(out_ap, in_ap, ACT.Sqrt, bias=eps, scale=scale).then_inc(done, 1)

            def ln_columns(p):
                sm = nb("small", p, 40)
                return sm[:, 28:30], sm[:, 24:28].rearrange("p (k s) -> p k s", k=GK)[:, :, 1]

            def turn_new(phase, i, p, bank_ap):
                act.wait_ge(new_turned, nth("12", phase, i, p))
                if started(i):
                    act.wait_ge(tab_done, nth("012", phase, i - 1, p))
                nc.scalar.activation(nb("newt", p), bank_ap, ACT.Copy).then_inc(new_copied, 1)

            def nodes1(i):
                for p in range(2):
                    act.wait_ge(x_turned, nth("013", 1, i, p))
                    if started(i):
                        act.wait_ge(norm_done, nth("1", 1, i - 1, p))
                    nc.scalar.activation(nb("xt", p), bank[4 * p][:, 0:GN], ACT.Copy).then_inc(x_copied, 1)
                    nc.scalar.activation(nb("xt2", p), bank[4 * p][:, 0:GN], ACT.Square).then_inc(x_squared, 1)
                for p in range(2):
                    act.wait_ge(attn_ready, nth("123", 1, i, p))
                    nc.scalar.activation(nb("at2", p), nb("at", p), ACT.Square).then_inc(attn_squared, 1)
                for p in range(2):
                    sm = nb("small", p, 40)
                    sqrt_step(norm_var, nth("1", 1, i, p), sm[:, 6:8], sm[:, 4:6], 1.0, norm_std)
                for p in range(2):
                    sqrt_step(ln_var, nth("1", 1, i, p), *ln_columns(p), 1.0, ln_std)
                for p in range(2):
                    turn_new(1, i, p, bank[4 * p + 2][:, 0:GN])

            def nodes2(i):
                for p in range(2):
                    sqrt_step(ln_var, GROUPS + 4 * i + p + 1, *ln_columns(p), 1.0, ln_std)
                for p in range(2):
                    act.wait_ge(mid_turned, 2 * i + p + 1)
                    if started(i):
                        act.wait_ge(h_done, 4 * i - 4 + p + 1)
                    nc.scalar.activation(nb("xt", p), bank[4 * p + 1][:, 0:GN], ACT.Copy).then_inc(mid_copied, 1)
                for layer, (buf, bias) in enumerate((("h1", b1_c), ("h2", b2_c))):
                    for p in range(2):
                        act.wait_ge(h_done, 4 * i + (2 * layer + p + 1))
                        if started(i):
                            act.wait_ge(h3_done, 2 * i + p - 1)
                        for o in range(2):
                            ins = nc.scalar.activation(nb(buf, p, 2 * GN)[:, o * GN:o * GN + GN],
                                                       bank[4 * p + 2 + layer][:, o * GN:o * GN + GN],
                                                       ACT.Identity, bias=bias[:, o:o + 1])
                        ins.then_inc(h_biased, 1)
                for p in range(2):
                    sqrt_step(ln_var, GROUPS + 4 * i + p + 3, *ln_columns(p), 1.0, ln_std)
                for p in range(2):
                    turn_new(2, i, p, bank[4 * p + 1][:, GN:2 * GN])

            def nodes3(i):
                for p in range(2):
                    act.wait_ge(x_turned, nth("013", 3, i, p))
                    if started(i):
                        act.wait_ge(res_done, nth("3", 3, i - 1, p))
                    nc.scalar.activation(nb("xt", p), bank[4 * p][:, 0:GN], ACT.Copy).then_inc(x_copied, 1)
                for p in range(2):
                    act.wait_ge(elu_arg, nth("3", 3, i, p))
                    nc.scalar.activation(nb("at2", p), nb("tmp", p), ACT.Exp).then_inc(elu_exp, 1)
                for p in range(2):
                    sqrt_step(ln_var, 3 * GROUPS + 2 * i + p + 1, *ln_columns(p), 1.0, ln_std)

            group_pairs(act, nodes0)
            with act.Fori(0, PAIRS) as i:
                edges0(i)
            group_pairs(act, nodes1)
            prepare(1, CH * 1, 0, 0)
            with act.Fori(0, PAIRS - 1) as i:
                edges_gat(1)(i)
            edges_gat(1)(PAIRS - 1, last=True)
            group_pairs(act, nodes2)
            prepare(2, CH * 2, 0, 0)
            with act.Fori(0, PAIRS - 1) as i:
                edges_gat(2)(i)
            edges_gat(2)(PAIRS - 1, last=True)
            group_pairs(act, nodes3)

        @block.tensor
        def _(pe):
            mm = nc.tensor.matmul
            pe.sem_inc(expanded, EXP_CREDIT)
            pe.sem_inc(agg_done, AGG_CREDIT)

            pe.wait_ge(consts, 8)
            pe.wait_ge(setup_dve, DTF_READY)
            for c in range(CH):
                ins = nc.tensor.transpose(bank[c // 16][:, TC * (c % 16):TC * (c % 16) + TC], dtf[0:TC, c, :], ident[0:TC, 0:TC])
            ins.then_inc(setup_pe, 1)
            pe.wait_ge(setup_dve, STF_READY)
            for c in range(CH):
                ins = nc.tensor.transpose(zb[:, c // 16, TC * (c % 16):TC * (c % 16) + TC], stf[:, c, :], ident[0:TC, 0:TC])
            ins.then_inc(setup_pe, 1)
            pe.wait_ge(setup_dve, DCOL_READY)
            for k in range(2):
                for n in range(2):
                    lo, hi = 512 * n, min(512 * n + 512, NT)
                    ins = mm(bank[4 + 2 * k + n][:, 0:hi - lo], pick[:, k, :], dcol[:, lo:hi], start=True, stop=True)
            ins.then_inc(setup_pe, 1)
            pe.wait_ge(setup_dve, NEXT_READY)
            for c in range(CH):
                ins = nc.tensor.transpose(zb[:, c // 16, TC * (c % 16):TC * (c % 16) + TC], stf[:, c, :], ident[0:TC, 0:TC])
            ins.then_inc(setup_pe, 1)
            pe.wait_ge(setup_dve, CENTRED)
            for k in range(3):
                nc.tensor.transpose(bank[0][:, k * P:k * P + P], we_raw[:, k * P:k * P + P], ident[:, :])
            for k in range(2):
                nc.tensor.transpose(bank[1][:, k * P:k * P + P], wn_raw[:, k * P:k * P + P], ident[:, :])
            for o in range(2):
                ins = mm(bank[1][:, 2 * P + o:2 * P + o + 1], w1u[:, o * P:o * P + P], u_col, start=True, stop=True)
            ins.then_inc(setup_pe, 1)
            pe.wait_ge(setup_dve, SETUP_DONE)

            def turn(src_ap, bank_ap, done):
                for kk in range(GK):
                    ins = nc.tensor.transpose(bank_ap[:, kk * P:kk * P + P], src_ap[:, kk * P:kk * P + P], ident[:, :])
                ins.then_inc(done, 1)

            def turn_x(phase, i, p):
                base = {0: 0, 1: 1, 2: 2, 3: 3}[phase] * 16 * GPAIRS
                pe.wait_ge(x_in[p], 16 * i + (base + 16))
                turn(nb("x", p), bank[4 * p][:, 0:GN], x_turned)

            def nodes0(i):
                for p in range(2):
                    if started(i):
                        pe.wait_ge(tab_copied, nth("012", 0, i - 1, p))
                    turn_x(0, i, p)
                    pe.wait_ge(x_copied, nth("013", 0, i, p))
                    for kk in range(GK):
                        ins = mm(bank[4 * p + 1 + kk][:, 0:2 * ZW], nb("xt", p)[:, kk * P:kk * P + P], w_sd[:, :],
                                 start=True, stop=True)
                    ins.then_inc(tab_done, 1)

            def turn_onehot(gc, j):
                g4, m = j // Q4, j % Q4
                pe.wait_ge(s_ready, gc * TC + (j + 1))
                if m == 0:
                    pe.wait_ge(oht_ready, gc * (TC // Q4) + (g4 + 1))
                ins = nc.tensor.transpose(ohb[g4 % 2][:, m * P:m * P + P], s_oh[:, j, :], ident[:, :])
                if m == Q4 - 1:
                    ins.then_inc(oh_turned, 1)

            def turn_onehots(gc, g4):
                for j in range(Q4 * g4, Q4 * g4 + Q4):
                    turn_onehot(gc, j)

            def onehots_copied(gc, g4):
                pe.wait_ge(oht_ready, gc * (TC // Q4) + (g4 + 1 + OHT_CREDIT))

            def expand(gc, q, g4):
                s = g4 // 2
                if g4 % 2 == 0:
                    pe.wait_ge(win_in[s], gc * 128 + 128)
                onehots_copied(gc, g4)
                for j in range(Q4 * g4, Q4 * g4 + Q4):
                    mm(bank[2 + q][:, j:j + 3 * TC + 1:TC], oht[:, j % OHT_RING, :], window(1, s, j % SB),
                       start=True, stop=True).then_inc(expanded, 1)

            def target_scores(gc, q, groups):
                for g4 in groups:
                    if g4 < TC // Q4:
                        turn_onehots(gc, g4)
                    if g4:
                        expand(gc, q, g4 - 1)

            def sum_windows(gc, weighted, vals, dens, next_chunk=None):
                for j in range(TC):
                    tt = gc * TC + j
                    if next_chunk is not None and j >= LAG:
                        turn_onehot(next_chunk[0], j - LAG)
                        if (j - LAG) % Q4 == Q4 - 1 and j - LAG >= Q4:
                            expand(next_chunk[0], next_chunk[2], (j - LAG) // Q4 - 1)
                    if j % SB == 0:
                        weighted(j // SB)
                    pe.wait_ge(acc_done, tt + (ACC_CREDIT + 1 - AGG_RING))
                    slot = agg_ps(j % AGG_RING)
                    mm(slot[:, 0:P], vals(j), s_oh[:, j, :], start=True, stop=True)
                    mm(slot[:, P:2 * P], dens(j), s_oh[:, j, :], start=True, stop=True).then_inc(agg_done, 1)
                if next_chunk is not None:
                    for j in range(TC - LAG, TC):
                        turn_onehot(next_chunk[0], j)
                    for g4 in (TC // Q4 - 2, TC // Q4 - 1):
                        expand(next_chunk[0], next_chunk[2], g4)

            def softmax_turns(gc):
                pe.wait_ge(logits_ready, gc + 1)
                nc.tensor.transpose(lt_ps, lg2[:, :], ident[:, :]).then_inc(logits_turned, 1)
                pe.wait_ge(weights_t, gc + 1)
                nc.tensor.transpose(ex_ps, ext[:, :], ident[:, :]).then_inc(weights_turned, 1)

            def edges0(i):
                for q in range(2):
                    gc = 2 * i + q
                    pe.wait_ge(acc_done, gc * TC + ACC_CREDIT)

                    def turn_edges(g4):
                        gg = 16 * i + (q * 8 + g4)
                        pe.wait_ge(ef_in[(g4 // 2) % 2], 128 * i + (64 * q + 32 * (g4 // 4) + 32))
                        pe.wait_ge(eft_copied, gg + 1)
                        for m in range(4):
                            ins = nc.tensor.transpose(efb[g4 % 2][:, m * P:m * P + P], efr[:, (g4 // 2) % 2, (4 * g4 + m) % SB, :],
                                                      ident[:, :])
                        ins.then_inc(ef_turned, 1)

                    turn_edges(0)
                    turn_onehots(gc, 0)
                    for g4 in range(8):
                        if g4 + 1 < 8:
                            turn_edges(g4 + 1)
                            turn_onehots(gc, g4 + 1)
                        gg = 16 * i + (q * 8 + g4)
                        s = g4 // 2
                        pe.wait_ge(eft_copied, gg + 1 + 2)
                        pe.wait_ge(z_copied, gg + 1)
                        if g4 % 2 == 0:
                            pe.wait_ge(gather_in[q][s], 128 * i + 128)
                            pe.wait_ge(win_in[s], gc * 128 + 128)
                        for m in range(4):
                            j = 4 * g4 + m
                            z = zb[:, m // 2, ZW * (m % 2):ZW * (m % 2) + ZW]
                            mm(z, eft[:, g4 % 2, m * P:m * P + P], w_ef[:, :], start=True, stop=False)
                            mm(z, ident[:, :], g(q, j, ZW), start=False, stop=False)
                            if m == 0:
                                onehots_copied(gc, g4)
                            mm(z, oht[:, j % OHT_RING, :], window(0, s, j % SB), start=False, stop=True).then_inc(expanded, 1)
                    softmax_turns(gc)

                    def weighted(s):
                        if s == 0:
                            pe.wait_ge(values_weighted, gc + 1)
                        else:
                            pe.wait_ge(rest_weighted, gc * (NSB - 1) + s)

                    sum_windows(gc, weighted, lambda j: ze[:, j, 0:D], lambda j: ex[:, j:j + 1].to_broadcast([P, P]))

            def edges_gat(k):
                def edges(i, last=False):
                    for q in range(2):
                        gc = 2 * i + (q + CH * k)
                        softmax_turns(gc)
                        pe.wait_ge(den_cols, gc - (CH - 1))
                        
                        def weighted(s):
                            if s < NSB - 1:
                                pe.wait_ge(values_weighted, gc * (NSB - 1) + (CH - CH * (NSB - 1) + s + 1))
                            else:
                                pe.wait_ge(rest_weighted, gc + (1 + CH * (NSB - 2)))

                        sum_windows(gc, weighted, lambda j: g(q, j, D), lambda j: ze[:, j, 0:D],
                                    following(i, q, k, last))
                return edges

            def tables(phase, i, p, bank_ap):
                pe.wait_ge(new_copied, nth("12", phase, i, p))
                if started(i):
                    pe.wait_ge(tab_copied, nth("012", phase, i - 1, p))
                for kk in range(GK):
                    ins = mm(bank_ap[:, kk * TW:kk * TW + TW], nb("newt", p)[:, kk * P:kk * P + P], w_t[:, phase - 1, :],
                             start=True, stop=True)
                ins.then_inc(tab_done, 1)

            def nodes1(i):
                for p in range(2):
                    turn_x(1, i, p)
                for p in range(2):
                    pe.wait_ge(attn_squared, nth("1", 1, i, p))
                    for kk in range(GK):
                        z = bank[4 * p + 1][:, kk * ZW:kk * ZW + ZW]
                        c = slice(kk * P, kk * P + P)
                        mm(z, nb("xt", p)[:, c], w_n[:, 0, :], start=True, stop=False)
                        mm(z, nb("at", p)[:, c], w_n[:, 1, :], start=False, stop=False)
                        mm(z[:, D + 1:ZW], nb("xt2", p)[:, c], one_c, start=False, stop=False)
                        ins = mm(z[:, D + 1:ZW], nb("at2", p)[:, c], one_c, start=False, stop=True)
                    ins.then_inc(norm_done, 1)
                for p in range(2):
                    pe.wait_ge(x_new, nth("123", 1, i, p))
                    turn(nb("new", p), bank[4 * p + 2][:, 0:GN], new_turned)
                for p in range(2):
                    tables(1, i, p, bank[4 * p + 3])

            def pick_weights(i):
                for p in range(2):
                    mm(bank[4 * p][:, 0:GN], sel[:, :], acc[:, 1, bass.ds(2 * GN * i + p * GN, GN)],
                       start=True, stop=True).then_inc(den_picked, 1)

            def nodes2(i):
                def nodes(p):
                    return bass.ds(2 * GN * i + p * GN, GN)
                if not started(i):
                    pick_weights(0)
                for p in range(2):
                    pe.wait_ge(attn_ready, nth("123", 2, i, p))
                    turn(nb("at", p), bank[4 * p][:, GN:2 * GN], attn_turned)
                for p in range(2):
                    pe.wait_ge(mid_ready, 2 * i + p + 1)
                    turn(nb("at2", p), bank[4 * p + 1][:, 0:GN], mid_turned)
                if more(i):
                    pick_weights(i + 1)
                for p in range(2):
                    pe.wait_ge(mid_copied, 2 * i + p + 1)
                    if started(i):
                        pe.wait_ge(tab_copied, nth("012", 2, i - 1, p))
                    for o in range(2):
                        z = bank[4 * p + 2][:, o * GN:o * GN + GN]
                        mm(z, w1[:, 0, o * P:o * P + P], nb("xt", p), start=True, stop=False)
                        ins = mm(z, w1[:, 1, o * P:o * P + P], acc[:, 1, nodes(p)], start=False, stop=True)
                    ins.then_inc(h_done, 1)
                for p in range(2):
                    pe.wait_ge(h_ready, 4 * i + p + 1)
                    for o in range(2):
                        z = bank[4 * p + 3][:, o * GN:o * GN + GN]
                        for kk in range(2):
                            ins = mm(z, w2[:, kk, o * P:o * P + P], nb("h1", p, 2 * GN)[:, kk * GN:kk * GN + GN],
                                     start=(kk == 0), stop=(kk == 1))
                    ins.then_inc(h_done, 1)
                for p in range(2):
                    pe.wait_ge(h_ready, 4 * i + p + 3)
                    for n in range(GK):
                        z = bank[4 * p + 3][:, n * P:n * P + P]
                        for kk in range(2):
                            ins = mm(z, nb("h2", p, 2 * GN)[:, kk * GN + n * P:kk * GN + n * P + P], w3[:, kk, :],
                                     start=(kk == 0), stop=(kk == 1))
                    ins.then_inc(h3_done, 1)
                for p in range(2):
                    pe.wait_ge(x_new, nth("123", 2, i, p))
                    turn(nb("new", p), bank[4 * p + 1][:, GN:2 * GN], new_turned)
                for p in range(2):
                    tables(2, i, p, bank[4 * p + 2])

            def nodes3(i):
                for p in range(2):
                    turn_x(3, i, p)
                for p in range(2):
                    pe.wait_ge(x_copied, nth("013", 3, i, p))
                    mm(bank[4 * p + 1][:, 0:GN], w_res[:, :], nb("xt", p), start=True, stop=True).then_inc(res_done, 1)
                for p in range(2):
                    pe.wait_ge(attn_ready, nth("123", 3, i, p))
                    turn(nb("at", p), bank[4 * p + 2][:, 0:GN], attn_turned)

            group_pairs(pe, nodes0)
            pe.wait_ge(tab_copied, GROUPS)
            with pe.Fori(0, PAIRS) as i:
                edges0(i)
            pe.wait_ge(acc_done, NT + ACC_CREDIT)
            group_pairs(pe, nodes1)
            pe.wait_ge(tab_copied, 2 * GROUPS)
            target_scores(CH * 1, 0, range(TC // Q4 + 1))
            with pe.Fori(0, PAIRS - 1) as i:
                edges_gat(1)(i)
            edges_gat(1)(PAIRS - 1, last=True)
            pe.wait_ge(acc_done, 2 * NT + ACC_CREDIT)
            group_pairs(pe, nodes2, peel_last=True)
            pe.wait_ge(tab_copied, 3 * GROUPS)
            target_scores(CH * 2, 0, range(TC // Q4 + 1))
            with pe.Fori(0, PAIRS - 1) as i:
                edges_gat(2)(i)
            edges_gat(2)(PAIRS - 1, last=True)
            pe.wait_ge(acc_done, 3 * NT + ACC_CREDIT)
            group_pairs(pe, nodes3)

        @block.vector
        def _(dve):
            v = nc.vector
            dve.sem_inc(acc_done, ACC_CREDIT)

            count = [0]

            def did(ins):
                count[0] += 1
                ins.then_inc(setup_dve, 1)
                return count[0]

            def then(ins):
                dve.wait_ge(setup_dve, did(ins))

            dve.wait_ge(edges_in, 16 * 15)
            assert did(v.tensor_copy(dtf, dti)) == DTF_READY
            assert did(v.tensor_copy(stf, sti)) == STF_READY
            dve.wait_ge(setup_pe, 2)
            for n in range(2):
                lo, hi = 512 * n, min(512 * n + 512, NT)
                did(v.tensor_copy(dcol[:, lo:hi], bank[n][:, 0:hi - lo]))
                did(v.tensor_copy(src_i[:, lo:hi], zb[:, n, 0:hi - lo]))
            dve.wait_ge(setup_dve, count[0])
            assert did(v.tensor_copy(first_i[:, :], dcol[0:1, :])) == DCOL_READY
            dve.wait_ge(edges_in, 16 * 18)
            assert did(v.tensor_copy(stf, sti)) == NEXT_READY
            dve.wait_ge(consts, 8)
            did(v.tensor_copy(iota_row[:, :], iota_i))
            did(v.tensor_copy(iota_c, col_i[:, 0:1]))
            then(v.tensor_scalar(col_i[:, 1:2], col_i[:, 0:1], F // 2, None, ALU.bitwise_and))
            then(v.tensor_copy(attr_mask, col_i[:, 1:2]))
            then(v.tensor_scalar(attr_mask, attr_mask, 2.0 / F, None, ALU.mult))
            then(v.tensor_scalar(den_mask, attr_mask, -1.0, 1.0, ALU.mult, ALU.add))
            did(v.memset(one_c, 1.0))
            dve.wait_ge(weights_in, 16 * N_WEIGHTS)
            assert did(v.memset(eps, EPS)) == BN_VAR
            then(v.tensor_reduce(rsum[:, 0:1], we_raw, AX.X, ALU.add))
            then(v.tensor_reduce(rsum[:, 1:2], wn_raw, AX.X, ALU.add))
            then(v.tensor_scalar(rsum[:, 2:3], rsum[:, 0:1], -1.0 / (3 * D), None, ALU.mult))
            then(v.tensor_scalar(rsum[:, 3:4], rsum[:, 1:2], -1.0 / (2 * D), None, ALU.mult))
            did(v.tensor_scalar(we_raw, we_raw, rsum[:, 2:3], None, ALU.add))
            assert did(v.tensor_scalar(wn_raw, wn_raw, rsum[:, 3:4], None, ALU.add)) == CENTRED
            dve.wait_ge(setup_pe, 3)
            for k, into in enumerate((first_b, last_b)):
                for n in range(2):
                    lo, hi = 512 * n, min(512 * n + 512, NT)
                    did(v.tensor_copy(into[:, lo:hi], bank[4 + 2 * k + n][:, 0:hi - lo]))
            dve.wait_ge(setup_dve, count[0])
            did(v.tensor_tensor(rel[:, :], dcol, first_b, ALU.subtract))
            dve.wait_ge(setup_pe, 4)
            for n in range(2):
                lo, hi = 512 * n, min(512 * n + 512, NT)
                then(v.tensor_tensor(tile_tmp[:, lo:hi], dcol[:, lo:hi], zb[:, n, 0:hi - lo], ALU.not_equal))
            then(v.tensor_scalar(times[:, :], tile_tmp[:, 0:NT], 1.0, None, ALU.add))
            then(v.tensor_tensor(pen_single, first_b, last_b, ALU.not_equal))
            then(v.tensor_tensor(pen_join_f[:, 1:NT], first_b[:, 1:NT], last_b[:, 0:NT - 1], ALU.not_equal))
            did(v.memset(pen_join_f[:, 0:1], 1.0))
            then(v.memset(pen_join_f[:, NT:NT + 1], 1.0))
            did(v.tensor_scalar(pen_join[:, :], pen_join_f, BIG, None, ALU.mult))
            did(v.memset(carry_f[:, 0:1], BIG))
            then(v.tensor_tensor(tile_tmp[:, 0:NT], pen_join_f[:, 1:NT + 1], pen_single, ALU.max))
            did(v.tensor_scalar(carry_f[:, 1:NT + 1], tile_tmp[:, 0:NT], BIG, None, ALU.mult))
            then(v.memset(fac[:, :], 1.0))
            then(v.tensor_tensor(tile_tmp[:, 0:NT], pen_join_f[:, 0:NT], pen_single, ALU.max))
            did(v.tensor_scalar(carry_r[:, :, 0:TC - 1],
                                tile_tmp[:, 0:NT].rearrange("p (c j) -> p c j", j=TC)[:, :, 1:TC][:, :, ::-1],
                                BIG, None, ALU.mult))
            did(v.memset(pen_f[:, :, 0:1], 0.0))
            did(v.memset(pen_r[:, :, 0:1], 0.0))
            half = CH // 2
            for n in range(2):
                cs = slice(n * half, n * half + half)
                d3 = dtf[:, cs, :]
                df = diff.rearrange("p (c e) -> p c e", e=P)
                dve.wait_ge(setup_dve, count[0])
                then(v.tensor_tensor(df[:, :, 1:P], d3[:, :, 1:P], d3[:, :, 0:P - 1], ALU.not_equal))
                did(v.tensor_scalar(pen_f[:, cs, 1:P], df[:, :, 1:P], BIG, None, ALU.mult))
                then(v.tensor_scalar(pen_r[:, cs, 1:P], df[:, :, 1:P][:, :, ::-1], BIG, None, ALU.mult))
                then(v.tensor_tensor(df, d3, d3[:, :, 0:1].to_broadcast([P, half, P]), ALU.not_equal))
                then(v.tensor_scalar(pen_first[:, cs, :], df, BIG, None, ALU.mult))
                then(v.tensor_tensor(df, d3, d3[:, :, P - 1:P].to_broadcast([P, half, P]), ALU.not_equal))
                then(v.tensor_scalar(pen_last[:, cs, :], df, BIG, None, ALU.mult))
            dve.wait_ge(setup_pe, 5)
            did(v.tensor_copy(w_sd[:, 0:D], bank[0][:, 0:D]))
            did(v.tensor_copy(w_ef[:, 0:D], bank[0][:, D:2 * D]))
            did(v.tensor_copy(w_sd[:, ZW:ZW + D], bank[0][:, 2 * D:3 * D]))
            for k in range(2):
                did(v.tensor_copy(w_n[:, k, 0:D], bank[1][:, k * D:k * D + D]))
                did(v.memset(w_n[:, k, D:D + 1], 1.0))
                did(v.memset(w_n[:, k, D + 1:ZW], 0.0))
                did(v.memset(w_sd[:, k * ZW + D:k * ZW + D + 1], 1.0))
                did(v.memset(w_sd[:, k * ZW + D + 1:k * ZW + ZW], 0.0))
            did(v.memset(w_ef[:, D:D + 1], 1.0))
            did(v.memset(w_ef[:, D + 1:ZW], 0.0))
            did(v.memset(b_t[:, 1, :], 0.0))
            for layer in range(2):
                for w in range(2):
                    a = a_raw[:, 2 * layer + w, :]
                    at = slice(D + H * w, D + H * w + H)
                    then(v.tensor_tensor(prod[:, w, :], w_t[:, layer, 0:D], a, ALU.mult))
                    then(v.tensor_reduce(w_t[:, layer, at], prod[:, w, :].rearrange("p (h f) -> p h f", h=H), AX.X, ALU.add))
                    if layer == 0:
                        then(v.tensor_tensor(prod[:, w, :], b_t[:, layer, 0:D], a, ALU.mult))
                        then(v.tensor_reduce(b_t[:, layer, at], prod[:, w, :].rearrange("p (h f) -> p h f", h=H), AX.X, ALU.add))
            then(v.tensor_tensor(b_t[:, 0, D + H:TW], b_t[:, 0, D + H:TW], ab_raw, ALU.add))
            dve.wait_ge(bn_std, 1)
            then(v.reciprocal(vec[:, 12:13], vec[:, 11:12]))
            then(v.tensor_tensor(bn_scale, vec[:, 12:13], bn_raw[:, 3:4], ALU.mult))
            then(v.tensor_tensor(vec[:, 13:14], bn_raw[:, 0:1], bn_raw[:, 1:2], ALU.subtract))
            then(v.tensor_tensor(vec[:, 14:15], vec[:, 13:14], bn_scale, ALU.mult))
            did(v.tensor_tensor(bn_shift, vec[:, 14:15], bn_raw[:, 4:5], ALU.add))
            dve.wait_ge(setup_pe, 5)
            did(v.tensor_tensor(b1_c, b1_c, bank[1][:, 2 * P:2 * P + 2], ALU.add))
            did(v.memset(blk[:, :, :], BIG))
            assert did(v.memset(cin[:, :, :], BIG)) == SETUP_DONE, count[0]
            dve.wait_ge(setup_dve, SETUP_DONE)

            steps = {"base": 0, "n": 0, "total": 0}

            def step(ins):
                steps["n"] += 1
                ins.then_inc(chain, 1)

            def ordered(ins=None):
                if ins is not None:
                    step(ins)
                dve.wait_ge(chain, steps["base"] + steps["n"])

            def stepped_loop(name, body, n, peel, peel_last=False):
                per = STEPS[name]
                start = steps["total"]
                if peel:
                    steps.update(base=start, n=0)
                    body(0)
                    assert steps["n"] == per, (name, steps["n"])
                with dve.Fori(int(peel), n - int(peel_last)) as i:
                    steps.update(base=start + per * i, n=0)
                    body(i)
                    assert steps["n"] == per, (name, steps["n"])
                steps["total"] = start + per * (n - int(peel_last))
                if peel_last:
                    apart(lambda: body(n - 1) if peel else body(n - 1, last=True))

            def apart(part):
                steps.update(base=steps["total"], n=0)
                part()
                steps["total"] += steps["n"]

            def nodes0(i):
                for p in range(2):
                    dve.wait_ge(tab_done, nth("012", 0, i, p))
                    dve.wait_ge(x_squared, nth("01", 0, i, p))
                    if started(i):
                        dve.wait_ge(tab_out[p], 32 * i)
                    tab = nb("tab", p, GK * 2 * ZW).rearrange("p (k s w) -> p k s w", k=GK, s=2)
                    for kk in range(GK):
                        v.tensor_copy(tab[:, kk, :, 0:D + 1],
                                      bank[4 * p + 1 + kk][:, 0:2 * ZW].rearrange("p (s w) -> p s w", s=2)[:, :, 0:D + 1])
                    v.tensor_copy(tab[:, :, :, D + 1],
                                  nb("small", p, 2).unsqueeze(2).to_broadcast([P, GK, 2])).then_inc(tab_copied, 1)

            def softmax(gc, i, q, k):
                c = bass.ds(2 * i + q, 1)
                t0 = 2 * TC * i + q * TC
                pf = pen_f[:, c, 0:P].rearrange("p a e -> p (a e)")
                pr = pen_r[:, c, :].rearrange("p a e -> p (a e)")
                p_first = pen_first[:, c, :].rearrange("p a e -> p (a e)")
                p_last = pen_last[:, c, :].rearrange("p a e -> p (a e)")
                cq, cp = cin[:, q, :], cin[:, 1 - q, :]
                dve.wait_ge(logits_turned, gc + 1)
                step(v.tensor_copy(cq[:, 0:1], cp[:, 32:33]))
                ordered(v.tensor_tensor_scan(mx[:, :], pf, lt_ps, BIG, ALU.add, ALU.max))
                ordered(v.transpose(blk[:, 0, :], mx[:, P - 32:P]))
                ordered(v.tensor_tensor(blk[:, 1, :], blk[:, 0, :], pen_join[:, bass.ds(t0 + 1, TC)], ALU.add))
                ordered(v.tensor_tensor_scan(cq[:, 1:33], carry_f[:, bass.ds(t0 + 1, TC)], blk[:, 1, :], cq[:, 0:1],
                                             ALU.add, ALU.max))
                ordered(v.transpose(blk[:, 2, :], cq[:, 0:32]))
                ordered(v.scalar_tensor_tensor(mx2[:, :], p_first, blk[:, 2, 31:32], mx[:, :], ALU.add, ALU.max))
                ordered(v.tensor_tensor_scan(mx[:, ::-1], pr, mx2[:, ::-1], BIG, ALU.add, ALU.max))
                ordered(v.transpose(blk[:, 3, :], mx[:, 0:32]))
                ordered(v.tensor_tensor(blk[:, 4, 0:TC - 1], blk[:, 3, 1:TC], pen_join[:, bass.ds(t0 + 1, TC - 1)], ALU.add))
                ordered(v.tensor_tensor_scan(blk[:, 5, 0:TC - 1][:, ::-1], carry_r[:, c, 0:TC - 1].rearrange("p a j -> p (a j)"),
                                             blk[:, 4, 0:TC - 1][:, ::-1], BIG, ALU.add, ALU.max))
                ordered(v.transpose(blk[:, 6, :], blk[:, 5, :]))
                ordered(v.scalar_tensor_tensor(mx2[:, :], p_last, blk[:, 6, 0:1], mx[:, :], ALU.add, ALU.max))
                v.tensor_tensor(lg[:, :], lt_ps, mx2[:, :], ALU.subtract).then_inc(shifted, 1)
                ordered(v.tensor_tensor(blk[:, 7, :], blk[:, 2, 31:32].to_broadcast([P, 32]),
                                        mx2[:, 0:1].to_broadcast([P, 32]), ALU.subtract))
                v.transpose(blk[:, 0, :], blk[:, 7, :]).then_inc(fac_arg, 1)

            def window_onehot(gc, i, q, j):
                v.tensor_scalar(s_oh[:, j, :], iota_row[:, :], rel[:, bass.ds(2 * TC * i + (q * TC + j), 1)], None,
                                ALU.is_equal).then_inc(s_ready, 1)

            def rescale(gc, i, q, k, regs):
                dve.wait_ge(fac_ready, gc + 1)
                first = dve.snap(regs[0][0], min_val=0, max_val=N)
                dve.wait_ge(acc_done, gc * TC + ACC_CREDIT)
                if k == 1:
                    ordered(v.scalar_tensor_tensor(fac[:, 1:2], fac[:, 0:1], den_mask, attr_mask, ALU.mult, ALU.add))
                    for half, f in ((0, fac[:, 0:1]), (1, fac[:, 1:2])):
                        col = acc[:, half, bass.ds(first, 1)]
                        step(v.tensor_scalar(col, col, f, None, ALU.mult))
                    ordered()
                else:
                    col = acc[:, 0:2, bass.ds(first, 1)]
                    ordered(v.tensor_scalar(col, col, fac[:, 0:1], None, ALU.mult))

            def sum_chunk(gc, i, q, regs, next_chunk):
                for j in range(TC):
                    if j % SB == 2 and j + SB < TC:
                        dve.load(regs[(j // SB + 1) % 2],
                                 first_i[0:1, bass.ds(2 * TC * i + (q * TC + (j // SB + 1) * SB), SB)])
                    first = dve.snap(regs[(j // SB) % 2][j % SB], min_val=0, max_val=N)
                    win_acc = acc[:, 0:2, bass.ds(first, P)]
                    dve.wait_ge(agg_done, gc * TC + (j + 1 + AGG_CREDIT))
                    if next_chunk is not None:
                        window_onehot(*next_chunk, j)
                    if j:
                        dve.wait_ge(acc_done, gc * TC + j + ACC_CREDIT)
                    v.tensor_tensor(win_acc, win_acc, agg_ps(j % AGG_RING).rearrange("p (a n) -> p a n", a=2),
                                    ALU.add).then_inc(acc_done, 1)

            def copy_weights(gc, i, q, k):
                dve.wait_ge(weights_turned, gc + 1)
                if k == 0:
                    v.tensor_copy(ex[:, :], ex_ps).then_inc(ex_ready, 1)
                else:
                    v.tensor_tensor(ex[:, :].rearrange("p (h j) -> p h j", h=H), ex_ps.rearrange("p (h j) -> p h j", h=H),
                                    times[:, bass.ds(2 * TC * i + q * TC, TC)].unsqueeze(1).to_broadcast([P, H, TC]),
                                    ALU.mult).then_inc(ex_ready, 1)

            def edges0(i, last=False):
                for q in range(2):
                    gc = 2 * i + q

                    def spreads(s):
                        c = slice(s * SB, s * SB + SB)
                        dve.wait_ge(squared, gc * TC + (s * SB + SB + SQ_CREDIT))
                        dve.wait_ge(z_copied, 8 * gc + (2 * s + 2 + 1))
                        step(v.tensor_scalar(att[:, 1, c], ze[:, c, D], 1.0 / (3 * D), None, ALU.mult))
                        ordered(v.tensor_tensor(att[:, 4, c], ze[:, c, D + 1], att[:, 0, c], ALU.add))
                        ordered(v.tensor_tensor(att[:, 5, c], att[:, 1, c], att[:, 1, c], ALU.mult))
                        ordered(v.scalar_tensor_tensor(att[:, 6, c], att[:, 4, c], 1.0 / (3 * D), att[:, 5, c],
                                                       ALU.mult, ALU.subtract))
                        v.tensor_scalar(att[:, 2, c], att[:, 6, c], 0.0, None, ALU.max).then_inc(var_ready, 1)

                    def edge_values(s):
                        tiles_ = range(s * SB, s * SB + SB)
                        dve.wait_ge(std_ready, gc * NSB + s + 1)
                        ordered(v.reciprocal(att[:, 4, s * SB:s * SB + SB], att[:, 3, s * SB:s * SB + SB]))
                        for j in tiles_:
                            ins = v.scalar_tensor_tensor(ze[:, j, 0:D], ze[:, j, 0:D], att[:, 4, j:j + 1], be, ALU.mult, ALU.add)
                        ordered(ins)
                        zz = ze[:, s * SB:s * SB + SB, 0:D]
                        ordered(v.scalar_tensor_tensor(zz, zz, 0.01, zz, ALU.mult, ALU.max))
                        for j in tiles_:
                            ins = v.tensor_tensor_reduce(out=(mx, mx2, lg, ext)[j % 4][:, :], in0=ze[:, j, 0:D], in1=ae,
                                                         scale=1.0, scalar=0.0, op0=ALU.mult, op1=ALU.add,
                                                         accum_out=att[:, 7, j:j + 1])
                            if j % 4 == 3:
                                ordered(ins)

                    for s in range(NSB):
                        spreads(s)
                        edge_values(s)
                    v.tensor_copy(lg2[:, :].rearrange("p (h j) -> p h j", h=H),
                                  att[:, 7, :].unsqueeze(1).to_broadcast([P, H, TC])).then_inc(logits_ready, 1)
                    softmax(gc, i, q, 0)
                    dve.load(regs0[0], first_i[0:1, bass.ds(2 * TC * i + q * TC, SB)])
                    copy_weights(gc, i, q, 0)
                    dve.wait_ge(ex_ready, gc + 1)
                    v.tensor_tensor(ze[:, 0:SB, 0:D], ze[:, 0:SB, 0:D], ex[:, 0:SB].unsqueeze(2).to_broadcast([P, SB, D]),
                                    ALU.mult).then_inc(values_weighted, 1)
                    rescale(gc, i, q, 0, regs0)
                    sum_chunk(gc, i, q, regs0, following(i, q, 0, last))

            def edges_gat(k, regs):
                def edges(i, last=False):
                    for q in range(2):
                        gc = 2 * i + (q + CH * k)
                        for s in range(NSB):
                            dve.wait_ge(gather_in[q][s], 128 * i + (128 + 128 * PAIRS * k))
                        dve.wait_ge(expanded, gc * TC + TC + EXP_CREDIT)
                        ordered(v.tensor_tensor(lg[:, :].rearrange("p (h j) -> p h j", h=H),
                                                bank[2 + q][:, 0:P].rearrange("p (h j) -> p h j", h=H),
                                                gq(q)[:, :, D:KW].rearrange("p j h -> p h j"), ALU.add))
                        v.scalar_tensor_tensor(lg2[:, :], lg[:, :], 0.2, lg[:, :], ALU.mult, ALU.max).then_inc(logits_ready, 1)
                        softmax(gc, i, q, k)
                        dve.load(regs[0], first_i[0:1, bass.ds(2 * TC * i + q * TC, SB)])
                        copy_weights(gc, i, q, k)
                        dve.wait_ge(ex_ready, gc + 1)
                        for s in range(NSB - 1):
                            vals = gq(q)[:, s * SB:s * SB + SB, 0:D].rearrange("p j (h x) -> p j h x", h=H)
                            w = ex[:, :].rearrange("p (h j) -> p j h", h=H)[:, s * SB:s * SB + SB, :]
                            v.tensor_tensor(vals, vals, w.unsqueeze(3).to_broadcast([P, SB, H, F]),
                                            ALU.mult).then_inc(values_weighted, 1)
                        rescale(gc, i, q, k, regs)
                        sum_chunk(gc, i, q, regs, following(i, q, k, last))
                return edges

            def small(p):
                return nb("small", p, 40)

            def layer_norm(y, into, var_count, done, before_write):
                def part(p, lo, hi):
                    return small(p)[:, lo:hi].rearrange("p (k s) -> p k s", k=GK)
                for p in range(2):
                    for kk in range(GK):
                        ins = v.bn_stats(part(p, 12, 24)[:, kk, :], nb(y, p)[:, kk * P:kk * P + P])
                    step(ins)
                ordered()
                dve.sem_inc(host, 1)
                for p in range(2):
                    for kk in range(GK):
                        ins = v.bn_aggr(part(p, 24, 28)[:, kk, :], part(p, 12, 24)[:, kk, :])
                    ins.then_inc(ln_var, 1)
                for p in range(2):
                    dve.wait_ge(ln_std, var_count + p)
                    step(v.reciprocal(small(p)[:, 30:32], small(p)[:, 28:30]))
                ordered()
                for p in range(2):
                    before_write(p)
                    for kk in range(GK):
                        ins = v.tensor_scalar(nb(into, p)[:, kk * P:kk * P + P], nb(y, p)[:, kk * P:kk * P + P],
                                              part(p, 24, 28)[:, kk, 0:1], small(p)[:, 30 + kk:31 + kk],
                                              ALU.subtract, ALU.mult)
                    ins.then_inc(done, 1)

            def stored(phase, i):
                def wait(p):
                    if not started(i):
                        return
                    if phase == 3:
                        dve.wait_ge(rows_out[p], 16 * i)
                    else:
                        dve.wait_ge(tab_out[p], 48 * i + 32 * GPAIRS + 48 * GPAIRS * (phase - 1))
                return wait

            def copy_tables(phase, i, p, bank_ap):
                dve.wait_ge(tab_done, nth("012", phase, i, p))
                v.tensor_tensor(nb("tab", p, GK * TW).rearrange("p (k w) -> p k w", k=GK),
                                bank_ap[:, 0:GK * TW].rearrange("p (k w) -> p k w", k=GK),
                                b_t[:, phase - 1, :].unsqueeze(1).to_broadcast([P, GK, TW]), ALU.add).then_inc(tab_copied, 1)

            def bc(row):
                return row.unsqueeze(1).to_broadcast([P, GK, D])

            def both(make):
                for p in range(2):
                    step(make(p))
                ordered()

            def quotients(i, sums, tmp, done=None):
                def nodes(p):
                    return bass.ds(2 * GN * i + p * GN, GN)
                both(lambda p: v.tensor_scalar(nb(tmp, p), sums(p, nodes(p)), TINY, None, ALU.max))
                both(lambda p: v.reciprocal(nb(tmp, p), nb(tmp, p)))
                if done is None:
                    both(lambda p: v.tensor_tensor(nb("at", p), acc[:, 0, nodes(p)], nb(tmp, p), ALU.mult))
                else:
                    for p in range(2):
                        v.tensor_tensor(nb("at", p), acc[:, 0, nodes(p)], nb(tmp, p), ALU.mult).then_inc(done, 1)

            def nodes1(i):
                z = [bank[4 * p + 1][:, 0:GK * ZW].rearrange("p (k w) -> p k w", k=GK) for p in range(2)]
                sm = [small(p) for p in range(2)]
                dve.wait_ge(norm_done, nth("1", 1, i, 1))
                both(lambda p: v.tensor_scalar(sm[p][:, 0:2], z[p][:, :, D], 1.0 / (2 * D), None, ALU.mult))
                both(lambda p: v.tensor_tensor(sm[p][:, 2:4], sm[p][:, 0:2], sm[p][:, 0:2], ALU.mult))
                both(lambda p: v.scalar_tensor_tensor(sm[p][:, 8:10], z[p][:, :, D + 1], 1.0 / (2 * D), sm[p][:, 2:4],
                                                      ALU.mult, ALU.subtract))
                for p in range(2):
                    v.tensor_scalar(sm[p][:, 4:6], sm[p][:, 8:10], 0.0, None, ALU.max).then_inc(norm_var, 1)
                dve.wait_ge(norm_std, nth("1", 1, i, 1))
                both(lambda p: v.reciprocal(sm[p][:, 10:12], sm[p][:, 6:8]))
                both(lambda p: v.tensor_tensor(tiles(nb("h", p)), z[p][:, :, 0:D],
                                               sm[p][:, 10:12].unsqueeze(2).to_broadcast([P, GK, D]), ALU.mult))
                both(lambda p: v.tensor_tensor(tiles(nb("h", p)), tiles(nb("h", p)), bc(bn_row), ALU.add))
                both(lambda p: v.scalar_tensor_tensor(nb("h", p), nb("h", p), 0.01, nb("h", p), ALU.mult, ALU.max))
                both(lambda p: v.tensor_tensor(nb("h", p), nb("h", p), nb("x", p), ALU.add))
                layer_norm("h", "new", nth("1", 1, i, 0), x_new, stored(1, i))
                if more(i):
                    quotients(i + 1, lambda p, nodes: acc[:, 1, nodes], "tmp", attn_ready)
                for p in range(2):
                    copy_tables(1, i, p, bank[4 * p + 3])

            def nodes2(i):
                dve.wait_ge(attn_turned, nth("23", 2, i, 1))
                for p in range(2):
                    dve.wait_ge(x_in[p], 16 * i + 16 + 2 * 16 * GPAIRS)
                    step(v.tensor_tensor(nb("h", p), bank[4 * p][:, GN:2 * GN], nb("x", p), ALU.add))
                ordered()
                layer_norm("h", "at2", GROUPS + 4 * i + 1, mid_ready, lambda p: None)
                if more(i):
                    dve.wait_ge(den_picked, 2 * i + 4)
                    quotients(i + 1, lambda p, nodes: bank[4 * p][:, 0:GN], "tmp", attn_ready)
                for layer, buf in enumerate(("h1", "h2")):
                    for p in range(2):
                        dve.wait_ge(h_biased, 4 * i + (2 * layer + p + 1))
                        b = nb(buf, p, 2 * GN)
                        v.scalar_tensor_tensor(b, b, 0.01, b, ALU.mult, ALU.max).then_inc(h_ready, 1)
                dve.wait_ge(h3_done, 2 * i + 2)
                both(lambda p: v.tensor_tensor(tiles(nb("h", p)), tiles(bank[4 * p + 3][:, 0:GN]), bc(b3_row), ALU.add))
                both(lambda p: v.tensor_tensor(nb("h", p), nb("h", p), nb("at2", p), ALU.add))
                layer_norm("h", "new", GROUPS + 4 * i + 3, x_new, stored(2, i))
                for p in range(2):
                    copy_tables(2, i, p, bank[4 * p + 2])

            def nodes3(i):
                a = [nb("at", p) for p in range(2)]
                dve.wait_ge(res_done, nth("3", 3, i, 1))
                both(lambda p: v.tensor_tensor(a[p], a[p], bank[4 * p + 1][:, 0:GN], ALU.add))
                both(lambda p: v.tensor_scalar(a[p], a[p], bn_scale, bn_shift, ALU.mult, ALU.add))
                for p in range(2):
                    v.tensor_scalar(nb("tmp", p), a[p], 0.0, None, ALU.min).then_inc(elu_arg, 1)
                dve.wait_ge(elu_exp, nth("3", 3, i, 1))
                both(lambda p: v.scalar_tensor_tensor(a[p], a[p], 0.0, nb("at2", p), ALU.max, ALU.add))
                for p in range(2):
                    v.tensor_scalar(a[p], a[p], -1.0, None, ALU.add).then_inc(attn_ready, 1)
                dve.wait_ge(attn_turned, nth("23", 3, i, 1))
                both(lambda p: v.tensor_tensor(nb("h", p), bank[4 * p + 2][:, 0:GN], nb("x", p), ALU.add))
                layer_norm("h", "new", 3 * GROUPS + 2 * i + 1, x_new, stored(3, i))
                if more(i):
                    quotients(i + 1, lambda p, nodes: acc[:, 1, nodes], "xt2")

            regs0 = [[dve.alloc_register(f"first_{n}_{m}") for m in range(SB)] for n in range(2)]

            def restart_carry(n):
                dve.wait_ge(zeroed, n)
                steps["base"], steps["n"] = steps["total"], 0
                ordered(v.memset(cin[:, 1, :], BIG))
                steps["total"] += 1

            stepped_loop("nodes0", nodes0, GPAIRS, True)
            restart_carry(1)
            for j in range(TC):
                window_onehot(0, 0, 0, j)
            stepped_loop("edges0", edges0, PAIRS, False, peel_last=True)
            dve.wait_ge(acc_done, NT + ACC_CREDIT)
            apart(lambda: quotients(0, lambda p, nodes: acc[:, 1, nodes], "tmp", attn_ready))
            stepped_loop("nodes1", nodes1, GPAIRS, True, peel_last=True)
            restart_carry(2)
            for j in range(TC):
                window_onehot(CH * 1, 0, 0, j)
            stepped_loop("edges1", edges_gat(1, regs0), PAIRS, False, peel_last=True)
            dve.wait_ge(acc_done, 2 * NT + ACC_CREDIT)
            dve.wait_ge(den_picked, 2)
            apart(lambda: quotients(0, lambda p, nodes: bank[4 * p][:, 0:GN], "tmp", attn_ready))
            stepped_loop("nodes2", nodes2, GPAIRS, True, peel_last=True)
            restart_carry(3)
            for j in range(TC):
                window_onehot(CH * 2, 0, 0, j)
            stepped_loop("edges2", edges_gat(2, regs0), PAIRS, False, peel_last=True)
            dve.wait_ge(acc_done, 3 * NT + ACC_CREDIT)
            apart(lambda: quotients(0, lambda p, nodes: acc[:, 1, nodes], "xt2"))
            stepped_loop("nodes3", nodes3, GPAIRS, True, peel_last=True)


_INS = ['x', 'src', 'dst', 'edge_attr_128', 'edge_attr_64', 'L0_gnn_W_e', 'L0_gnn_b_e', 'L0_gnn_a_e', 'L0_gnn_W_n',
        'L0_gnn_b_n', 'L1_gnn_W_w', 'L1_gnn_W_b', 'L1_gnn_a_w', 'L1_gnn_a_b', 'L2_gnn_u', 'L2_gnn_w1', 'L2_gnn_b1',
        'L2_gnn_w2', 'L2_gnn_b2', 'L2_gnn_w3', 'L2_gnn_b3', 'L3_gnn_W', 'L3_gnn_att_src', 'L3_gnn_att_dst',
        'L3_gnn_bias', 'L3_gnn_W_res', 'L3_gnn_bn_gamma', 'L3_gnn_bn_beta', 'L3_gnn_bn_mean', 'L3_gnn_bn_var']
_OUT = ((N, D), 'float32')


def kernel(**inputs):
    import numpy as _np
    import concourse.bacc as _bacc
    from concourse import mybir as _mybir
    from concourse.bass_utils import run_bass_kernel_spmd as _run

    nc = _bacc.Bacc("TRN2", target_bir_lowering=False, num_devices=1)
    arrays, args = {}, {}
    for name in _INS:
        a = _np.ascontiguousarray(inputs[name])
        arrays[f"in_{name}_dram"] = a
        args[name] = nc.dram_tensor(f"in_{name}_dram", a.shape, _mybir.dt.from_np(a.dtype), kind="ExternalInput").ap()
    shape, dtype = _OUT
    out = nc.dram_tensor("out_0_dram", shape, _mybir.dt.from_np(_np.dtype(dtype)), kind="ExternalOutput").ap()
    graph_kernel(nc, args, out)
    r = _run(nc, [arrays], core_ids=[0])
    return r.results[0]["out_0_dram"]
```
